# Optimizing a Trainium2 kernel written in Bass

```python
import numpy as np
import jax
import jax.numpy as jnp

def _softmax(x, axis=-1):
    return jax.nn.softmax(x, axis=axis)

def _gelu(x):
    return jax.nn.gelu(x, approximate=True)

def _silu(x):
    return jax.nn.silu(x)

def _sigmoid(x):
    return jax.nn.sigmoid(x)

def _layernorm(x, axis=-1, eps=1e-05):
    m = jnp.mean(x, axis=axis, keepdims=True)
    v = jnp.var(x, axis=axis, keepdims=True)
    return (x - m) / jnp.sqrt(v + eps)

def _scatter_add(tgt, idx, src, axis=0):
    return tgt.at[idx].add(src)

def _segment_sum(src, seg, n):
    return jax.ops.segment_sum(src, seg, n)
kernel_name = 'mk_xattn_ffn_d1_seqx_r2_27e98e'

def setup_inputs(seed: int=0):
    np.random.seed(seed)
    _w = jnp.asarray

    def _rec_inputs():
        import jax
        import jax.numpy as jnp
        _rk = jax.random.key(seed)
        x = 7.22e-05 + 1 * jax.random.normal(jax.random.fold_in(_rk, 1), (1, 4096, 512), jnp.float32)
        _lenS = 4096 - jax.random.randint(jax.random.fold_in(_rk, 7), (1,), 0, max(1, 4096 // 4) + 1, jnp.int32)
        _lenS2 = 3202 - jax.random.randint(jax.random.fold_in(_rk, 8), (1,), 0, max(1, 3202 // 4) + 1, jnp.int32)
        _ctx_1024P = jax.random.normal(jax.random.fold_in(_rk, 11), (1, 16, 512), jnp.float32)
        _ctx_1024c = jax.random.dirichlet(jax.random.fold_in(_rk, 511), 0.3 * jnp.ones((16,), jnp.float32), (1, 3202))
        _ctx_1024t = jnp.einsum('bsk,bkd->bsd', _ctx_1024c, _ctx_1024P)
        _ctx_1024t = _ctx_1024t * jax.lax.rsqrt(jnp.mean(jnp.square(_ctx_1024t)) + 1e-12) * 0.953939
        ctx_1024 = 4.13588e-05 + 0.999923 * (_ctx_1024t + 0.3 * jax.random.normal(jax.random.fold_in(_rk, 611), (1, 3202, 512), jnp.float32))
        return (x, ctx_1024)
    x, ctx_1024 = _rec_inputs()

    def _L0_xattn_setup():
        import jax, jax.numpy as jnp
        import numpy as np
        from math import sqrt
        D_MODEL = 512
        OUT_D = 512
        N_HEADS = 16
        D_HEAD = D_MODEL // N_HEADS

        def _xavier(key, fan_in, fan_out):
            limit = sqrt(6.0 / (fan_in + fan_out))
            return jax.random.uniform(key, (fan_in, fan_out), jnp.float32, -limit, limit)
        key = jax.random.key(seed)
        ks = jax.random.split(key, 7)
        B, L = (4, 1024)
        queries = jax.random.normal(ks[0], (B, L, D_MODEL), jnp.float32)
        keys = jax.random.normal(ks[1], (B, L, D_MODEL), jnp.float32)
        values = jax.random.normal(ks[2], (B, L, D_MODEL), jnp.float32)
        Wq = _xavier(ks[3], D_MODEL, N_HEADS * D_HEAD)
        Wk = _xavier(ks[4], D_MODEL, N_HEADS * D_HEAD)
        Wv = _xavier(ks[5], D_MODEL, N_HEADS * D_HEAD)
        Wo = _xavier(ks[6], N_HEADS * D_HEAD, OUT_D)
        bq = jnp.zeros((N_HEADS * D_HEAD,), jnp.float32)
        bk = jnp.zeros((N_HEADS * D_HEAD,), jnp.float32)
        bv = jnp.zeros((N_HEADS * D_HEAD,), jnp.float32)
        bo = jnp.zeros((OUT_D,), jnp.float32)
        return {'queries': queries, 'keys': keys, 'values': values, 'Wq': Wq, 'bq': bq, 'Wk': Wk, 'bk': bk, 'Wv': Wv, 'bv': bv, 'Wo': Wo, 'bo': bo}
    _L0_xattn_all = _L0_xattn_setup()
    _L0_xattn_in = {k: v for k, v in _L0_xattn_all.items() if k in ('Wq', 'bq', 'Wk', 'bk', 'Wv', 'bv', 'Wo', 'bo')}
    del _L0_xattn_all

    def _L0_ffn_setup():
        import jax, jax.numpy as jnp
        import numpy as np
        IN_F = 512
        OUT_F = 512
        N_EXPERTS = 8
        TOP_K = 2
        key = jax.random.key(seed)
        ks = jax.random.split(key, 5)
        scale_in = 1.0 / np.sqrt(IN_F)
        x = jax.random.normal(ks[0], (4, 1024, IN_F), dtype=jnp.float32)
        W_experts = jax.random.uniform(ks[1], (N_EXPERTS, OUT_F, IN_F), jnp.float32, -scale_in, scale_in)
        b_experts = jax.random.uniform(ks[2], (N_EXPERTS, OUT_F), jnp.float32, -scale_in, scale_in)
        W_router = jax.random.uniform(ks[3], (N_EXPERTS, IN_F), jnp.float32, -scale_in, scale_in)
        b_router = jax.random.uniform(ks[4], (N_EXPERTS,), jnp.float32, -scale_in, scale_in)
        return {'x': x, 'W_experts': W_experts, 'b_experts': b_experts, 'W_router': W_router, 'b_router': b_router}
    _L0_ffn_all = _L0_ffn_setup()
    _L0_ffn_in = {k: v for k, v in _L0_ffn_all.items() if k in ('W_experts', 'b_experts', 'W_router', 'b_router')}
    del _L0_ffn_all
    return {'x': x, 'ctx_1024': ctx_1024, 'L0_xattn_Wq': _L0_xattn_in['Wq'], 'L0_xattn_bq': _L0_xattn_in['bq'], 'L0_xattn_Wk': _L0_xattn_in['Wk'], 'L0_xattn_bk': _L0_xattn_in['bk'], 'L0_xattn_Wv': _L0_xattn_in['Wv'], 'L0_xattn_bv': _L0_xattn_in['bv'], 'L0_xattn_Wo': _L0_xattn_in['Wo'], 'L0_xattn_bo': _L0_xattn_in['bo'], 'L0_ffn_W_experts': _L0_ffn_in['W_experts'], 'L0_ffn_b_experts': _L0_ffn_in['b_experts'], 'L0_ffn_W_router': _L0_ffn_in['W_router'], 'L0_ffn_b_router': _L0_ffn_in['b_router']}

def reference(x, ctx_1024, L0_xattn_Wq, L0_xattn_bq, L0_xattn_Wk, L0_xattn_bk, L0_xattn_Wv, L0_xattn_bv, L0_xattn_Wo, L0_xattn_bo, L0_ffn_W_experts, L0_ffn_b_experts, L0_ffn_W_router, L0_ffn_b_router):
    import jax
    import jax.numpy as jnp

    def _L0_xattn_ref(queries, keys, values, Wq, bq, Wk, bk, Wv, bv, Wo, bo):
        import jax, jax.numpy as jnp
        import numpy as np
        from math import sqrt
        D_MODEL = 512
        OUT_D = 512
        N_HEADS = 16
        D_HEAD = D_MODEL // N_HEADS

        def _xavier(key, fan_in, fan_out):
            limit = sqrt(6.0 / (fan_in + fan_out))
            return jax.random.uniform(key, (fan_in, fan_out), jnp.float32, -limit, limit)
        B, L, _ = queries.shape
        _, S, _ = keys.shape
        H, E = (N_HEADS, D_HEAD)
        q = (queries @ Wq + bq).reshape(B, L, H, E)
        k = (keys @ Wk + bk).reshape(B, S, H, E)
        v = (values @ Wv + bv).reshape(B, S, H, E)
        scale = 1.0 / sqrt(E)
        scores = jnp.einsum('blhe,bshe->bhls', q, k)
        A = jax.nn.softmax(scale * scores, axis=-1)
        out = jnp.einsum('bhls,bshd->blhd', A, v)
        out = out.transpose(0, 2, 1, 3).reshape(B, L, H * E)
        return out @ Wo + bo

    def _L0_ffn_ref(x, W_experts, b_experts, W_router, b_router):
        import jax, jax.numpy as jnp
        import numpy as np
        IN_F = 512
        OUT_F = 512
        N_EXPERTS = 8
        TOP_K = 2
        router_logits = jnp.einsum('bsd,ed->bse', x, W_router) + b_router
        router_weights = jax.nn.softmax(router_logits, axis=-1)
        if TOP_K < N_EXPERTS:
            topk_w, topk_idx = jax.lax.top_k(router_weights, TOP_K)
            sparse = jnp.zeros_like(router_weights)
            router_weights = jnp.take_along_axis(sparse, topk_idx, axis=-1)
            router_weights = sparse.at[..., :].set(0.0)
            b_idx = jnp.arange(sparse.shape[0])[:, None, None]
            s_idx = jnp.arange(sparse.shape[1])[None, :, None]
            router_weights = sparse.at[b_idx, s_idx, topk_idx].set(topk_w)
        expert_out = jnp.einsum('bsd,eod->bseo', x, W_experts) + b_experts
        return jnp.einsum('bseo,bse->bso', expert_out, router_weights)
    x = x + _L0_xattn_ref(_layernorm(x, axis=-1), ctx_1024, ctx_1024, L0_xattn_Wq, L0_xattn_bq, L0_xattn_Wk, L0_xattn_bk, L0_xattn_Wv, L0_xattn_bv, L0_xattn_Wo, L0_xattn_bo)
    x = x + _L0_ffn_ref(_layernorm(x, axis=-1), L0_ffn_W_experts, L0_ffn_b_experts, L0_ffn_W_router, L0_ffn_b_router)
    return x

_drawn_inputs = setup_inputs


def setup_inputs(seed=0):
    import zlib

    import numpy as np

    out = dict(_drawn_inputs(seed))
    spreads = {'L0_xattn_bq': (0.0, 0.287),
     'L0_xattn_bk': (0.0, 0.8),
     'L0_xattn_bv': (0.0, 0.1),
     'L0_xattn_bo': (0.0, 0.1)}
    factors = {'L0_ffn_b_experts': 8.0}
    for name, (base, spread) in spreads.items():
        noise = np.random.default_rng([zlib.crc32(name.encode()), seed]).standard_normal(out[name].shape)
        drawn = base * np.exp(spread * noise) if base else spread * noise
        out[name] = jnp.asarray(drawn.astype(out[name].dtype))
    for name, factor in factors.items():
        out[name] = (out[name] * factor).astype(out[name].dtype)
    return out
```

```python
from contextlib import ExitStack

import concourse.bass as bass
from concourse import mybir

F32 = mybir.dt.float32
F32R = mybir.dt.float32r
U32 = mybir.dt.uint32
ALU = mybir.AluOpType
ACT = mybir.ActivationFunctionType
AX = mybir.AxisListType
ds = bass.ds

P = 128
CH = 512
EPS = 1e-5
HEADS, DH = 16, 32
HG = P // DH
S_RING = 3
P_RING = 4
LAG = 2
SUM_ON_PE = (6, 12, 18, 24)
K_PIECES = 4


def split(n, parts):
    cuts = [round(n * i / parts) for i in range(parts + 1)]
    return [(a, b - a) for a, b in zip(cuts, cuts[1:])]


def build_program(nc, x, ctxT, Wq, bq, Wk, bk, Wv, bv, Wo, bo, WeT, be, WrT, br, out):
    L, D = x.shape
    S = ctxT.shape[1]
    KT = D // P
    NG = HEADS // HG
    NC = L // CH
    NSC = -(-S // CH)
    NT = -(-S // P)
    SP_ = NT * P
    LAST = S - (NT - 1) * P
    NE = br.shape[0]
    SCALE = float(DH) ** -0.5
    TPC = CH // P

    def dram(name, shape, dt):
        return nc.dram_tensor(name, shape, dt, kind="Internal").ap()

    kh_d = dram("kh_scratch", [P, NG, SP_], F32)
    kl_d = dram("kl_scratch", [P, NG, SP_], F32)
    v_d = dram("v_scratch", [P, NT, D], F32)
    qh_d = dram("qh_scratch", [P, NG, L], F32)
    ql_d = dram("ql_scratch", [P, NG, L], F32)
    shift_d = dram("shift_scratch", [HEADS, L], F32)
    o_d = dram("o_scratch", [D, L], F32)

    ctx = ExitStack()
    with ctx:
        def sb(name, shape, dt, where=None):
            return (where or ctx).enter_context(nc.sbuf_tensor(name, shape, dt))

        def sem(name):
            return ctx.enter_context(nc.semaphore(name))

        psum = ctx.enter_context(nc.psum_tensor("psum", [P, 8, CH], F32))
        ident = sb("ident", [P, P], F32)
        ident_ready = sem("ident_ready")

        projections(nc, ExitStack(), sb, sem, psum, ident, ident_ready, locals())
        attention(nc, ExitStack(), sb, sem, psum, locals())
        experts(nc, ExitStack(), sb, sem, psum, ident, locals())


def projections(nc, mem, sb0, sem, psum, ident, ident_ready, g):
    L, D, S, KT, NG, NC, NSC, NT, LAST, TPC = (g[n] for n in "L D S KT NG NC NSC NT LAST TPC".split())
    x, ctxT, kh_d, kl_d, v_d, qh_d, ql_d = (g[n] for n in "x ctxT kh_d kl_d v_d qh_d ql_d".split())
    last_w = S - (NSC - 1) * CH

    with mem:
        def sb(name, shape, dt):
            return sb0(name, shape, dt, mem)

        w_raw = [sb(f"w_raw_{n}", [P, KT, D], F32) for n in "kvq"]
        w_hi = [sb(f"w_hi_{n}", [P, KT, D], F32R) for n in "kvq"]
        w_lo = [sb(f"w_lo_{n}", [P, KT, D], F32R) for n in "kvq"]
        bk_col = sb("bk_col", [P, NG], F32)
        bq_col = sb("bq_col", [P, NG], F32)
        bv_all = sb("bv_all", [P, D], F32)
        raw = [sb(f"raw{b}", [P, TPC, CH], F32) for b in range(2)]
        a_hi = [sb(f"a_hi{b}", [P, KT, CH], F32R) for b in range(2)]
        a_lo = [sb(f"a_lo{b}", [P, KT, CH], F32R) for b in range(2)]
        o_hi = [sb(f"o_hi{b}", [P, NG, CH], F32R) for b in range(2)]
        o_lo = [sb(f"o_lo{b}", [P, NG, CH], F32R) for b in range(2)]
        v_sb = [sb(f"v_sb{b}", [P, TPC, D], F32) for b in range(2)]
        xn = [sb(f"xn{b}", [P, TPC, D], F32) for b in range(2)]
        stats = sb("stats", [P, TPC, 6], F32)
        mv = sb("mv", [P, TPC, 2], F32)
        var = sb("var", [P, TPC], F32)
        std = sb("std", [P, TPC], F32)
        rstd = sb("rstd", [P, TPC], F32)
        tmp = sb("tmp", [P, TPC], F32)

        w_in = [sem(f"w_in_{n}") for n in "kvq"]
        bias_in = sem("bias_in")
        w_hi_ready = sem("w_hi_ready")
        w_lo_ready = sem("w_lo_ready")
        wq_lo_ready = sem("wq_lo_ready")
        c_in = [sem(f"c_in{b}") for b in range(2)]
        x_in = [sem(f"x_in{b}") for b in range(2)]
        c_hi = sem("c_hi")
        c_lo = sem("c_lo")
        k_mm = sem("k_mm")
        v_mm = sem("v_mm")
        k_hi = sem("k_hi")
        k_lo = sem("k_lo")
        v_out = sem("v_out")
        k_stored = [sem(f"k_stored{b}") for b in range(2)]
        v_stored = [sem(f"v_stored{b}") for b in range(2)]
        ln_step = sem("ln_step")
        stats_ready = sem("stats_ready")
        stats_passed = sem("stats_passed")
        var_ready = sem("var_ready")
        std_ready = sem("std_ready")
        xn_ready = sem("xn_ready")
        x_turned = sem("x_turned")
        x_hi = sem("x_hi")
        x_lo = sem("x_lo")
        q_mm = sem("q_mm")
        q_hi = sem("q_hi")
        q_lo = sem("q_lo")
        q_stored = [sem(f"q_stored{b}") for b in range(2)]

        ctx_v = ctxT.rearrange("(k p) s -> p k s", p=P)
        x_v = x.rearrange("(u p s) d -> p s u d", p=P, s=HEADS)
        per_place = L // HEADS // P
        places = TPC // per_place
        pairs = (NSC - 1) // 2
        assert NSC % 2 == 1 and NC % 2 == 0
        LN_STEPS = TPC + 5

        with nc.Block() as block:
            @block.sync
            def _(sp):
                def load_ctx(c, b, w):
                    sp.dma_start(raw[b][:, :, 0:w], ctx_v[:, :, ds(c * CH, w)]).then_inc(c_in[b], 16)

                sp.dma_start(w_raw[0][:], g["Wk"].rearrange("(k p) n -> p k n", p=P)).then_inc(w_in[0], 16)
                load_ctx(0, 0, CH)
                sp.dma_start(w_raw[1][:], g["Wv"].rearrange("(k p) n -> p k n", p=P)).then_inc(w_in[1], 16)
                sp.dma_start(bk_col[:], g["bk"]).then_inc(bias_in, 16)
                sp.dma_start(bq_col[:], g["bq"]).then_inc(bias_in, 16)
                sp.dma_start(bv_all[:], g["bv"].rearrange("(o n) -> o n", o=1).to_broadcast([P, D])).then_inc(bias_in, 16)
                load_ctx(1, 1, CH)
                sp.dma_start(w_raw[2][:], g["Wq"].rearrange("(k p) n -> p k n", p=P)).then_inc(w_in[2], 16)

                def store_kv(c, b, w):
                    sp.wait_ge(k_hi, (c + 1) * NG)
                    sp.wait_ge(k_lo, (c + 1) * NG)
                    sp.dma_start(kh_d[:, :, ds(c * CH, w)], o_hi[b][:, :, 0:w].bitcast(F32)).then_inc(k_stored[b], 16)
                    sp.dma_start(kl_d[:, :, ds(c * CH, w)], o_lo[b][:, :, 0:w].bitcast(F32)).then_inc(k_stored[b], 16)
                    if w == CH:
                        sp.wait_ge(v_out, (c + 1) * TPC)
                        sp.dma_start(v_d[:, ds(c * TPC, TPC), :], v_sb[b][:]).then_inc(v_stored[b], 16)
                    else:
                        full = w // P
                        sp.wait_ge(v_out, c * TPC + full + 1)
                        sp.dma_start(v_d[:, ds(c * TPC, full), :], v_sb[b][:, 0:full, :]).then_inc(v_stored[b], 16)
                        sp.dma_start(v_d[0:LAST, ds(c * TPC + full, 1), :], v_sb[b][0:LAST, full:full + 1, :]).then_inc(v_stored[b], 16)

                with sp.Fori(0, pairs - 1) as i:
                    for b in range(2):
                        c = i * 2 + b
                        sp.wait_ge(c_hi, c + 1)
                        sp.wait_ge(c_lo, c + 1)
                        load_ctx(c + 2, b, CH)
                        store_kv(c, b, CH)
                c = 2 * (pairs - 1)
                sp.wait_ge(c_hi, c + 1)
                sp.wait_ge(c_lo, c + 1)
                load_ctx(c + 2, 0, last_w)
                store_kv(c, 0, CH)
                store_kv(c + 1, 1, CH)

                def load_x(c, b):
                    for s in range(places):
                        sp.dma_start(raw[b][:, s * per_place:(s + 1) * per_place, :],
                                     x_v[:, ds(c * places + s, 1), :, :].rearrange("p s u d -> p (s u) d")).then_inc(x_in[b], 16)

                sp.wait_ge(c_hi, NSC)
                sp.wait_ge(c_lo, NSC)
                load_x(0, 0)
                load_x(1, 1)
                store_kv(c + 2, 0, last_w)

                def store_q(c, b):
                    sp.wait_ge(q_hi, (c + 1) * NG)
                    sp.wait_ge(q_lo, (c + 1) * NG)
                    sp.dma_start(qh_d[:, :, ds(c * CH, CH)], o_hi[b][:].bitcast(F32)).then_inc(q_stored[b], 16)
                    sp.dma_start(ql_d[:, :, ds(c * CH, CH)], o_lo[b][:].bitcast(F32)).then_inc(q_stored[b], 16)

                with sp.Fori(0, NC // 2 - 1) as i:
                    for b in range(2):
                        c = i * 2 + b
                        sp.wait_ge(xn_ready, c + 1)
                        load_x(c + 2, b)
                        store_q(c, b)
                for b in range(2):
                    store_q(NC - 2 + b, b)
                for b in range(2):
                    sp.wait_ge(k_stored[b], 32 * ((NSC + 1 - b) // 2))
                    sp.wait_ge(v_stored[b], 16 * ((NSC + 1 - b) // 2 + (1 - b)))
                    sp.wait_ge(q_stored[b], 32 * (NC // 2))

            @block.gpsimd
            def _(pool):
                pool.memset(ident[:], 0.0).then_inc(ident_ready, 1)
                pool.wait_ge(ident_ready, 1)
                pool.affine_select(out=ident[:], in_=ident[:], compare_op=ALU.not_equal, fill=1.0,
                                   base=0, pattern=[[-1, P]], channel_multiplier=1).then_inc(ident_ready, 1)
                pool.wait_ge(w_in[2], 16)
                pool.wait_ge(w_hi_ready, 3)
                pool.tensor_tensor(w_lo[2][:], w_raw[2][:], w_hi[2][:].bitcast(F32), ALU.subtract).then_inc(wq_lo_ready, 1)

            @block.scalar
            def _(act):
                act.wait_ge(w_in[0], 16)
                act.activation(w_hi[0][:], w_raw[0][:], ACT.Copy).then_inc(w_hi_ready, 1)

                def ctx_chunk(c, b, i, w):
                    act.wait_ge(c_in[b], 16 * (i + 1))
                    if not (isinstance(c, int) and c == 0):
                        act.wait_ge(v_mm, (c - 1) * TPC)
                    act.activation(a_hi[b][:, :, 0:w], raw[b][:, :, 0:w], ACT.Copy).then_inc(c_hi, 1)

                def k_chunk(c, b, i, w):
                    act.wait_ge(k_stored[b], i * 32)
                    for j in range(NG):
                        act.wait_ge(k_mm, c * NG + (j + 1))
                        act.activation(o_hi[b][:, j, 0:w], psum[:, j, 0:w], ACT.Identity,
                                       bias=bk_col[:, j:j + 1]).then_inc(k_hi, 1)

                ctx_chunk(0, 0, 0, CH)
                act.wait_ge(w_in[1], 16)
                act.activation(w_hi[1][:], w_raw[1][:], ACT.Copy).then_inc(w_hi_ready, 1)
                act.wait_ge(w_in[2], 16)
                act.activation(w_hi[2][:], w_raw[2][:], ACT.Copy).then_inc(w_hi_ready, 1)
                act.wait_ge(bias_in, 48)

                def ctx_pair(i, w_next):
                    k_chunk(i * 2, 0, i, CH)
                    ctx_chunk(i * 2 + 1, 1, i, CH)
                    k_chunk(i * 2 + 1, 1, i, CH)
                    ctx_chunk(i * 2 + 2, 0, i + 1, w_next)

                with act.Fori(0, pairs - 1) as i:
                    ctx_pair(i, CH)
                ctx_pair(pairs - 1, last_w)
                k_chunk(NSC - 1, 0, pairs, last_w)

                def x_stats(c):
                    act.wait_ge(var_ready, c + 1)
                    act.activation(std[:], var[:], ACT.Sqrt).then_inc(std_ready, 1)

                def x_split(c, b):
                    for k in range(KT):
                        act.wait_ge(x_turned, c * KT + (k + 1))
                        act.activation(a_hi[b][:, k, :], psum[:, k, :], ACT.Copy).then_inc(x_hi, 1)

                def q_chunk(c, b, first_stored):
                    act.wait_ge(q_stored[b], first_stored)
                    for j in range(NG):
                        act.wait_ge(q_mm, c * NG + (j + 1))
                        act.activation(o_hi[b][:, j, :], psum[:, 4 + j, :], ACT.Identity,
                                       bias=bq_col[:, j:j + 1]).then_inc(q_hi, 1)

                x_stats(0)
                act.wait_ge(v_mm, (NSC - 1) * TPC + last_w // P + 1)
                for b in range(2):
                    act.wait_ge(k_stored[b], 32 * ((NSC + 1 - b) // 2))
                x_split(0, 0)
                with act.Fori(0, NC // 2 - 1) as i:
                    for b in range(2):
                        c = i * 2 + b
                        x_stats(c + 1)
                        x_split(c + 1, 1 - b)
                        q_chunk(c, b, i * 32)
                c = NC - 2
                x_stats(c + 1)
                x_split(c + 1, 1)
                q_chunk(c, 0, 32 * (NC // 2 - 1))
                q_chunk(c + 1, 1, 32 * (NC // 2 - 1))

            @block.vector
            def _(dve):
                def w_low(n):
                    dve.wait_ge(w_hi_ready, n + 1)
                    dve.tensor_tensor(w_lo[n][:], w_raw[n][:], w_hi[n][:].bitcast(F32), ALU.subtract).then_inc(w_lo_ready, 1)

                def ctx_low(c, b, w):
                    dve.wait_ge(c_hi, c + 1)
                    dve.tensor_tensor(a_lo[b][:, :, 0:w], raw[b][:, :, 0:w], a_hi[b][:, :, 0:w].bitcast(F32),
                                      ALU.subtract).then_inc(c_lo, 1)

                def k_low(c, b, w):
                    for j in range(NG):
                        dve.wait_ge(k_hi, c * NG + (j + 1))
                        dve.scalar_tensor_tensor(out=o_lo[b][:, j, 0:w], in0=psum[:, j, 0:w], scalar=bk_col[:, j:j + 1],
                                                 in1=o_hi[b][:, j, 0:w].bitcast(F32), op0=ALU.add, op1=ALU.subtract).then_inc(k_lo, 1)

                def v_chunk(c, b, i, w):
                    dve.wait_ge(v_stored[b], i * 16)
                    for t in range(-(-w // P)):
                        n = min(P, w - t * P)
                        dve.wait_ge(v_mm, c * TPC + (t + 1))
                        dve.tensor_tensor(v_sb[b][0:n, t, :], psum[0:n, 4 + t, :], bv_all[0:n, :], ALU.add).then_inc(v_out, 1)

                w_low(0)
                ctx_low(0, 0, CH)
                w_low(1)
                dve.wait_ge(bias_in, 48)

                def ctx_pair(i, w_next):
                    k_low(i * 2, 0, CH)
                    ctx_low(i * 2 + 1, 1, CH)
                    v_chunk(i * 2, 0, i, CH)
                    k_low(i * 2 + 1, 1, CH)
                    ctx_low(i * 2 + 2, 0, w_next)
                    v_chunk(i * 2 + 1, 1, i, CH)

                with dve.Fori(0, pairs - 1) as i:
                    ctx_pair(i, CH)
                ctx_pair(pairs - 1, last_w)
                k_low(NSC - 1, 0, last_w)
                v_chunk(NSC - 1, 0, pairs, last_w)

                def ln(c, b, i):
                    base = c * LN_STEPS
                    n = [0]

                    def step(ins, wait=True):
                        n[0] += 1
                        ins.then_inc(ln_step, 1)
                        if wait:
                            dve.wait_ge(ln_step, base + n[0])

                    dve.wait_ge(x_in[b], (16 * places) * (i + 1))
                    for t in range(TPC):
                        ins = dve.bn_stats(stats[:, t, :], raw[b][:, t, :])
                    ins.then_inc(stats_ready, 1)
                    dve.wait_ge(stats_ready, c + 1)
                    dve.sem_inc(stats_passed, 1)
                    for t in range(TPC):
                        step(dve.bn_aggr(mv[:, t, :], stats[:, t, :]), t == TPC - 1)
                    dve.tensor_scalar(var[:], mv[:, :, 1], EPS, None, ALU.add).then_inc(var_ready, 1)
                    dve.wait_ge(std_ready, c + 1)
                    step(dve.reciprocal(rstd[:], std[:]))
                    step(dve.tensor_tensor(tmp[:], rstd[:], rstd[:], ALU.mult))
                    step(dve.tensor_tensor(tmp[:], tmp[:], var[:], ALU.mult))
                    step(dve.tensor_scalar(tmp[:], tmp[:], -0.5, 1.5, ALU.mult, ALU.add))
                    step(dve.tensor_tensor(rstd[:], rstd[:], tmp[:], ALU.mult))
                    assert n[0] == LN_STEPS
                    for t in range(TPC):
                        ins = dve.tensor_scalar(xn[b][:, t, :], raw[b][:, t, :], mv[:, t, 0:1], rstd[:, t:t + 1],
                                                ALU.subtract, ALU.mult)
                    ins.then_inc(xn_ready, 1)

                def x_low(c, b):
                    for k in range(KT):
                        dve.wait_ge(x_hi, c * KT + (k + 1))
                        dve.tensor_tensor(a_lo[b][:, k, :], psum[:, k, :], a_hi[b][:, k, :].bitcast(F32),
                                          ALU.subtract).then_inc(x_lo, 1)

                def q_low(c, b):
                    for j in range(NG):
                        dve.wait_ge(q_hi, c * NG + (j + 1))
                        dve.scalar_tensor_tensor(out=o_lo[b][:, j, :], in0=psum[:, 4 + j, :], scalar=bq_col[:, j:j + 1],
                                                 in1=o_hi[b][:, j, :].bitcast(F32), op0=ALU.add, op1=ALU.subtract).then_inc(q_lo, 1)

                ln(0, 0, 0)
                x_low(0, 0)
                with dve.Fori(0, NC // 2 - 1) as i:
                    ln(i * 2 + 1, 1, i)
                    x_low(i * 2 + 1, 1)
                    q_low(i * 2, 0)
                    ln(i * 2 + 2, 0, i + 1)
                    x_low(i * 2 + 2, 0)
                    q_low(i * 2 + 1, 1)
                ln(NC - 1, 1, NC // 2 - 1)
                x_low(NC - 1, 1)
                q_low(NC - 2, 0)
                q_low(NC - 1, 1)

            @block.tensor
            def _(pe):
                def products(bank, m, n, lhs, rhs):
                    terms = [(k, a, b) for k in range(KT) for a, b in ((0, 0), (0, 1), (1, 0))]
                    for q, (k, a, b) in enumerate(terms):
                        mm = pe.matmul(psum[0:m, bank, 0:n], lhs[a](k), rhs[b](k), start=q == 0, stop=q == len(terms) - 1)
                    return mm

                def k_products(c, b, w):
                    pe.wait_ge(c_hi, c + 1)
                    pe.wait_ge(c_lo, c + 1)
                    pe.wait_ge(k_lo, c * NG)
                    for j in range(NG):
                        products(j, P, w, [lambda k, W=W: W[0][:, k, j * P:(j + 1) * P] for W in (w_hi, w_lo)],
                                 [lambda k, A=A: A[b][:, k, 0:w] for A in (a_hi, a_lo)]).then_inc(k_mm, 1)

                def v_products(c, b, w):
                    pe.wait_ge(v_out, c * TPC)
                    for t in range(-(-w // P)):
                        products(4 + t, P, D, [lambda k, A=A: A[b][:, k, t * P:(t + 1) * P] for A in (a_hi, a_lo)],
                                 [lambda k, W=W: W[1][:, k, :] for W in (w_hi, w_lo)]).then_inc(v_mm, 1)

                pe.wait_ge(w_hi_ready, 1)
                pe.wait_ge(w_lo_ready, 1)
                k_products(0, 0, CH)
                pe.wait_ge(w_hi_ready, 2)
                pe.wait_ge(w_lo_ready, 2)

                def ctx_pair(i, w_next):
                    v_products(i * 2, 0, CH)
                    k_products(i * 2 + 1, 1, CH)
                    v_products(i * 2 + 1, 1, CH)
                    k_products(i * 2 + 2, 0, w_next)

                with pe.Fori(0, pairs - 1) as i:
                    ctx_pair(i, CH)
                ctx_pair(pairs - 1, last_w)
                v_products(NSC - 1, 0, last_w)

                def turn(c, b):
                    pe.wait_ge(xn_ready, c + 1)
                    pe.wait_ge(x_lo, c * KT)
                    for k in range(KT):
                        for t in range(TPC):
                            mm = pe.transpose(psum[:, k, t * P:(t + 1) * P], xn[b][:, t, k * P:(k + 1) * P], ident[:])
                        mm.then_inc(x_turned, 1)

                def q_products(c, b, js):
                    pe.wait_ge(x_hi, (c + 1) * KT)
                    pe.wait_ge(x_lo, (c + 1) * KT)
                    pe.wait_ge(q_lo, c * NG)
                    for j in js:
                        products(4 + j, P, CH, [lambda k, W=W: W[2][:, k, j * P:(j + 1) * P] for W in (w_hi, w_lo)],
                                 [lambda k, A=A: A[b][:, k, :] for A in (a_hi, a_lo)]).then_inc(q_mm, 1)

                pe.wait_ge(ident_ready, 2)
                pe.wait_ge(k_lo, NSC * NG)
                turn(0, 0)
                pe.wait_ge(v_out, (NSC - 1) * TPC + last_w // P + 1)
                pe.wait_ge(w_hi_ready, 3)
                pe.wait_ge(wq_lo_ready, 1)
                half = NG // 2
                with pe.Fori(0, NC // 2 - 1) as i:
                    for b in range(2):
                        c = i * 2 + b
                        q_products(c, b, range(half))
                        turn(c + 1, 1 - b)
                        q_products(c, b, range(half, NG))
                q_products(NC - 2, 0, range(half))
                turn(NC - 1, 1)
                q_products(NC - 2, 0, range(half, NG))
                q_products(NC - 1, 1, range(NG))


def attention(nc, mem, sb0, sem, psum, g):
    S, SP_, NG, NC, NT, LAST, SCALE, D = (g[n] for n in "S SP_ NG NC NT LAST SCALE D".split())
    kh_d, kl_d, v_d, qh_d, ql_d, shift_d, o_d = (g[n] for n in "kh_d kl_d v_d qh_d ql_d shift_d o_d".split())
    NIT = NG * NC
    NP = 2 * NT
    ROWS = 3 * DH
    SH = ROWS
    TPC = CH // P

    with mem:
        def sb(name, shape, dt):
            return sb0(name, shape, dt, mem)

        k_st = sb("k_st", [SH + 1, HG, SP_], F32R)
        q_st = sb("q_st", [SH + 1, HG, CH], F32R)
        q_next = sb("q_next", [SH + 1, HG, CH], F32)
        v_st = sb("v_st", [P, NT, P], F32)
        ones = sb("ones", [P, DH], F32)
        ones_last = sb("ones_last", [P, DH], F32)
        probs = sb("probs", [P, P_RING, HG, CH], F32)
        sums = sb("sums", [P, HG, CH], F32)
        recip = sb("recip", [P, CH], F32)
        o_sb = sb("o_sb", [P, CH], F32)
        mx = sb("mx", [P, TPC, HG, 2], F32)
        mxx = sb("mxx", [P, HG, TPC], F32)
        neg = sb("neg", [P, HG, TPC], F32R)

        pieces = split(NT, K_PIECES)
        piece_of = {a: n for n, (a, _) in enumerate(pieces)}

        filled = sem("filled")
        row_filled = sem("row_filled")
        ma_k_in = sem("ma_k_in")
        ma_q_in = sem("ma_q_in")
        ma_mm = sem("ma_mm")
        ma_max = sem("ma_max")
        ma_neg = sem("ma_neg")
        ma_fold = sem("ma_fold")
        ma_stored = sem("ma_stored")
        q_in = sem("q_in")
        q_ready = sem("q_ready")
        k_in = [sem(f"k_in{n}") for n in range(K_PIECES)]
        v_in = [sem(f"v_in{n}") for n in range(K_PIECES)]
        s_ready = sem("s_ready")
        exp_done = sem("exp_done")
        pv_done = sem("pv_done")
        added = sem("added")
        o_ready = sem("o_ready")
        inverted = sem("inverted")
        o_left = sem("o_left")
        o_stored = sem("o_stored")

        def load_k(sp, j, first, n, count):
            for r, src in enumerate((kh_d, kh_d, kl_d)):
                sp.dma_start(k_st[r * DH:(r + 1) * DH, :, first:first + n].bitcast(F32),
                             src[:, ds(j, 1), first:first + n].rearrange("(h d) o s -> d (h o) s", d=DH)).then_inc(count, 16)

        def load_q(sp, dst, j, c, count):
            for r, src in enumerate((qh_d, ql_d, qh_d)):
                sp.dma_start(dst[r * DH:(r + 1) * DH, :, :],
                             src[:, ds(j, 1), ds(c * CH, CH)].rearrange("(h d) o s -> d (h o) s", d=DH)).then_inc(count, 16)

        s_slot = [n % S_RING for n in range(NP)]
        if NP % S_RING == 1:
            s_slot[-1] = 1
        s_prev = [max([m for m in range(n) if s_slot[m] == s_slot[n]], default=None) for n in range(NP)]
        on_pe = set(SUM_ON_PE) | {NT - 1}
        on_dve = [t for t in range(NT) if t not in on_pe]
        adds = len(on_dve) - 1
        add_of = {t: max(n, 1) for n, t in enumerate(on_dve)}
        assert 0 in on_dve and 1 in on_dve

        with nc.Block() as block:
            @block.gpsimd
            def _(pool):
                pool.memset(k_st[SH:SH + 1, :, 0:S].bitcast(F32), 1.0).then_inc(row_filled, 1)

            @block.sync
            def _(sp):
                with sp.Fori(0, NG) as j:
                    sp.wait_ge(ma_mm, j * (NC * TPC * HG * 2))
                    load_k(sp, j, 0, S, ma_k_in)
                    with sp.Fori(0, NC) as c:
                        sp.wait_ge(ma_mm, j * (NC * TPC * HG * 2) + c * (TPC * HG * 2))
                        load_q(sp, q_st[:].bitcast(F32), j, c, ma_q_in)
                        sp.wait_ge(ma_neg, j * NC + c + 1)
                        for h in range(HG):
                            sp.dma_start(shift_d[ds(j * HG + h, 1), ds(c * CH, CH)].rearrange("h (t p) -> p (h t)", p=P),
                                         neg[:, h, :].bitcast(F32), allow_slow_non_contiguous=True).then_inc(ma_stored, 16)
                sp.wait_ge(ma_stored, NIT * HG * 16)

                def queries(j, c):
                    load_q(sp, q_next, j, c, q_in)
                    sp.dma_start(q_next[SH:SH + 1, :, :], shift_d[ds(j * HG, HG), ds(c * CH, CH)].rearrange("(o h) l -> o h l", o=1)).then_inc(q_in, 16)

                def keys_values(j, before):
                    for n, (a, m) in enumerate(pieces):
                        if before is not None:
                            sp.wait_ge(s_ready, before * NP + 2 * (a + m))
                        load_k(sp, j, a * P, min((a + m) * P, S) - a * P, k_in[n])
                        if before is not None:
                            sp.wait_ge(pv_done, before * NT + (a + m))
                        full = m - (n == K_PIECES - 1)
                        sp.dma_start(v_st[:, a:a + full, :], v_d[:, a:a + full, ds(j * P, P)]).then_inc(v_in[n], 16)
                        if n == K_PIECES - 1:
                            sp.dma_start(v_st[0:LAST, NT - 1, :], v_d[0:LAST, NT - 1, ds(j * P, P)]).then_inc(v_in[n], 16)

                def result(j, c, it):
                    sp.wait_ge(o_left, it + 1)
                    sp.dma_start(o_d[ds(j * P, P), ds(c * CH, CH)], o_sb[:]).then_inc(o_stored, 16)

                queries(0, 0)
                sp.wait_ge(filled, 5)
                keys_values(0, None)

                def group(j, last):
                    with sp.Fori(0, NC - 1) as c:
                        it = j * NC + c
                        sp.wait_ge(q_ready, it + 1)
                        queries(j, c + 1)
                        result(j, c, it)
                    it = j * NC + NC - 1
                    if not last:
                        sp.wait_ge(q_ready, it + 1)
                        queries(j + 1, 0)
                        keys_values(j + 1, it)
                    result(j, NC - 1, it)

                with sp.Fori(0, NG - 1) as j:
                    group(j, False)
                group(NG - 1, True)
                sp.wait_ge(o_stored, NIT * 16)

            @block.scalar
            def _(act):
                act.preload_act_table(ACT.Exp)
                act.wait_ge(filled, 5)
                with act.Fori(0, NIT) as it:
                    act.wait_ge(q_in, (it + 1) * 64)
                    act.wait_ge(s_ready, it * NP)
                    nc.scalar.activation(q_st[:], q_next[:], ACT.Copy).then_inc(q_ready, 1)
                    for n in range(NP):
                        t, half = divmod(n, 2)
                        act.wait_ge(s_ready, it * NP + (n + 1))
                        if half == 0:
                            if t >= P_RING:
                                act.wait_ge(pv_done, it * NT + (t - P_RING + 1))
                                if t - P_RING in add_of:
                                    act.wait_ge(added, it * adds + add_of[t - P_RING])
                            elif t == 0:
                                act.wait_ge(pv_done, it * NT)
                                act.wait_ge(added, it * adds)
                        nc.scalar.activation(probs[:, t % P_RING, 2 * half:2 * half + 2, :],
                                             psum[:, 2 * s_slot[n]:2 * s_slot[n] + 2, :], ACT.Exp, scale=SCALE).then_inc(exp_done, 1)

            @block.vector
            def _(dve):
                dve.memset(k_st[:, :, S:SP_].bitcast(F32), 0.0).then_inc(filled, 1)
                dve.memset(v_st[:, NT - 1, :], 0.0).then_inc(filled, 1)
                dve.memset(ones[:], 1.0).then_inc(filled, 1)
                dve.memset(ones_last[:], 0.0).then_inc(filled, 1)
                dve.wait_ge(filled, 4)
                dve.memset(ones_last[0:LAST, :], 1.0).then_inc(filled, 1)

                with dve.Fori(0, NIT) as it:
                    k = 0
                    for t in range(TPC):
                        for h in range(HG):
                            for half in range(2):
                                k += 1
                                dve.wait_ge(ma_mm, it * (TPC * HG * 2) + k)
                                w = 4 * CH if half == 0 else S - 4 * CH
                                dve.tensor_reduce(mx[:, t, h, half:half + 1],
                                                  psum[:, 4 * half:8, :].rearrange("p b n -> p (b n)")[:, 0:w], AX.X, ALU.max).then_inc(ma_max, 1)
                    dve.wait_ge(ma_max, (it + 1) * (TPC * HG * 2))
                    dve.tensor_tensor(mxx[:], mx[:, :, :, 0].rearrange("p t h -> p h t"), mx[:, :, :, 1].rearrange("p t h -> p h t"),
                                      ALU.max).then_inc(ma_fold, 1)
                    dve.wait_ge(ma_fold, it + 1)
                    dve.wait_ge(ma_stored, it * (HG * 16))
                    dve.tensor_scalar(neg[:], mxx[:], -1.0, None, ALU.mult).then_inc(ma_neg, 1)

                with dve.Fori(0, NIT) as it:
                    k = 0
                    for t in on_dve[1:]:
                        dve.wait_ge(exp_done, it * NP + (2 * t + 2))
                        if k == 0:
                            dve.wait_ge(o_ready, it)
                            a = probs[:, on_dve[0] % P_RING]
                        else:
                            dve.wait_ge(added, it * adds + k)
                            a = sums[:]
                        nc.vector.tensor_tensor(sums[:], a, probs[:, t % P_RING], ALU.add).then_inc(added, 1)
                        k += 1
                    dve.wait_ge(o_ready, it + 1)
                    nc.vector.reciprocal(recip[:], psum[:, 7, :]).then_inc(inverted, 1)
                    dve.wait_ge(inverted, it + 1)
                    dve.wait_ge(o_stored, it * 16)
                    nc.vector.tensor_tensor(o_sb[:], psum[:, 6, :], recip[:], ALU.mult).then_inc(o_left, 1)

            @block.tensor
            def _(pe):
                with pe.Fori(0, NG) as j:
                    with pe.Fori(0, NC) as c:
                        it = j * NC + c
                        pe.wait_ge(ma_k_in, (j + 1) * 48)
                        pe.wait_ge(ma_q_in, (it + 1) * 48)
                        k = 0
                        for t in range(TPC):
                            for h in range(HG):
                                for half in range(2):
                                    if k >= 2:
                                        pe.wait_ge(ma_max, it * (TPC * HG * 2) + (k - 1))
                                    elif k == 0:
                                        pe.wait_ge(ma_max, it * (TPC * HG * 2))
                                    k += 1
                                    for b in range(4 * half, min(4 * half + 4, -(-S // CH))):
                                        w = min(CH, S - b * CH)
                                        mm = pe.matmul(psum[:, b, 0:w], q_st[0:ROWS, h, t * P:(t + 1) * P],
                                                       k_st[0:ROWS, h, b * CH:b * CH + w], start=True, stop=True)
                                    mm.then_inc(ma_mm, 1)

                def weigh(it, t, j):
                    if t in piece_of:
                        n = piece_of[t]
                        pe.wait_ge(v_in[n], (j + 1) * (16 * (1 + (n == K_PIECES - 1))))
                    pe.wait_ge(exp_done, it * NP + (2 * t + 2))
                    if t == 0:
                        pe.wait_ge(o_left, it)
                    for h in range(HG):
                        mm = nc.tensor.matmul(psum[h * DH:(h + 1) * DH, 6, :], v_st[:, t, h * DH:(h + 1) * DH],
                                              probs[:, t % P_RING, h, :], start=t == 0, stop=t == NT - 1)
                    if t in on_pe:
                        for h in range(HG):
                            mm = nc.tensor.matmul(psum[h * DH:(h + 1) * DH, 7, :], (ones_last if t == NT - 1 else ones)[:],
                                                  probs[:, t % P_RING, h, :], start=t == min(on_pe), stop=False)
                    mm.then_inc(pv_done, 1)

                pe.wait_ge(filled, 5)
                pe.wait_ge(row_filled, 1)
                with pe.Fori(0, NG) as j:
                    with pe.Fori(0, NC) as c:
                        it = j * NC + c
                        pe.wait_ge(q_ready, it + 1)
                        for t in range(NT + LAG):
                            if t < NT:
                                if t in piece_of:
                                    pe.wait_ge(k_in[piece_of[t]], (j + 1) * 48)
                                for half in range(2):
                                    n = 2 * t + half
                                    if s_prev[n] is not None:
                                        pe.wait_ge(exp_done, it * NP + (s_prev[n] + 1))
                                    for e in range(2):
                                        h = 2 * half + e
                                        mm = nc.tensor.matmul(psum[:, 2 * s_slot[n] + e, :], k_st[:, h, t * P:(t + 1) * P],
                                                              q_st[:, h, :], start=True, stop=True)
                                        if e == 1:
                                            mm.then_inc(s_ready, 1)
                            if t >= LAG:
                                weigh(it, t - LAG, j)
                        pe.wait_ge(added, (it + 1) * adds)
                        for h in range(HG):
                            mm = nc.tensor.matmul(psum[h * DH:(h + 1) * DH, 7, :], ones[:], sums[:, h, :], start=False, stop=True)
                        mm.then_inc(o_ready, 1)


def experts(nc, mem, sb0, sem, psum, ident, g):
    L, D, KT, NG, NE = (g[n] for n in "L D KT NG NE".split())
    x, o_d, out, Wo, WeT, WrT = (g[n] for n in "x o_d out Wo WeT WrT".split())
    NTL = L // P
    assert NTL == 2 * HEADS
    ROUND = 4
    WO_BANK, T_BANK, R_BANK, B_BANK = 4, 5, 6, 7

    with mem:
        def sb(name, shape, dt):
            return sb0(name, shape, dt, mem)

        we_hi = sb("we_hi", [P, KT, NE, D], F32R)
        we_lo = sb("we_lo", [P, KT, NE, D], F32R)
        w_raw = [sb(f"we_raw{b}", [P, KT, D], F32) for b in range(2)]
        wo_hi = sb("wo_hi", [P, NG, D], F32R)
        wo_lo = sb("wo_lo", [P, NG, D], F32R)
        wr_raw = sb("wr_raw", [P, KT, NE], F32)
        wr_hi = sb("wr_hi", [P, KT, NE], F32R)
        wr_lo = sb("wr_lo", [P, KT, NE], F32R)
        bo_all = sb("bo_all", [P, D], F32)
        br_all = sb("br_all", [P, NE], F32)
        be_sb = sb("be_sb", [NE, D], F32)
        number = sb("number", [P, NE], F32)

        def two(name, shape, dt):
            return [sb(f"{name}{b}", shape, dt) for b in range(2)]

        o_raw = two("o_raw", [P, NG, P], F32)
        x_raw = two("x_raw", [P, D], F32)
        xb = two("xb", [P, D], F32)
        o_hi = two("att_hi", [P, NG, P], F32R)
        o_lo = two("att_lo", [P, NG, P], F32R)
        y = two("y", [P, D], F32)
        yn = sb("yn", [P, D], F32)
        y_hi = two("y_hi", [P, KT, P], F32R)
        y_lo = two("y_lo", [P, KT, P], F32R)
        acc = two("acc", [P, D], F32)
        w = two("w", [P, NE], F32)
        wT = sb("wT", [NE, P], F32)
        stats = sb("stats3", [P, 6], F32)
        mv = sb("mv3", [P, 2], F32)
        var = sb("var3", [P, 1], F32)
        std = sb("std3", [P, 1], F32)
        rstd = sb("rstd3", [P, 1], F32)
        tmp = sb("tmp3", [P, 1], F32)
        logits = sb("logits", [P, NE], F32)
        top = sb("top", [P, 8], F32)
        top_at = sb("top_at", [P, 8], U32)
        top_at_f = sb("top_at_f", [P, 2], F32)
        neg_top = sb("neg_top", [P, 1], F32)
        ex = sb("ex", [P, NE], F32)
        total = sb("total", [P, 1], F32)
        inv = sb("inv", [P, 1], F32)
        chosen1 = sb("chosen1", [P, NE], F32)
        chosen = sb("chosen", [P, NE], F32)

        small_in = sem("small_in")
        wo_in = sem("wo_in")
        we_in = [sem(f"we_in{b}") for b in range(2)]
        hi_ready = sem("hi_ready")
        lo_ready = sem("lo_ready")
        numbered = sem("numbered")
        t_in = [sem(f"t_in{b}") for b in range(2)]
        att_hi = sem("att_hi_done")
        att_lo = sem("att_lo_done")
        xb_done = sem("xb_done")
        wo_mm = sem("wo_mm")
        chain = sem("chain")
        stats_ready = sem("stats_ready3")
        y_done = sem("y_done")
        var_ready = sem("var_ready3")
        std_ready = sem("std_ready3")
        yn_ready = sem("yn_ready")
        turned = sem("turned")
        yh_done = sem("yh_done")
        yl_done = sem("yl_done")
        r_mm = sem("r_mm")
        logits_ready = sem("logits_ready")
        neg_ready = sem("neg_ready")
        ex_ready = sem("ex_ready")
        w_ready = sem("w_ready")
        w_turned = sem("w_turned")
        wT_ready = sem("wT_ready")
        b_mm = sem("b_mm")
        begun = sem("begun")
        e_mm = sem("e_mm")
        mixed = sem("mixed")
        stored = [sem(f"stored{b}") for b in range(2)]

        CHAIN = 12

        def pairs_of_tiles(eng, body):
            with eng.Fori(0, NTL // 2 - 1) as h:
                for b in range(2):
                    body(h * 2 + b, b, h, False)
            for b in range(2):
                body(NTL - 2 + b, b, NTL // 2 - 1, b == 1)

        with nc.Block() as block:
            @block.sync
            def _(sp):
                def load_tile(i, b, head):
                    o_v = o_d.rearrange("n (k a u r) -> n a k u r", a=HG, u=2, r=P)
                    for a in range(HG):
                        sp.dma_start(o_raw[b][a * DH:(a + 1) * DH, :, :],
                                     o_v[ds(head * DH, DH), a, :, b, :]).then_inc(t_in[b], 16)
                    sp.dma_start(x_raw[b][:], x[ds(i * P, P), :]).then_inc(t_in[b], 16)

                load_tile(0, 0, 0)
                sp.dma_start(w_raw[0][:], Wo.rearrange("(j p) n -> p j n", p=P)).then_inc(wo_in, 16)
                sp.dma_start(wr_raw[:], WrT.rearrange("(k p) e -> p k e", p=P)).then_inc(small_in, 16)
                sp.dma_start(bo_all[:], g["bo"].rearrange("(o n) -> o n", o=1).to_broadcast([P, D])).then_inc(small_in, 16)
                sp.dma_start(br_all[:], g["br"].rearrange("(o n) -> o n", o=1).to_broadcast([P, NE])).then_inc(small_in, 16)
                sp.dma_start(be_sb[:], g["be"]).then_inc(small_in, 16)
                load_tile(1, 1, 0)
                for e in range(NE):
                    b = (e + 1) % 2
                    if e > 0:
                        sp.wait_ge(hi_ready, e + 1)
                        sp.wait_ge(lo_ready, e + 1)
                    sp.dma_start(w_raw[b][:], WeT[:, e * D:(e + 1) * D].rearrange("(k p) n -> p k n", p=P)).then_inc(we_in[b], 16)

                def tile(i, b, h, last):
                    if not (isinstance(h, int)):
                        sp.wait_ge(att_lo, i + 1)
                        sp.wait_ge(xb_done, i + 1)
                        load_tile(i + 2, b, h + 1)
                    sp.wait_ge(mixed, (i + 1) * NE)
                    sp.dma_start(out[ds(i * P, P), :], acc[b][:]).then_inc(stored[b], 16)

                pairs_of_tiles(sp, tile)
                for b in range(2):
                    sp.wait_ge(stored[b], 16 * (NTL // 2))

            @block.gpsimd
            def _(pool):
                pool.iota(number[:], [[1, NE]], base=0, channel_multiplier=0, allow_small_or_imprecise_dtypes=True).then_inc(numbered, 1)
                pool.wait_ge(small_in, 64)

                def inputs(i, b, h):
                    pool.wait_ge(t_in[b], (h + 1) * (16 * (HG + 1)))
                    if not (isinstance(i, int) and i < 2):
                        pool.wait_ge(y_done, i - 1)
                        pool.wait_ge(wo_mm, i - 1)
                    pool.tensor_tensor(xb[b][:], x_raw[b][:], bo_all[:], ALU.add).then_inc(xb_done, 1)
                    pool.wait_ge(att_hi, i + 1)
                    pool.tensor_tensor(o_lo[b][:], o_raw[b][:], o_hi[b][:].bitcast(F32), ALU.subtract).then_inc(att_lo, 1)

                inputs(0, 0, 0)
                inputs(1, 1, 0)
                with pool.Fori(1, NTL // 2) as h:
                    for b in range(2):
                        inputs(h * 2 + b, b, h)

            @block.scalar
            def _(act):
                def att_split(i, b, h):
                    act.wait_ge(t_in[b], (h + 1) * (16 * (HG + 1)))
                    if not (isinstance(i, int) and i < 2):
                        act.wait_ge(wo_mm, i - 1)
                    act.activation(o_hi[b][:], o_raw[b][:], ACT.Copy).then_inc(att_hi, 1)

                def root(i):
                    act.wait_ge(var_ready, i + 1)
                    act.activation(std[:], var[:], ACT.Sqrt).then_inc(std_ready, 1)

                def y_split(i, b):
                    act.wait_ge(turned, i + 1)
                    act.activation(y_hi[b][:], psum[:, T_BANK, :].rearrange("p (k n) -> p k n", k=KT), ACT.Copy).then_inc(yh_done, 1)

                def exps(i):
                    act.wait_ge(neg_ready, i + 1)
                    act.activation(ex[:], logits[:], ACT.Exp, bias=neg_top[:], accum_out=total[:]).then_inc(ex_ready, 1)

                att_split(0, 0, 0)
                act.wait_ge(wo_in, 16)
                act.activation(wo_hi[:], w_raw[0][:], ACT.Copy).then_inc(hi_ready, 1)
                act.wait_ge(small_in, 64)
                act.activation(wr_hi[:], wr_raw[:], ACT.Copy).then_inc(hi_ready, 1)
                att_split(1, 1, 0)
                root(0)
                y_split(0, 0)
                exps(0)
                for e in range(NE):
                    b = (e + 1) % 2
                    act.wait_ge(we_in[b], 16 * (e // 2 + 1))
                    act.activation(we_hi[:, :, e, :], w_raw[b][:], ACT.Copy).then_inc(hi_ready, 1)

                def tile(i, b, h, last):
                    if last:
                        return
                    root(i + 1)
                    y_split(i + 1, 1 - b)
                    exps(i + 1)
                    if not isinstance(h, int):
                        att_split(i + 2, b, h + 1)

                pairs_of_tiles(act, tile)

            @block.vector
            def _(dve):
                def before_turn(i, b, n):
                    def step(ins):
                        n[0] += 1
                        ins.then_inc(chain, 1)
                        dve.wait_ge(chain, i * CHAIN + n[0])

                    dve.wait_ge(wo_mm, i + 1)
                    dve.wait_ge(xb_done, i + 1)
                    dve.tensor_tensor(y[b][:], psum[:, WO_BANK, :], xb[b][:], ALU.add).then_inc(y_done, 1)
                    dve.wait_ge(y_done, i + 1)
                    dve.bn_stats(stats[:], y[b][:]).then_inc(stats_ready, 1)
                    dve.wait_ge(numbered, 1)
                    dve.wait_ge(stats_ready, i + 1)
                    step(dve.bn_aggr(mv[:], stats[:]))
                    dve.tensor_scalar(var[:], mv[:, 1:2], EPS, None, ALU.add).then_inc(var_ready, 1)
                    dve.wait_ge(std_ready, i + 1)
                    step(dve.reciprocal(rstd[:], std[:]))
                    step(dve.tensor_tensor(tmp[:], rstd[:], rstd[:], ALU.mult))
                    step(dve.tensor_tensor(tmp[:], tmp[:], var[:], ALU.mult))
                    step(dve.tensor_scalar(tmp[:], tmp[:], -0.5, 1.5, ALU.mult, ALU.add))
                    step(dve.tensor_tensor(rstd[:], rstd[:], tmp[:], ALU.mult))
                    dve.tensor_scalar(yn[:], y[b][:], mv[:, 0:1], rstd[:], ALU.subtract, ALU.mult).then_inc(yn_ready, 1)

                def after_turn(i, b):
                    dve.wait_ge(yh_done, i + 1)
                    dve.tensor_tensor(y_lo[b][:], psum[:, T_BANK, :].rearrange("p (k n) -> p k n", k=KT),
                                      y_hi[b][:].bitcast(F32), ALU.subtract).then_inc(yl_done, 1)

                def route(i, b, n):
                    def step(ins):
                        n[0] += 1
                        ins.then_inc(chain, 1)
                        dve.wait_ge(chain, i * CHAIN + n[0])

                    dve.wait_ge(r_mm, i + 1)
                    dve.tensor_tensor(logits[:], psum[:, R_BANK, 0:NE], br_all[:], ALU.add).then_inc(logits_ready, 1)
                    dve.wait_ge(numbered, 1)
                    dve.wait_ge(logits_ready, i + 1)
                    step(dve.max(top[:], logits[:]))
                    dve.tensor_scalar(neg_top[:], top[:, 0:1], -1.0, None, ALU.mult).then_inc(neg_ready, 1)
                    step(dve.max_index(top_at[:], top[:], logits[:]))
                    step(dve.tensor_copy(top_at_f[:], top_at[:, 0:2]))
                    step(dve.tensor_scalar(chosen1[:], number[:], top_at_f[:, 0:1], None, ALU.is_equal))
                    dve.scalar_tensor_tensor(out=chosen[:], in0=number[:], scalar=top_at_f[:, 1:2], in1=chosen1[:],
                                             op0=ALU.is_equal, op1=ALU.add).then_inc(chain, 1)
                    n[0] += 1
                    dve.wait_ge(ex_ready, i + 1)
                    dve.reciprocal(inv[:], total[:]).then_inc(chain, 1)
                    n[0] += 1
                    assert n[0] == CHAIN
                    dve.wait_ge(chain, i * CHAIN + n[0])
                    dve.scalar_tensor_tensor(out=w[b][:], in0=ex[:], scalar=inv[:], in1=chosen[:],
                                             op0=ALU.mult, op1=ALU.mult).then_inc(w_ready, 1)

                def copy_wT(i):
                    dve.wait_ge(w_turned, i + 1)
                    dve.tensor_copy(wT[:], psum[0:NE, R_BANK, P:2 * P]).then_inc(wT_ready, 1)

                def begin(i, b, h):
                    dve.wait_ge(b_mm, i + 1)
                    dve.wait_ge(stored[b], h * 16)
                    dve.tensor_tensor(acc[b][:], psum[:, B_BANK, :], y[b][:], ALU.add).then_inc(begun, 1)

                def mix(i, b, es):
                    for e in es:
                        if e == 0:
                            dve.wait_ge(begun, i + 1)
                        else:
                            dve.wait_ge(mixed, i * NE + e)
                        dve.wait_ge(e_mm, i * NE + (e + 1))
                        dve.scalar_tensor_tensor(out=acc[b][:], in0=psum[:, e % ROUND, :], scalar=w[b][:, e:e + 1],
                                                 in1=acc[b][:], op0=ALU.mult, op1=ALU.add).then_inc(mixed, 1)

                dve.wait_ge(hi_ready, 1)
                dve.tensor_tensor(wo_lo[:], w_raw[0][:], wo_hi[:].bitcast(F32), ALU.subtract).then_inc(lo_ready, 1)
                dve.wait_ge(hi_ready, 2)
                dve.tensor_tensor(wr_lo[:], wr_raw[:], wr_hi[:].bitcast(F32), ALU.subtract).then_inc(lo_ready, 1)
                dve.wait_ge(small_in, 64)
                dve.wait_ge(numbered, 1)
                n = [0]
                before_turn(0, 0, n)
                after_turn(0, 0)
                route(0, 0, n)
                copy_wT(0)
                begin(0, 0, 0)
                for e in range(NE):
                    b = (e + 1) % 2
                    dve.wait_ge(hi_ready, e + 3)
                    dve.tensor_tensor(we_lo[:, :, e, :], w_raw[b][:], we_hi[:, :, e, :].bitcast(F32), ALU.subtract).then_inc(lo_ready, 1)

                def tile(i, b, h, last):
                    n = [0]
                    if not last:
                        before_turn(i + 1, 1 - b, n)
                    mix(i, b, (0, 1))
                    if not last:
                        after_turn(i + 1, 1 - b)
                    mix(i, b, (2, 3))
                    if not last:
                        route(i + 1, 1 - b, n)
                    mix(i, b, (4, 5, 6))
                    if not last:
                        copy_wT(i + 1)
                    mix(i, b, (7,))
                    if not last:
                        begin(i + 1, 1 - b, h + b)

                pairs_of_tiles(dve, tile)

            @block.tensor
            def _(pe):
                def products(out_ap, lhs, rhs, parts):
                    terms = [(k, a, b) for k in range(parts) for a, b in ((0, 0), (0, 1), (1, 0))]
                    for q, (k, a, b) in enumerate(terms):
                        mm = pe.matmul(out_ap, lhs[a](k), rhs[b](k), start=q == 0, stop=q == len(terms) - 1)
                    return mm

                def project(i, b):
                    pe.wait_ge(att_hi, i + 1)
                    pe.wait_ge(att_lo, i + 1)
                    pe.wait_ge(y_done, i)
                    products(psum[:, WO_BANK, :], [lambda j, A=A: A[b][:, j, :] for A in (o_hi, o_lo)],
                             [lambda j, W=W: W[:, j, :] for W in (wo_hi, wo_lo)], NG).then_inc(wo_mm, 1)

                def turn(i):
                    pe.wait_ge(yn_ready, i + 1)
                    pe.wait_ge(yl_done, i)
                    for k in range(KT):
                        mm = pe.transpose(psum[:, T_BANK, k * P:(k + 1) * P], yn[:, k * P:(k + 1) * P], ident[:])
                    mm.then_inc(turned, 1)

                def route(i, b):
                    pe.wait_ge(yh_done, i + 1)
                    pe.wait_ge(yl_done, i + 1)
                    pe.wait_ge(wT_ready, i)
                    products(psum[:, R_BANK, 0:NE], [lambda k, A=A: A[b][:, k, :] for A in (y_hi, y_lo)],
                             [lambda k, W=W: W[:, k, :] for W in (wr_hi, wr_lo)], KT).then_inc(r_mm, 1)

                def turn_w(i, b):
                    pe.wait_ge(w_ready, i + 1)
                    pe.transpose(psum[0:NE, R_BANK, P:2 * P], w[b][:], ident[:]).then_inc(w_turned, 1)

                def biases(i):
                    pe.wait_ge(wT_ready, i + 1)
                    pe.wait_ge(begun, i)
                    pe.matmul(psum[:, B_BANK, :], wT[:], be_sb[:], start=True, stop=True).then_inc(b_mm, 1)

                def expert(i, b, es):
                    for e in es:
                        if e >= ROUND:
                            pe.wait_ge(mixed, i * NE + (e - ROUND + 1))
                        elif e == 0:
                            pe.wait_ge(mixed, i * NE)
                        products(psum[:, e % ROUND, :], [lambda k, A=A: A[b][:, k, :] for A in (y_hi, y_lo)],
                                 [lambda k, W=W: W[:, k, e, :] for W in (we_hi, we_lo)], KT).then_inc(e_mm, 1)

                pe.wait_ge(hi_ready, 1)
                pe.wait_ge(lo_ready, 1)
                project(0, 0)
                turn(0)
                pe.wait_ge(hi_ready, 2)
                pe.wait_ge(lo_ready, 2)
                route(0, 0)
                turn_w(0, 0)
                pe.wait_ge(small_in, 64)
                biases(0)

                def tile(i, b, h, last):
                    if not last:
                        project(i + 1, 1 - b)
                    expert(i, b, (0, 1))
                    if not last:
                        turn(i + 1)
                    expert(i, b, (2, 3))
                    if not last:
                        route(i + 1, 1 - b)
                    expert(i, b, (4, 5, 6))
                    if not last:
                        turn_w(i + 1, 1 - b)
                    expert(i, b, (7,))
                    if not last:
                        biases(i + 1)

                pe.wait_ge(hi_ready, NE + 2)
                pe.wait_ge(lo_ready, NE + 2)
                pairs_of_tiles(pe, tile)


_DRAM = ["x", "ctxT", "Wq", "bq", "Wk", "bk", "Wv", "bv", "Wo", "bo", "WeT", "be", "WrT", "br"]


def kernel(x, ctx_1024, L0_xattn_Wq, L0_xattn_bq, L0_xattn_Wk, L0_xattn_bk, L0_xattn_Wv, L0_xattn_bv,
           L0_xattn_Wo, L0_xattn_bo, L0_ffn_W_experts, L0_ffn_b_experts, L0_ffn_W_router, L0_ffn_b_router):
    import numpy as np
    import concourse.bacc as bacc
    from concourse.bass_utils import run_bass_kernel_spmd

    x, ctx = np.asarray(x)[0], np.asarray(ctx_1024)[0]
    experts_in_out = np.asarray(L0_ffn_W_experts).transpose(2, 0, 1)


    def columns(bias):
        return np.asarray(bias).reshape(-1, P).T

    laid_out = [
        x, ctx.T, L0_xattn_Wq, columns(L0_xattn_bq), L0_xattn_Wk, columns(L0_xattn_bk), L0_xattn_Wv, L0_xattn_bv,
        L0_xattn_Wo, L0_xattn_bo, experts_in_out.reshape(experts_in_out.shape[0], -1), L0_ffn_b_experts,
        np.asarray(L0_ffn_W_router).T, L0_ffn_b_router,
    ]
    nc = bacc.Bacc("TRN2", target_bir_lowering=False, num_devices=1)
    arrays, aps = {}, []
    for name, a in zip(_DRAM, laid_out):
        a = np.ascontiguousarray(a)
        arrays[f"in_{name}"] = a
        aps.append(nc.dram_tensor(f"in_{name}", a.shape, mybir.dt.from_np(a.dtype), kind="ExternalInput").ap())
    out = nc.dram_tensor("out", x.shape, F32, kind="ExternalOutput").ap()
    build_program(nc, *aps, out)
    r = run_bass_kernel_spmd(nc, [arrays], core_ids=[0])
    return r.results[0]["out"][None]
```

```python
from contextlib import ExitStack

import concourse.bass as bass
from concourse import mybir

F32 = mybir.dt.float32
F32R = mybir.dt.float32r
U32 = mybir.dt.uint32
I32 = mybir.dt.int32
ALU = mybir.AluOpType
ACT = mybir.ActivationFunctionType
AX = mybir.AxisListType
ds = bass.ds

P = 128
CH = 512
EPS = 1e-5
HEADS, DH = 16, 32
HG = P // DH
WIDEST = 30.0
SLACK = 1.02
S_RING = 3
P_RING = 6
LAG = 3
SUM_ON_PE = ()
SUM_ON_POOL = (1, 4, 7, 10, 13, 16, 19)
POOL_BEFORE = 23
K_PIECES = 4


def split(n, parts):
    cuts = [round(n * i / parts) for i in range(parts + 1)]
    return [(a, b - a) for a, b in zip(cuts, cuts[1:])]


def build_program(nc, x, ctxT, Wq, bq, Wk, bk, Wv, bv, Wo, bo, WeT, be, WrT, br, out):
    L, D = x.shape
    S = ctxT.shape[1]
    KT = D // P
    NG = HEADS // HG
    NC = L // CH
    NSC = -(-S // CH)
    NT = -(-S // P)
    SP_ = NT * P
    LAST = S - (NT - 1) * P
    NE = br.shape[0]
    SCALE = float(DH) ** -0.5
    TPC = CH // P

    def dram(name, shape, dt):
        return nc.dram_tensor(name, shape, dt, kind="Internal").ap()

    kh_d = dram("kh_scratch", [P, NG, SP_], F32)
    kl_d = dram("kl_scratch", [P, NG, SP_], F32)
    v_d = dram("v_scratch", [P, NT, D], F32)
    qh_d = dram("qh_scratch", [P, NG, L], F32)
    ql_d = dram("ql_scratch", [P, NG, L], F32)
    shift_d = dram("shift_scratch", [HG, NG, L], F32)
    o_d = dram("o_scratch", [D, L], F32)

    ctx = ExitStack()
    with ctx:
        def sb(name, shape, dt, where=None):
            return (where or ctx).enter_context(nc.sbuf_tensor(name, shape, dt))

        def sem(name):
            return ctx.enter_context(nc.semaphore(name))

        psum = ctx.enter_context(nc.psum_tensor("psum", [P, 8, CH], F32))
        ident = sb("ident", [P, P], F32)
        ident_ready = sem("ident_ready")
        unbounded = sb("unbounded", [1, 1], I32)

        projections(nc, ExitStack(), sb, sem, psum, ident, ident_ready, unbounded, locals())
        attention(nc, ExitStack(), sb, sem, psum, unbounded, locals())
        experts(nc, ExitStack(), sb, sem, psum, ident, locals())


def projections(nc, mem, sb0, sem, psum, ident, ident_ready, unbounded, g):
    L, D, S, KT, NG, NC, NSC, NT, LAST, TPC = (g[n] for n in "L D S KT NG NC NSC NT LAST TPC".split())
    x, ctxT, kh_d, kl_d, v_d, qh_d, ql_d, shift_d, SCALE = (g[n] for n in "x ctxT kh_d kl_d v_d qh_d ql_d shift_d SCALE".split())
    last_w = S - (NSC - 1) * CH

    with mem:
        def sb(name, shape, dt):
            return sb0(name, shape, dt, mem)

        w_raw = [sb(f"w_raw_{n}", [P, KT, D], F32) for n in "kvq"]
        w_hi = [sb(f"w_hi_{n}", [P, KT, D], F32R) for n in "kvq"]
        w_lo = [sb(f"w_lo_{n}", [P, KT, D], F32R) for n in "kvq"]
        bk_col = sb("bk_col", [P, NG], F32)
        bq_col = sb("bq_col", [P, NG], F32)
        bv_all = sb("bv_all", [P, D], F32)
        raw = [sb(f"raw{b}", [P, TPC, CH], F32) for b in range(2)]
        a_hi = [sb(f"a_hi{b}", [P, KT, CH], F32R) for b in range(2)]
        a_lo = [sb(f"a_lo{b}", [P, KT, CH], F32R) for b in range(2)]
        o_hi = [sb(f"o_hi{b}", [P, NG, CH], F32R) for b in range(2)]
        o_lo = [sb(f"o_lo{b}", [P, NG, CH], F32R) for b in range(2)]
        v_sb = [sb(f"v_sb{b}", [P, TPC, D], F32) for b in range(2)]
        xn = [sb(f"xn{b}", [P, TPC, D], F32) for b in range(2)]
        stats = sb("stats", [P, TPC, 6], F32)
        mv = sb("mv", [P, TPC, 2], F32)
        var = sb("var", [P, TPC], F32)
        std = sb("std", [P, TPC], F32)
        rstd = sb("rstd", [P, TPC], F32)
        tmp = sb("tmp", [P, TPC], F32)
        squares = sb("squares", [P, NG, CH], F32R)
        of_head = sb("of_head", [P, NG, P], F32R)
        k_norms = sb("k_norms", [P, NSC], F32)
        q_norms = sb("q_norms", [P, NC], F32)
        k_norm = sb("k_norm", [P, 1], F32)
        q_norm = sb("q_norm", [P, 1], F32)
        norms = sb("norms", [P, 1], F32)
        widest = sb("widest", [1, 1], F32)
        bound = sb("bound", [1, 1], F32)
        too_wide = sb("too_wide", [1, 1], F32)
        ones_row = sb("ones_row", [1, CH], F32)
        neg_bound = sb("neg_bound", [1, CH], F32R)

        w_in = [sem(f"w_in_{n}") for n in "kvq"]
        bias_in = sem("bias_in")
        w_hi_ready = sem("w_hi_ready")
        w_lo_ready = sem("w_lo_ready")
        wq_lo_ready = sem("wq_lo_ready")
        c_in = [sem(f"c_in{b}") for b in range(2)]
        x_in = [sem(f"x_in{b}") for b in range(2)]
        c_hi = sem("c_hi")
        c_lo = sem("c_lo")
        k_mm = sem("k_mm")
        v_mm = sem("v_mm")
        k_hi = sem("k_hi")
        k_lo = sem("k_lo")
        v_out = sem("v_out")
        k_stored = [sem(f"k_stored{b}") for b in range(2)]
        v_stored = [sem(f"v_stored{b}") for b in range(2)]
        ln_step = sem("ln_step")
        stats_ready = sem("stats_ready")
        stats_passed = sem("stats_passed")
        var_ready = sem("var_ready")
        std_ready = sem("std_ready")
        xn_ready = sem("xn_ready")
        x_turned = sem("x_turned")
        x_hi = sem("x_hi")
        x_lo = sem("x_lo")
        q_mm = sem("q_mm")
        q_hi = sem("q_hi")
        q_lo = sem("q_lo")
        q_stored = [sem(f"q_stored{b}") for b in range(2)]
        selector = sem("selector")
        k_squared = sem("k_squared")
        q_squared = sem("q_squared")
        k_summed = sem("k_summed")
        q_summed = sem("q_summed")
        k_searched = sem("k_searched")
        q_searched = sem("q_searched")
        fold = sem("fold")
        folded = sem("folded")
        norms_turned = sem("norms_turned")
        widest_ready = sem("widest_ready")
        bound_ready = sem("bound_ready")
        neg_ready = sem("neg_bound_ready")
        shift_stored = sem("shift_stored")

        ctx_v = ctxT.rearrange("(k p) s -> p k s", p=P)
        x_v = x.rearrange("(u p s) d -> p s u d", p=P, s=HEADS)
        per_place = L // HEADS // P
        places = TPC // per_place
        pairs = (NSC - 1) // 2
        assert NSC % 2 == 1 and NC % 2 == 0
        K_SUM_BANK, Q_SUM_BANK = 0, 3
        LN_STEPS = TPC + 5

        with nc.Block() as block:
            @block.sync
            def _(sp):
                def load_ctx(c, b, w):
                    sp.dma_start(raw[b][:, :, 0:w], ctx_v[:, :, ds(c * CH, w)]).then_inc(c_in[b], 16)

                sp.dma_start(w_raw[0][:], g["Wk"].rearrange("(k p) n -> p k n", p=P)).then_inc(w_in[0], 16)
                load_ctx(0, 0, CH)
                sp.dma_start(w_raw[1][:], g["Wv"].rearrange("(k p) n -> p k n", p=P)).then_inc(w_in[1], 16)
                sp.dma_start(bk_col[:], g["bk"]).then_inc(bias_in, 16)
                sp.dma_start(bq_col[:], g["bq"]).then_inc(bias_in, 16)
                sp.dma_start(bv_all[:], g["bv"].rearrange("(o n) -> o n", o=1).to_broadcast([P, D])).then_inc(bias_in, 16)
                load_ctx(1, 1, CH)
                sp.dma_start(w_raw[2][:], g["Wq"].rearrange("(k p) n -> p k n", p=P)).then_inc(w_in[2], 16)

                def store_kv(c, b, w):
                    sp.wait_ge(k_hi, (c + 1) * NG)
                    sp.wait_ge(k_lo, (c + 1) * NG)
                    sp.dma_start(kh_d[:, :, ds(c * CH, w)], o_hi[b][:, :, 0:w].bitcast(F32)).then_inc(k_stored[b], 16)
                    sp.dma_start(kl_d[:, :, ds(c * CH, w)], o_lo[b][:, :, 0:w].bitcast(F32)).then_inc(k_stored[b], 16)
                    if w == CH:
                        sp.wait_ge(v_out, (c + 1) * TPC)
                        sp.dma_start(v_d[:, ds(c * TPC, TPC), :], v_sb[b][:]).then_inc(v_stored[b], 16)
                    else:
                        full = w // P
                        sp.wait_ge(v_out, c * TPC + full + 1)
                        sp.dma_start(v_d[:, ds(c * TPC, full), :], v_sb[b][:, 0:full, :]).then_inc(v_stored[b], 16)
                        sp.dma_start(v_d[0:LAST, ds(c * TPC + full, 1), :], v_sb[b][0:LAST, full:full + 1, :]).then_inc(v_stored[b], 16)

                with sp.Fori(0, pairs - 1) as i:
                    for b in range(2):
                        c = i * 2 + b
                        sp.wait_ge(c_hi, c + 1)
                        sp.wait_ge(c_lo, c + 1)
                        load_ctx(c + 2, b, CH)
                        store_kv(c, b, CH)
                c = 2 * (pairs - 1)
                sp.wait_ge(c_hi, c + 1)
                sp.wait_ge(c_lo, c + 1)
                load_ctx(c + 2, 0, last_w)
                store_kv(c, 0, CH)
                store_kv(c + 1, 1, CH)

                def load_x(c, b):
                    for s in range(places):
                        sp.dma_start(raw[b][:, s * per_place:(s + 1) * per_place, :],
                                     x_v[:, ds(c * places + s, 1), :, :].rearrange("p s u d -> p (s u) d")).then_inc(x_in[b], 16)

                sp.wait_ge(c_hi, NSC)
                sp.wait_ge(c_lo, NSC)
                load_x(0, 0)
                load_x(1, 1)
                store_kv(c + 2, 0, last_w)

                def store_q(c, b):
                    sp.wait_ge(q_hi, (c + 1) * NG)
                    sp.wait_ge(q_lo, (c + 1) * NG)
                    sp.dma_start(qh_d[:, :, ds(c * CH, CH)], o_hi[b][:].bitcast(F32)).then_inc(q_stored[b], 16)
                    sp.dma_start(ql_d[:, :, ds(c * CH, CH)], o_lo[b][:].bitcast(F32)).then_inc(q_stored[b], 16)

                with sp.Fori(0, NC // 2 - 1) as i:
                    for b in range(2):
                        c = i * 2 + b
                        sp.wait_ge(xn_ready, c + 1)
                        load_x(c + 2, b)
                        store_q(c, b)
                for b in range(2):
                    store_q(NC - 2 + b, b)
                sp.wait_ge(neg_ready, 1)
                sp.dma_start(shift_d.rearrange("(o g) j (c n) -> o (g j c) n", o=1, n=CH),
                             neg_bound[:].bitcast(F32).rearrange("o (r n) -> o r n", r=1).to_broadcast([1, HG * NG * NC, CH])).then_inc(shift_stored, 16)
                sp.wait_ge(shift_stored, 16)
                for b in range(2):
                    sp.wait_ge(k_stored[b], 32 * ((NSC + 1 - b) // 2))
                    sp.wait_ge(v_stored[b], 16 * ((NSC + 1 - b) // 2 + (1 - b)))
                    sp.wait_ge(q_stored[b], 32 * (NC // 2))

            @block.gpsimd
            def _(pool):
                pool.memset(ident[:], 0.0).then_inc(ident_ready, 1)
                pool.wait_ge(ident_ready, 1)
                pool.affine_select(out=ident[:], in_=ident[:], compare_op=ALU.not_equal, fill=1.0,
                                   base=0, pattern=[[-1, P]], channel_multiplier=1).then_inc(ident_ready, 1)
                def square(c, b, w, hi, squared, summed):
                    for j in range(NG):
                        pool.wait_ge(hi, c * NG + (j + 1))
                        if j == 0 and summed is not None:
                            pool.wait_ge(*summed)
                        h = o_hi[b][:, j, 0:w].bitcast(F32)
                        pool.tensor_tensor(squares[:, j, 0:w], h, h, ALU.mult).then_inc(squared, 1)

                square(0, 0, CH, k_hi, k_squared, None)
                pool.wait_ge(w_in[2], 16)
                pool.wait_ge(w_hi_ready, 3)
                pool.tensor_tensor(w_lo[2][:], w_raw[2][:], w_hi[2][:].bitcast(F32), ALU.subtract).then_inc(wq_lo_ready, 1)
                with pool.Fori(0, pairs - 1) as i:
                    square(i * 2 + 1, 1, CH, k_hi, k_squared, (k_summed, i * 2 + 1))
                    square(i * 2 + 2, 0, CH, k_hi, k_squared, (k_summed, i * 2 + 2))
                square(NSC - 2, 1, CH, k_hi, k_squared, (k_summed, NSC - 2))
                square(NSC - 1, 0, last_w, k_hi, k_squared, (k_summed, NSC - 1))
                square(0, 0, CH, q_hi, q_squared, (k_summed, NSC))
                with pool.Fori(0, NC // 2 - 1) as i:
                    square(i * 2 + 1, 1, CH, q_hi, q_squared, (q_summed, i * 2 + 1))
                    square(i * 2 + 2, 0, CH, q_hi, q_squared, (q_summed, i * 2 + 2))
                square(NC - 1, 1, CH, q_hi, q_squared, (q_summed, NC - 1))

            @block.scalar
            def _(act):
                act.wait_ge(w_in[0], 16)
                act.activation(w_hi[0][:], w_raw[0][:], ACT.Copy).then_inc(w_hi_ready, 1)

                def ctx_chunk(c, b, i, w):
                    act.wait_ge(c_in[b], 16 * (i + 1))
                    if not (isinstance(c, int) and c == 0):
                        act.wait_ge(v_mm, (c - 1) * TPC)
                    act.activation(a_hi[b][:, :, 0:w], raw[b][:, :, 0:w], ACT.Copy).then_inc(c_hi, 1)

                def k_chunk(c, b, i, w):
                    act.wait_ge(k_stored[b], i * 32)
                    for j in range(NG):
                        act.wait_ge(k_mm, c * NG + (j + 1))
                        act.activation(o_hi[b][:, j, 0:w], psum[:, j, 0:w], ACT.Identity,
                                       bias=bk_col[:, j:j + 1]).then_inc(k_hi, 1)

                ctx_chunk(0, 0, 0, CH)
                act.wait_ge(w_in[1], 16)
                act.activation(w_hi[1][:], w_raw[1][:], ACT.Copy).then_inc(w_hi_ready, 1)
                act.wait_ge(w_in[2], 16)
                act.activation(w_hi[2][:], w_raw[2][:], ACT.Copy).then_inc(w_hi_ready, 1)
                act.wait_ge(bias_in, 48)

                def ctx_pair(i, w_next):
                    k_chunk(i * 2, 0, i, CH)
                    ctx_chunk(i * 2 + 1, 1, i, CH)
                    k_chunk(i * 2 + 1, 1, i, CH)
                    ctx_chunk(i * 2 + 2, 0, i + 1, w_next)

                with act.Fori(0, pairs - 1) as i:
                    ctx_pair(i, CH)
                ctx_pair(pairs - 1, last_w)
                k_chunk(NSC - 1, 0, pairs, last_w)

                def x_stats(c):
                    act.wait_ge(var_ready, c + 1)
                    act.activation(std[:], var[:], ACT.Sqrt).then_inc(std_ready, 1)

                def x_split(c, b):
                    for k in range(KT):
                        act.wait_ge(x_turned, c * KT + (k + 1))
                        act.activation(a_hi[b][:, k, :], psum[:, k, :], ACT.Copy).then_inc(x_hi, 1)

                def q_chunk(c, b, first_stored):
                    act.wait_ge(q_stored[b], first_stored)
                    for j in range(NG):
                        act.wait_ge(q_mm, c * NG + (j + 1))
                        act.activation(o_hi[b][:, j, :], psum[:, 4 + j, :], ACT.Identity,
                                       bias=bq_col[:, j:j + 1]).then_inc(q_hi, 1)

                x_stats(0)
                act.wait_ge(v_mm, (NSC - 1) * TPC + last_w // P + 1)
                for b in range(2):
                    act.wait_ge(k_stored[b], 32 * ((NSC + 1 - b) // 2))
                x_split(0, 0)
                with act.Fori(0, NC // 2 - 1) as i:
                    for b in range(2):
                        c = i * 2 + b
                        x_stats(c + 1)
                        x_split(c + 1, 1 - b)
                        q_chunk(c, b, i * 32)
                c = NC - 2
                x_stats(c + 1)
                x_split(c + 1, 1)
                q_chunk(c, 0, 32 * (NC // 2 - 1))
                q_chunk(c + 1, 1, 32 * (NC // 2 - 1))
                act.wait_ge(widest_ready, 1)
                act.activation(bound[:], widest[:], ACT.Sqrt, scale=SLACK).then_inc(bound_ready, 1)

            @block.vector
            def _(dve):
                def w_low(n):
                    dve.wait_ge(w_hi_ready, n + 1)
                    dve.tensor_tensor(w_lo[n][:], w_raw[n][:], w_hi[n][:].bitcast(F32), ALU.subtract).then_inc(w_lo_ready, 1)

                def ctx_low(c, b, w):
                    dve.wait_ge(c_hi, c + 1)
                    dve.tensor_tensor(a_lo[b][:, :, 0:w], raw[b][:, :, 0:w], a_hi[b][:, :, 0:w].bitcast(F32),
                                      ALU.subtract).then_inc(c_lo, 1)

                def k_low(c, b, w):
                    for j in range(NG):
                        dve.wait_ge(k_hi, c * NG + (j + 1))
                        dve.scalar_tensor_tensor(out=o_lo[b][:, j, 0:w], in0=psum[:, j, 0:w], scalar=bk_col[:, j:j + 1],
                                                 in1=o_hi[b][:, j, 0:w].bitcast(F32), op0=ALU.add, op1=ALU.subtract).then_inc(k_lo, 1)

                def v_chunk(c, b, i, w):
                    dve.wait_ge(v_stored[b], i * 16)
                    for t in range(-(-w // P)):
                        n = min(P, w - t * P)
                        dve.wait_ge(v_mm, c * TPC + (t + 1))
                        dve.tensor_tensor(v_sb[b][0:n, t, :], psum[0:n, 4 + t, :], bv_all[0:n, :], ALU.add).then_inc(v_out, 1)
                        if t == min(1, w // P - 1):
                            search(k_norms, c, K_SUM_BANK, w, k_summed, k_searched)

                def search(norms_of, c, bank, w, summed, searched):
                    dve.wait_ge(summed, c + 1)
                    dve.tensor_reduce(norms_of[:, ds(c, 1)], psum[:, bank, 0:w], AX.X, ALU.max).then_inc(searched, 1)

                w_low(0)
                ctx_low(0, 0, CH)
                dve.memset(of_head[:].bitcast(F32), 0.0).then_inc(selector, 1)
                dve.memset(ones_row[:], 1.0).then_inc(selector, 1)
                dve.wait_ge(selector, 1)
                for j in range(NG):
                    for h in range(HG):
                        dve.memset(of_head[h * DH:(h + 1) * DH, j, HG * j + h:HG * j + h + 1].bitcast(F32), 1.0).then_inc(selector, 1)
                w_low(1)
                dve.wait_ge(bias_in, 48)

                def ctx_pair(i, w_next):
                    k_low(i * 2, 0, CH)
                    ctx_low(i * 2 + 1, 1, CH)
                    v_chunk(i * 2, 0, i, CH)
                    k_low(i * 2 + 1, 1, CH)
                    ctx_low(i * 2 + 2, 0, w_next)
                    v_chunk(i * 2 + 1, 1, i, CH)

                with dve.Fori(0, pairs - 1) as i:
                    ctx_pair(i, CH)
                ctx_pair(pairs - 1, last_w)
                k_low(NSC - 1, 0, last_w)
                v_chunk(NSC - 1, 0, pairs, last_w)

                def ln(c, b, i):
                    base = c * LN_STEPS
                    n = [0]

                    def step(ins, wait=True):
                        n[0] += 1
                        ins.then_inc(ln_step, 1)
                        if wait:
                            dve.wait_ge(ln_step, base + n[0])

                    dve.wait_ge(x_in[b], (16 * places) * (i + 1))
                    for t in range(TPC):
                        ins = dve.bn_stats(stats[:, t, :], raw[b][:, t, :])
                    ins.then_inc(stats_ready, 1)
                    dve.wait_ge(stats_ready, c + 1)
                    dve.sem_inc(stats_passed, 1)
                    for t in range(TPC):
                        step(dve.bn_aggr(mv[:, t, :], stats[:, t, :]), t == TPC - 1)
                    dve.tensor_scalar(var[:], mv[:, :, 1], EPS, None, ALU.add).then_inc(var_ready, 1)
                    dve.wait_ge(std_ready, c + 1)
                    step(dve.reciprocal(rstd[:], std[:]))
                    step(dve.tensor_tensor(tmp[:], rstd[:], rstd[:], ALU.mult))
                    step(dve.tensor_tensor(tmp[:], tmp[:], var[:], ALU.mult))
                    step(dve.tensor_scalar(tmp[:], tmp[:], -0.5, 1.5, ALU.mult, ALU.add))
                    step(dve.tensor_tensor(rstd[:], rstd[:], tmp[:], ALU.mult))
                    assert n[0] == LN_STEPS
                    for t in range(TPC):
                        ins = dve.tensor_scalar(xn[b][:, t, :], raw[b][:, t, :], mv[:, t, 0:1], rstd[:, t:t + 1],
                                                ALU.subtract, ALU.mult)
                    ins.then_inc(xn_ready, 1)

                def x_low(c, b):
                    for k in range(KT):
                        dve.wait_ge(x_hi, c * KT + (k + 1))
                        dve.tensor_tensor(a_lo[b][:, k, :], psum[:, k, :], a_hi[b][:, k, :].bitcast(F32),
                                          ALU.subtract).then_inc(x_lo, 1)

                def q_low(c, b):
                    for j in range(NG):
                        dve.wait_ge(q_hi, c * NG + (j + 1))
                        dve.scalar_tensor_tensor(out=o_lo[b][:, j, :], in0=psum[:, 4 + j, :], scalar=bq_col[:, j:j + 1],
                                                 in1=o_hi[b][:, j, :].bitcast(F32), op0=ALU.add, op1=ALU.subtract).then_inc(q_lo, 1)

                def q_search(c):
                    search(q_norms, c, Q_SUM_BANK, CH, q_summed, q_searched)

                ln(0, 0, 0)
                x_low(0, 0)
                ln(1, 1, 0)
                x_low(1, 1)
                q_low(0, 0)
                with dve.Fori(0, NC // 2 - 1) as i:
                    ln(i * 2 + 2, 0, i + 1)
                    q_search(i * 2)
                    x_low(i * 2 + 2, 0)
                    q_low(i * 2 + 1, 1)
                    ln(i * 2 + 3, 1, i + 1)
                    q_search(i * 2 + 1)
                    x_low(i * 2 + 3, 1)
                    q_low(i * 2 + 2, 0)
                q_search(NC - 2)
                q_low(NC - 1, 1)
                q_search(NC - 1)

                dve.wait_ge(k_searched, NSC)
                dve.wait_ge(q_searched, NC)
                dve.tensor_reduce(k_norm[:], k_norms[:], AX.X, ALU.max).then_inc(fold, 1)
                dve.tensor_reduce(q_norm[:], q_norms[:], AX.X, ALU.max).then_inc(fold, 1)
                dve.wait_ge(fold, 2)
                dve.tensor_tensor(norms[:], k_norm[:], q_norm[:], ALU.mult).then_inc(folded, 1)
                dve.wait_ge(norms_turned, 1)
                dve.tensor_reduce(widest[:], psum[0:1, K_SUM_BANK, 0:P], AX.X, ALU.max).then_inc(widest_ready, 1)
                dve.wait_ge(bound_ready, 1)
                dve.tensor_scalar(neg_bound[:], ones_row[:], bound[:], -1.0, ALU.mult, ALU.mult).then_inc(neg_ready, 1)
                dve.tensor_scalar(too_wide[:], bound[:], WIDEST / SCALE, None, ALU.is_le).then_inc(fold, 1)
                dve.wait_ge(fold, 3)
                dve.tensor_scalar(too_wide[:], too_wide[:], -1.0, 1.0, ALU.mult, ALU.add).then_inc(fold, 1)
                dve.wait_ge(fold, 4)
                dve.tensor_copy(unbounded[:], too_wide[:]).then_inc(fold, 1)
                dve.wait_ge(fold, 5)

            @block.tensor
            def _(pe):
                def products(bank, m, n, lhs, rhs):
                    terms = [(k, a, b) for k in range(KT) for a, b in ((0, 0), (0, 1), (1, 0))]
                    for q, (k, a, b) in enumerate(terms):
                        mm = pe.matmul(psum[0:m, bank, 0:n], lhs[a](k), rhs[b](k), start=q == 0, stop=q == len(terms) - 1)
                    return mm

                def sum_squares(c, bank, w, squared, summed):
                    pe.wait_ge(squared, (c + 1) * NG)
                    for j in range(NG):
                        mm = pe.matmul(psum[:, bank, 0:w], of_head[:, j, :], squares[:, j, 0:w], start=j == 0, stop=j == NG - 1)
                    mm.then_inc(summed, 1)

                def k_products(c, b, w):
                    if not (isinstance(c, int) and c == 0):
                        pe.wait_ge(k_searched, c)
                    pe.wait_ge(c_hi, c + 1)
                    pe.wait_ge(c_lo, c + 1)
                    pe.wait_ge(k_lo, c * NG)
                    for j in range(NG):
                        products(j, P, w, [lambda k, W=W: W[0][:, k, j * P:(j + 1) * P] for W in (w_hi, w_lo)],
                                 [lambda k, A=A: A[b][:, k, 0:w] for A in (a_hi, a_lo)]).then_inc(k_mm, 1)

                def v_products(c, b, w):
                    pe.wait_ge(v_out, c * TPC)
                    for t in range(-(-w // P)):
                        products(4 + t, P, D, [lambda k, A=A: A[b][:, k, t * P:(t + 1) * P] for A in (a_hi, a_lo)],
                                 [lambda k, W=W: W[1][:, k, :] for W in (w_hi, w_lo)]).then_inc(v_mm, 1)
                        if t == min(1, w // P - 1):
                            pe.wait_ge(k_lo, c * NG + 1)
                            sum_squares(c, K_SUM_BANK, w, k_squared, k_summed)

                pe.wait_ge(w_hi_ready, 1)
                pe.wait_ge(w_lo_ready, 1)
                k_products(0, 0, CH)
                pe.wait_ge(w_hi_ready, 2)
                pe.wait_ge(w_lo_ready, 2)
                pe.wait_ge(selector, 2 + HEADS)

                def ctx_pair(i, w_next):
                    v_products(i * 2, 0, CH)
                    k_products(i * 2 + 1, 1, CH)
                    v_products(i * 2 + 1, 1, CH)
                    k_products(i * 2 + 2, 0, w_next)

                with pe.Fori(0, pairs - 1) as i:
                    ctx_pair(i, CH)
                ctx_pair(pairs - 1, last_w)
                v_products(NSC - 1, 0, last_w)

                def turn(c, b):
                    if not (isinstance(c, int) and c < 2):
                        pe.wait_ge(q_searched, c - 1)
                    pe.wait_ge(xn_ready, c + 1)
                    pe.wait_ge(x_lo, c * KT)
                    for k in range(KT):
                        for t in range(TPC):
                            mm = pe.transpose(psum[:, k, t * P:(t + 1) * P], xn[b][:, t, k * P:(k + 1) * P], ident[:])
                        mm.then_inc(x_turned, 1)

                def q_products(c, b, js):
                    pe.wait_ge(x_hi, (c + 1) * KT)
                    pe.wait_ge(x_lo, (c + 1) * KT)
                    pe.wait_ge(q_lo, c * NG)
                    for j in js:
                        products(4 + j, P, CH, [lambda k, W=W: W[2][:, k, j * P:(j + 1) * P] for W in (w_hi, w_lo)],
                                 [lambda k, A=A: A[b][:, k, :] for A in (a_hi, a_lo)]).then_inc(q_mm, 1)

                pe.wait_ge(ident_ready, 2)
                pe.wait_ge(k_lo, NSC * NG)
                pe.wait_ge(k_searched, NSC)
                turn(0, 0)
                pe.wait_ge(v_out, (NSC - 1) * TPC + last_w // P + 1)
                pe.wait_ge(w_hi_ready, 3)
                pe.wait_ge(wq_lo_ready, 1)
                half = NG // 2

                def q_chunk(c, b):
                    q_products(c, b, range(half))
                    if not (isinstance(c, int) and c == 0):
                        sum_squares(c - 1, Q_SUM_BANK, CH, q_squared, q_summed)
                    if not (isinstance(c, int) and c == NC - 1):
                        turn(c + 1, 1 - b)
                    q_products(c, b, range(half, NG))

                q_chunk(0, 0)
                with pe.Fori(0, NC // 2 - 1) as i:
                    q_chunk(i * 2 + 1, 1)
                    q_chunk(i * 2 + 2, 0)
                q_chunk(NC - 1, 1)
                pe.wait_ge(q_searched, NC - 1)
                sum_squares(NC - 1, Q_SUM_BANK, CH, q_squared, q_summed)
                pe.wait_ge(folded, 1)
                pe.transpose(psum[0:1, K_SUM_BANK, 0:P], norms[:], ident[:]).then_inc(norms_turned, 1)


def attention(nc, mem, sb0, sem, psum, unbounded, g):
    S, SP_, NG, NC, NT, LAST, SCALE, D = (g[n] for n in "S SP_ NG NC NT LAST SCALE D".split())
    kh_d, kl_d, v_d, qh_d, ql_d, shift_d, o_d = (g[n] for n in "kh_d kl_d v_d qh_d ql_d shift_d o_d".split())
    NIT = NG * NC
    NP = 2 * NT
    ROWS = 3 * DH
    SH = ROWS
    O_BANK, SUM_BANK = 6, 7
    TPC = CH // P

    with mem:
        def sb(name, shape, dt):
            return sb0(name, shape, dt, mem)

        k_st = sb("k_st", [SH + 1, HG, SP_], F32R)
        q_st = sb("q_st", [SH + 1, 2, HG, CH], F32R)
        v_st = sb("v_st", [P, NT, P], F32)
        ones = sb("ones", [P, DH], F32)
        ones_last = sb("ones_last", [P, DH], F32)
        probs = sb("probs", [P, P_RING + LAG, HG, CH], F32)
        sums = sb("sums", [P, HG, CH], F32)
        pool_sums = sb("pool_sums", [P, HG, CH], F32)
        row_sums = sb("row_sums", [P, CH], F32)
        recip = sb("recip", [P, CH], F32)
        o_sb = sb("o_sb", [P, CH], F32)
        mx = sb("mx", [P, TPC, HG, 2], F32)
        mxx = sb("mxx", [P, HG, TPC], F32)
        neg = sb("neg", [P, HG, TPC], F32R)

        pieces = split(NT, K_PIECES)
        piece_of = {a: n for n, (a, _) in enumerate(pieces)}

        filled = sem("filled")
        row_filled = sem("row_filled")
        ma_k_in = sem("ma_k_in")
        ma_q_in = sem("ma_q_in")
        ma_mm = sem("ma_mm")
        ma_max = sem("ma_max")
        ma_neg = sem("ma_neg")
        ma_fold = sem("ma_fold")
        ma_stored = sem("ma_stored")
        q_in = [sem(f"q_in{b}") for b in range(2)]
        k_in = [sem(f"k_in{n}") for n in range(K_PIECES)]
        v_in = [sem(f"v_in{n}") for n in range(K_PIECES)]
        s_ready = sem("s_ready")
        exp_done = sem("exp_done")
        pv_done = sem("pv_done")
        added = sem("added")
        pool_added = sem("pool_added")
        sums_ready = sem("sums_ready")
        sums_left = sem("sums_left")
        inverted = sem("inverted")
        o_final = sem("o_final")
        o_left = sem("o_left")
        o_stored = sem("o_stored")

        def load_k(sp, j, first, n, count):
            for r, src in enumerate((kh_d, kh_d, kl_d)):
                sp.dma_start(k_st[r * DH:(r + 1) * DH, :, first:first + n].bitcast(F32),
                             src[:, ds(j, 1), first:first + n].rearrange("(h d) o s -> d (h o) s", d=DH)).then_inc(count, 16)

        def load_q(sp, b, it, count):
            for r, src in enumerate((qh_d, ql_d, qh_d)):
                sp.dma_start(q_st[r * DH:(r + 1) * DH, b, :, :].bitcast(F32),
                             src.rearrange("(h d) j l -> d h (j l)", d=DH)[:, :, ds(it * CH, CH)]).then_inc(count, 16)

        s_slot = [n % S_RING for n in range(NP)]
        if NP % S_RING == 1:
            s_slot[-1] = 1
        p_slot = [t % P_RING if t < NT - LAG else P_RING + t - (NT - LAG) for t in range(NT)]

        def before(slots, n):
            found = [(0, m) for m in range(n) if slots[m] == slots[n]] or [(-1, m) for m in range(len(slots)) if slots[m] == slots[n]]
            return found[-1]

        on_pe = set(SUM_ON_PE) | {NT - 1}
        on_pool = list(SUM_ON_POOL)
        on_dve = [t for t in range(NT) if t not in on_pe and t not in on_pool]
        on_dve.insert(on_dve.index(POOL_BEFORE), None)
        adds, pool_adds = len(on_dve) - 1, len(on_pool) - 1
        add_of = {t: max(n, 1) for n, t in enumerate(on_dve)}
        pool_add_of = {t: max(n, 1) for n, t in enumerate(on_pool)}

        with nc.Block() as block:
            @block.gpsimd
            def _(pool):
                pool.memset(k_st[SH:SH + 1, :, 0:S].bitcast(F32), 1.0).then_inc(row_filled, 1)

                with pool.Fori(0, NIT) as it:
                    for k, t in enumerate(on_pool[1:]):
                        pool.wait_ge(exp_done, it * NP + (2 * t + 2))
                        if k == 0:
                            pool.wait_ge(sums_ready, it)
                            a = probs[:, p_slot[on_pool[0]]]
                        else:
                            pool.wait_ge(pool_added, it * pool_adds + k)
                            a = pool_sums[:]
                        pool.tensor_tensor(pool_sums[:], a, probs[:, p_slot[t]], ALU.add).then_inc(pool_added, 1)

            @block.sync
            def _(sp):
                with sp.If(sp.value_load(unbounded[0:1, 0:1], min_val=0, max_val=1) == 1):
                    with sp.Fori(0, NG) as j:
                        sp.wait_ge(ma_mm, j * (NC * TPC * HG * 2))
                        load_k(sp, j, 0, S, ma_k_in)
                        with sp.Fori(0, NC) as c:
                            sp.wait_ge(ma_mm, j * (NC * TPC * HG * 2) + c * (TPC * HG * 2))
                            load_q(sp, 0, j * NC + c, ma_q_in)
                            sp.wait_ge(ma_neg, j * NC + c + 1)
                            for h in range(HG):
                                sp.dma_start(shift_d[h, ds(j, 1), ds(c * CH, CH)].rearrange("o (t p) -> p (o t)", p=P),
                                             neg[:, h, :].bitcast(F32), allow_slow_non_contiguous=True).then_inc(ma_stored, 16)
                    sp.wait_ge(ma_stored, NIT * HG * 16)

                def queries(it, b):
                    load_q(sp, b, it, q_in[b])
                    sp.dma_start(q_st[SH:SH + 1, b, :, :].bitcast(F32),
                                 shift_d.rearrange("(o h) j l -> o h (j l)", o=1)[:, :, ds(it * CH, CH)]).then_inc(q_in[b], 16)

                def keys_values(j, before):
                    for n, (a, m) in enumerate(pieces):
                        if before is not None:
                            sp.wait_ge(s_ready, before * NP + 2 * (a + m))
                        load_k(sp, j, a * P, min((a + m) * P, S) - a * P, k_in[n])
                        if before is not None:
                            sp.wait_ge(pv_done, before * NT + (a + m))
                        full = m - (n == K_PIECES - 1)
                        sp.dma_start(v_st[:, a:a + full, :], v_d[:, a:a + full, ds(j * P, P)]).then_inc(v_in[n], 16)
                        if n == K_PIECES - 1:
                            sp.dma_start(v_st[0:LAST, NT - 1, :], v_d[0:LAST, NT - 1, ds(j * P, P)]).then_inc(v_in[n], 16)

                def result(j, c, it):
                    sp.wait_ge(o_final, it + 1)
                    sp.dma_start(o_d[ds(j * P, P), ds(c * CH, CH)], o_sb[:]).then_inc(o_stored, 16)

                def step(j, c, b, reload, more=True):
                    it = j * NC + c
                    if more:
                        sp.wait_ge(s_ready, it * NP)
                        queries(it + 1, 1 - b)
                    if reload:
                        keys_values(j + 1, it)
                    result(j, c, it)

                queries(0, 0)
                sp.wait_ge(filled, 5)
                keys_values(0, None)

                def group(j, last):
                    with sp.Fori(0, NC // 2 - 1) as i:
                        for b in range(2):
                            step(j, i * 2 + b, b, False)
                    step(j, NC - 2, 0, False)
                    step(j, NC - 1, 1, not last, not last)

                with sp.Fori(0, NG - 1) as j:
                    group(j, False)
                group(NG - 1, True)
                sp.wait_ge(o_stored, NIT * 16)

            @block.scalar
            def _(act):
                act.preload_act_table(ACT.Exp)

                def step(it):
                    first = isinstance(it, int)
                    for n in range(NP):
                        t, half = divmod(n, 2)
                        act.wait_ge(s_ready, it * NP + (n + 1))
                        if half == 0:
                            ago, u = before(p_slot, t)
                            if not (first and ago):
                                act.wait_ge(pv_done, (it + ago) * NT + (u + 1))
                                if u in add_of:
                                    act.wait_ge(added, (it + ago) * adds + add_of[u])
                                if u in pool_add_of:
                                    act.wait_ge(pool_added, (it + ago) * pool_adds + pool_add_of[u])
                        nc.scalar.activation(probs[:, p_slot[t], 2 * half:2 * half + 2, :],
                                             psum[:, 2 * s_slot[n]:2 * s_slot[n] + 2, :], ACT.Exp, scale=SCALE).then_inc(exp_done, 1)

                step(0)
                with act.Fori(1, NIT) as it:
                    step(it)

            @block.vector
            def _(dve):
                dve.memset(k_st[:, :, S:SP_].bitcast(F32), 0.0).then_inc(filled, 1)
                dve.memset(v_st[:, NT - 1, :], 0.0).then_inc(filled, 1)
                dve.memset(ones[:], 1.0).then_inc(filled, 1)
                dve.memset(ones_last[:], 0.0).then_inc(filled, 1)
                dve.wait_ge(filled, 4)
                dve.memset(ones_last[0:LAST, :], 1.0).then_inc(filled, 1)

                with dve.If(dve.value_load(unbounded[0:1, 0:1], min_val=0, max_val=1) == 1):
                    with dve.Fori(0, NIT) as it:
                        k = 0
                        for t in range(TPC):
                            for h in range(HG):
                                for half in range(2):
                                    k += 1
                                    dve.wait_ge(ma_mm, it * (TPC * HG * 2) + k)
                                    w = 4 * CH if half == 0 else S - 4 * CH
                                    dve.tensor_reduce(mx[:, t, h, half:half + 1],
                                                      psum[:, 4 * half:8, :].rearrange("p b n -> p (b n)")[:, 0:w], AX.X, ALU.max).then_inc(ma_max, 1)
                        dve.wait_ge(ma_max, (it + 1) * (TPC * HG * 2))
                        dve.tensor_tensor(mxx[:], mx[:, :, :, 0].rearrange("p t h -> p h t"), mx[:, :, :, 1].rearrange("p t h -> p h t"),
                                          ALU.max).then_inc(ma_fold, 1)
                        dve.wait_ge(ma_fold, it + 1)
                        dve.wait_ge(ma_stored, it * (HG * 16))
                        dve.tensor_scalar(neg[:], mxx[:], -1.0, None, ALU.mult).then_inc(ma_neg, 1)

                with dve.Fori(0, NIT) as it:
                    for k, t in enumerate(on_dve[1:]):
                        if t is None:
                            dve.wait_ge(pool_added, (it + 1) * pool_adds)
                            term = pool_sums[:]
                        else:
                            dve.wait_ge(exp_done, it * NP + (2 * t + 2))
                            term = probs[:, p_slot[t]]
                        if k == 0:
                            dve.wait_ge(sums_ready, it)
                            a = probs[:, p_slot[on_dve[0]]]
                        else:
                            dve.wait_ge(added, it * adds + k)
                            a = sums[:]
                        nc.vector.tensor_tensor(sums[:], a, term, ALU.add).then_inc(added, 1)
                    dve.wait_ge(sums_ready, it + 1)
                    nc.vector.tensor_copy(row_sums[:], psum[:, SUM_BANK, :]).then_inc(sums_left, 1)
                    dve.wait_ge(pv_done, (it + 1) * NT)
                    dve.wait_ge(o_stored, it * 16)
                    nc.vector.tensor_copy(o_sb[:], psum[:, O_BANK, :]).then_inc(o_left, 1)
                    dve.wait_ge(sums_left, it + 1)
                    nc.vector.reciprocal(recip[:], row_sums[:]).then_inc(inverted, 1)
                    dve.wait_ge(o_left, it + 1)
                    dve.wait_ge(inverted, it + 1)
                    nc.vector.tensor_tensor(o_sb[:], o_sb[:], recip[:], ALU.mult).then_inc(o_final, 1)

            @block.tensor
            def _(pe):
                with pe.If(pe.value_load(unbounded[0:1, 0:1], min_val=0, max_val=1) == 1):
                    with pe.Fori(0, NG) as j:
                        with pe.Fori(0, NC) as c:
                            it = j * NC + c
                            pe.wait_ge(ma_k_in, (j + 1) * 48)
                            pe.wait_ge(ma_q_in, (it + 1) * 48)
                            k = 0
                            for t in range(TPC):
                                for h in range(HG):
                                    for half in range(2):
                                        if k >= 2:
                                            pe.wait_ge(ma_max, it * (TPC * HG * 2) + (k - 1))
                                        elif k == 0:
                                            pe.wait_ge(ma_max, it * (TPC * HG * 2))
                                        k += 1
                                        for b in range(4 * half, min(4 * half + 4, -(-S // CH))):
                                            w = min(CH, S - b * CH)
                                            mm = pe.matmul(psum[:, b, 0:w], q_st[0:ROWS, 0, h, t * P:(t + 1) * P],
                                                           k_st[0:ROWS, h, b * CH:b * CH + w], start=True, stop=True)
                                        mm.then_inc(ma_mm, 1)

                def scores(it, b, i_of, t, first=False):
                    if t == 0:
                        pe.wait_ge(q_in[b], (i_of + 1) * 64)
                    if t in piece_of:
                        pe.wait_ge(k_in[piece_of[t]], (i_of // (NC // 2) + 1) * 48)
                    for half in range(2):
                        n = 2 * t + half
                        ago, m = before(s_slot, n)
                        if not (first and ago):
                            pe.wait_ge(exp_done, (it + ago) * NP + (m + 1))
                        for h in (2 * half, 2 * half + 1):
                            mm = nc.tensor.matmul(psum[:, 2 * s_slot[n] + h % 2, :], k_st[:, h, t * P:(t + 1) * P],
                                                  q_st[:, b, h, :], start=True, stop=True)
                        mm.then_inc(s_ready, 1)

                def over_keys(bank, lhs, rhs, start, stop):
                    for h in range(HG):
                        mm = nc.tensor.matmul(psum[h * DH:(h + 1) * DH, bank, :], lhs(h), rhs(h), start=start, stop=stop)
                    return mm

                def weigh(it, i, t):
                    if t in piece_of:
                        n = piece_of[t]
                        pe.wait_ge(v_in[n], (i // (NC // 2) + 1) * (16 * (1 + (n == K_PIECES - 1))))
                    pe.wait_ge(exp_done, it * NP + (2 * t + 2))
                    if t == 0:
                        pe.wait_ge(o_left, it)
                    p = p_slot[t]

                    def values():
                        return over_keys(O_BANK, lambda h: v_st[:, t, h * DH:(h + 1) * DH], lambda h: probs[:, p, h, :], t == 0, t == NT - 1)

                    def sum_tile():
                        o = ones_last if t == NT - 1 else ones
                        return over_keys(SUM_BANK, lambda h: o[:], lambda h: probs[:, p, h, :], t == min(on_pe), False)

                    if t < NT - 1:
                        mm = values()
                        if t in on_pe:
                            mm = sum_tile()
                        mm.then_inc(pv_done, 1)
                    else:
                        sum_tile()
                        pe.wait_ge(added, (it + 1) * adds)
                        over_keys(SUM_BANK, lambda h: ones[:], lambda h: sums[:, h, :], False, True).then_inc(sums_ready, 1)
                        values().then_inc(pv_done, 1)

                pe.wait_ge(filled, 5)
                pe.wait_ge(row_filled, 1)

                def step(it, b, i, i_next):
                    for t in range(NT):
                        if t + LAG < NT:
                            scores(it, b, i, t + LAG, isinstance(it, int) and it == 0)
                        elif i_next is not None:
                            scores(it + 1, 1 - b, i_next, t + LAG - NT)
                        weigh(it, i, t)

                for t in range(LAG):
                    scores(0, 0, 0, t, True)
                with pe.Fori(0, NIT // 2 - 1) as i:
                    step(i * 2, 0, i, i)
                    step(i * 2 + 1, 1, i, i + 1)
                i = NIT // 2 - 1
                step(NIT - 2, 0, i, i)
                step(NIT - 1, 1, i, None)


def experts(nc, mem, sb0, sem, psum, ident, g):
    L, D, KT, NG, NE = (g[n] for n in "L D KT NG NE".split())
    x, o_d, out, Wo, WeT, WrT = (g[n] for n in "x o_d out Wo WeT WrT".split())
    NTL = L // P
    assert NTL == 2 * HEADS
    ROUND = 4
    WO_BANK, T_BANK, R_BANK, B_BANK = 4, 5, 6, 7

    with mem:
        def sb(name, shape, dt):
            return sb0(name, shape, dt, mem)

        we_hi = sb("we_hi", [P, KT, NE, D], F32R)
        we_lo = sb("we_lo", [P, KT, NE, D], F32R)
        w_raw = [sb(f"we_raw{b}", [P, KT, D], F32) for b in range(2)]
        wo_hi = sb("wo_hi", [P, NG, D], F32R)
        wo_lo = sb("wo_lo", [P, NG, D], F32R)
        wr_raw = sb("wr_raw", [P, KT, NE], F32)
        wr_hi = sb("wr_hi", [P, KT, NE], F32R)
        wr_lo = sb("wr_lo", [P, KT, NE], F32R)
        bo_all = sb("bo_all", [P, D], F32)
        br_all = sb("br_all", [P, NE], F32)
        be_sb = sb("be_sb", [NE, D], F32)
        number = sb("number", [P, NE], F32)

        def two(name, shape, dt):
            return [sb(f"{name}{b}", shape, dt) for b in range(2)]

        o_raw = two("o_raw", [P, NG, P], F32)
        x_raw = two("x_raw", [P, D], F32)
        xb = two("xb", [P, D], F32)
        o_hi = two("att_hi", [P, NG, P], F32R)
        o_lo = two("att_lo", [P, NG, P], F32R)
        y = two("y", [P, D], F32)
        yn = sb("yn", [P, D], F32)
        y_hi = two("y_hi", [P, KT, P], F32R)
        y_lo = two("y_lo", [P, KT, P], F32R)
        acc = two("acc", [P, D], F32)
        w = two("w", [P, NE], F32)
        wT = sb("wT", [NE, P], F32)
        stats = sb("stats3", [P, 6], F32)
        mv = sb("mv3", [P, 2], F32)
        var = sb("var3", [P, 1], F32)
        std = sb("std3", [P, 1], F32)
        rstd = sb("rstd3", [P, 1], F32)
        tmp = sb("tmp3", [P, 1], F32)
        logits = sb("logits", [P, NE], F32)
        top = sb("top", [P, 8], F32)
        top_at = sb("top_at", [P, 8], U32)
        top_at_f = sb("top_at_f", [P, 2], F32)
        neg_top = sb("neg_top", [P, 1], F32)
        ex = sb("ex", [P, NE], F32)
        total = sb("total", [P, 1], F32)
        inv = sb("inv", [P, 1], F32)
        chosen1 = sb("chosen1", [P, NE], F32)
        chosen = sb("chosen", [P, NE], F32)

        small_in = sem("small_in")
        wo_in = sem("wo_in")
        we_in = [sem(f"we_in{b}") for b in range(2)]
        hi_ready = sem("hi_ready")
        lo_ready = sem("lo_ready")
        numbered = sem("numbered")
        t_in = [sem(f"t_in{b}") for b in range(2)]
        att_hi = sem("att_hi_done")
        att_lo = sem("att_lo_done")
        xb_done = sem("xb_done")
        wo_mm = sem("wo_mm")
        chain = sem("chain")
        stats_ready = sem("stats_ready3")
        y_done = sem("y_done")
        var_ready = sem("var_ready3")
        std_ready = sem("std_ready3")
        yn_ready = sem("yn_ready")
        turned = sem("turned")
        yh_done = sem("yh_done")
        yl_done = sem("yl_done")
        r_mm = sem("r_mm")
        logits_ready = sem("logits_ready")
        neg_ready = sem("neg_ready")
        ex_ready = sem("ex_ready")
        w_ready = sem("w_ready")
        w_turned = sem("w_turned")
        wT_ready = sem("wT_ready")
        b_mm = sem("b_mm")
        begun = sem("begun")
        e_mm = sem("e_mm")
        mixed = sem("mixed")
        stored = [sem(f"stored{b}") for b in range(2)]

        CHAIN = 12

        def pairs_of_tiles(eng, body):
            with eng.Fori(0, NTL // 2 - 1) as h:
                for b in range(2):
                    body(h * 2 + b, b, h, False)
            for b in range(2):
                body(NTL - 2 + b, b, NTL // 2 - 1, b == 1)

        with nc.Block() as block:
            @block.sync
            def _(sp):
                def load_tile(i, b, head):
                    o_v = o_d.rearrange("n (k a u r) -> n a k u r", a=HG, u=2, r=P)
                    for a in range(HG):
                        sp.dma_start(o_raw[b][a * DH:(a + 1) * DH, :, :],
                                     o_v[ds(head * DH, DH), a, :, b, :]).then_inc(t_in[b], 16)
                    sp.dma_start(x_raw[b][:], x[ds(i * P, P), :]).then_inc(t_in[b], 16)

                load_tile(0, 0, 0)
                sp.dma_start(w_raw[0][:], Wo.rearrange("(j p) n -> p j n", p=P)).then_inc(wo_in, 16)
                sp.dma_start(wr_raw[:], WrT.rearrange("(k p) e -> p k e", p=P)).then_inc(small_in, 16)
                sp.dma_start(bo_all[:], g["bo"].rearrange("(o n) -> o n", o=1).to_broadcast([P, D])).then_inc(small_in, 16)
                sp.dma_start(br_all[:], g["br"].rearrange("(o n) -> o n", o=1).to_broadcast([P, NE])).then_inc(small_in, 16)
                sp.dma_start(be_sb[:], g["be"]).then_inc(small_in, 16)
                load_tile(1, 1, 0)
                for e in range(NE):
                    b = (e + 1) % 2
                    if e > 0:
                        sp.wait_ge(hi_ready, e + 1)
                        sp.wait_ge(lo_ready, e + 1)
                    sp.dma_start(w_raw[b][:], WeT[:, e * D:(e + 1) * D].rearrange("(k p) n -> p k n", p=P)).then_inc(we_in[b], 16)

                def tile(i, b, h, last):
                    if not (isinstance(h, int)):
                        sp.wait_ge(att_lo, i + 1)
                        sp.wait_ge(xb_done, i + 1)
                        load_tile(i + 2, b, h + 1)
                    sp.wait_ge(mixed, (i + 1) * NE)
                    sp.dma_start(out[ds(i * P, P), :], acc[b][:]).then_inc(stored[b], 16)

                pairs_of_tiles(sp, tile)
                for b in range(2):
                    sp.wait_ge(stored[b], 16 * (NTL // 2))

            @block.gpsimd
            def _(pool):
                pool.iota(number[:], [[1, NE]], base=0, channel_multiplier=0, allow_small_or_imprecise_dtypes=True).then_inc(numbered, 1)
                pool.wait_ge(small_in, 64)

                def inputs(i, b, h):
                    pool.wait_ge(t_in[b], (h + 1) * (16 * (HG + 1)))
                    if not (isinstance(i, int) and i < 2):
                        pool.wait_ge(y_done, i - 1)
                        pool.wait_ge(wo_mm, i - 1)
                    pool.tensor_tensor(xb[b][:], x_raw[b][:], bo_all[:], ALU.add).then_inc(xb_done, 1)
                    pool.wait_ge(att_hi, i + 1)
                    pool.tensor_tensor(o_lo[b][:], o_raw[b][:], o_hi[b][:].bitcast(F32), ALU.subtract).then_inc(att_lo, 1)

                inputs(0, 0, 0)
                inputs(1, 1, 0)
                with pool.Fori(1, NTL // 2) as h:
                    for b in range(2):
                        inputs(h * 2 + b, b, h)

            @block.scalar
            def _(act):
                def att_split(i, b, h):
                    act.wait_ge(t_in[b], (h + 1) * (16 * (HG + 1)))
                    if not (isinstance(i, int) and i < 2):
                        act.wait_ge(wo_mm, i - 1)
                    act.activation(o_hi[b][:], o_raw[b][:], ACT.Copy).then_inc(att_hi, 1)

                def root(i):
                    act.wait_ge(var_ready, i + 1)
                    act.activation(std[:], var[:], ACT.Sqrt).then_inc(std_ready, 1)

                def y_split(i, b):
                    act.wait_ge(turned, i + 1)
                    act.activation(y_hi[b][:], psum[:, T_BANK, :].rearrange("p (k n) -> p k n", k=KT), ACT.Copy).then_inc(yh_done, 1)

                def exps(i):
                    act.wait_ge(neg_ready, i + 1)
                    act.activation(ex[:], logits[:], ACT.Exp, bias=neg_top[:], accum_out=total[:]).then_inc(ex_ready, 1)

                att_split(0, 0, 0)
                act.wait_ge(wo_in, 16)
                act.activation(wo_hi[:], w_raw[0][:], ACT.Copy).then_inc(hi_ready, 1)
                act.wait_ge(small_in, 64)
                act.activation(wr_hi[:], wr_raw[:], ACT.Copy).then_inc(hi_ready, 1)
                att_split(1, 1, 0)
                root(0)
                y_split(0, 0)
                exps(0)
                for e in range(NE):
                    b = (e + 1) % 2
                    act.wait_ge(we_in[b], 16 * (e // 2 + 1))
                    act.activation(we_hi[:, :, e, :], w_raw[b][:], ACT.Copy).then_inc(hi_ready, 1)

                def tile(i, b, h, last):
                    if last:
                        return
                    root(i + 1)
                    y_split(i + 1, 1 - b)
                    exps(i + 1)
                    if not isinstance(h, int):
                        att_split(i + 2, b, h + 1)

                pairs_of_tiles(act, tile)

            @block.vector
            def _(dve):
                def before_turn(i, b, n):
                    def step(ins):
                        n[0] += 1
                        ins.then_inc(chain, 1)
                        dve.wait_ge(chain, i * CHAIN + n[0])

                    dve.wait_ge(wo_mm, i + 1)
                    dve.wait_ge(xb_done, i + 1)
                    dve.tensor_tensor(y[b][:], psum[:, WO_BANK, :], xb[b][:], ALU.add).then_inc(y_done, 1)
                    dve.wait_ge(y_done, i + 1)
                    dve.bn_stats(stats[:], y[b][:]).then_inc(stats_ready, 1)
                    dve.wait_ge(numbered, 1)
                    dve.wait_ge(stats_ready, i + 1)
                    step(dve.bn_aggr(mv[:], stats[:]))
                    dve.tensor_scalar(var[:], mv[:, 1:2], EPS, None, ALU.add).then_inc(var_ready, 1)
                    dve.wait_ge(std_ready, i + 1)
                    step(dve.reciprocal(rstd[:], std[:]))
                    step(dve.tensor_tensor(tmp[:], rstd[:], rstd[:], ALU.mult))
                    step(dve.tensor_tensor(tmp[:], tmp[:], var[:], ALU.mult))
                    step(dve.tensor_scalar(tmp[:], tmp[:], -0.5, 1.5, ALU.mult, ALU.add))
                    step(dve.tensor_tensor(rstd[:], rstd[:], tmp[:], ALU.mult))
                    dve.tensor_scalar(yn[:], y[b][:], mv[:, 0:1], rstd[:], ALU.subtract, ALU.mult).then_inc(yn_ready, 1)

                def after_turn(i, b):
                    dve.wait_ge(yh_done, i + 1)
                    dve.tensor_tensor(y_lo[b][:], psum[:, T_BANK, :].rearrange("p (k n) -> p k n", k=KT),
                                      y_hi[b][:].bitcast(F32), ALU.subtract).then_inc(yl_done, 1)

                def route(i, b, n):
                    def step(ins):
                        n[0] += 1
                        ins.then_inc(chain, 1)
                        dve.wait_ge(chain, i * CHAIN + n[0])

                    dve.wait_ge(r_mm, i + 1)
                    dve.tensor_tensor(logits[:], psum[:, R_BANK, 0:NE], br_all[:], ALU.add).then_inc(logits_ready, 1)
                    dve.wait_ge(numbered, 1)
                    dve.wait_ge(logits_ready, i + 1)
                    step(dve.max(top[:], logits[:]))
                    dve.tensor_scalar(neg_top[:], top[:, 0:1], -1.0, None, ALU.mult).then_inc(neg_ready, 1)
                    step(dve.max_index(top_at[:], top[:], logits[:]))
                    step(dve.tensor_copy(top_at_f[:], top_at[:, 0:2]))
                    step(dve.tensor_scalar(chosen1[:], number[:], top_at_f[:, 0:1], None, ALU.is_equal))
                    dve.scalar_tensor_tensor(out=chosen[:], in0=number[:], scalar=top_at_f[:, 1:2], in1=chosen1[:],
                                             op0=ALU.is_equal, op1=ALU.add).then_inc(chain, 1)
                    n[0] += 1
                    dve.wait_ge(ex_ready, i + 1)
                    dve.reciprocal(inv[:], total[:]).then_inc(chain, 1)
                    n[0] += 1
                    assert n[0] == CHAIN
                    dve.wait_ge(chain, i * CHAIN + n[0])
                    dve.scalar_tensor_tensor(out=w[b][:], in0=ex[:], scalar=inv[:], in1=chosen[:],
                                             op0=ALU.mult, op1=ALU.mult).then_inc(w_ready, 1)

                def copy_wT(i):
                    dve.wait_ge(w_turned, i + 1)
                    dve.tensor_copy(wT[:], psum[0:NE, R_BANK, P:2 * P]).then_inc(wT_ready, 1)

                def begin(i, b, h):
                    dve.wait_ge(b_mm, i + 1)
                    dve.wait_ge(stored[b], h * 16)
                    dve.tensor_tensor(acc[b][:], psum[:, B_BANK, :], y[b][:], ALU.add).then_inc(begun, 1)

                def mix(i, b, es):
                    for e in es:
                        if e == 0:
                            dve.wait_ge(begun, i + 1)
                        else:
                            dve.wait_ge(mixed, i * NE + e)
                        dve.wait_ge(e_mm, i * NE + (e + 1))
                        dve.scalar_tensor_tensor(out=acc[b][:], in0=psum[:, e % ROUND, :], scalar=w[b][:, e:e + 1],
                                                 in1=acc[b][:], op0=ALU.mult, op1=ALU.add).then_inc(mixed, 1)

                dve.wait_ge(hi_ready, 1)
                dve.tensor_tensor(wo_lo[:], w_raw[0][:], wo_hi[:].bitcast(F32), ALU.subtract).then_inc(lo_ready, 1)
                dve.wait_ge(hi_ready, 2)
                dve.tensor_tensor(wr_lo[:], wr_raw[:], wr_hi[:].bitcast(F32), ALU.subtract).then_inc(lo_ready, 1)
                dve.wait_ge(small_in, 64)
                dve.wait_ge(numbered, 1)
                n = [0]
                before_turn(0, 0, n)
                after_turn(0, 0)
                route(0, 0, n)
                copy_wT(0)
                begin(0, 0, 0)
                for e in range(NE):
                    b = (e + 1) % 2
                    dve.wait_ge(hi_ready, e + 3)
                    dve.tensor_tensor(we_lo[:, :, e, :], w_raw[b][:], we_hi[:, :, e, :].bitcast(F32), ALU.subtract).then_inc(lo_ready, 1)

                def tile(i, b, h, last):
                    n = [0]
                    if not last:
                        before_turn(i + 1, 1 - b, n)
                    mix(i, b, (0, 1))
                    if not last:
                        after_turn(i + 1, 1 - b)
                    mix(i, b, (2, 3))
                    if not last:
                        route(i + 1, 1 - b, n)
                    mix(i, b, (4, 5, 6))
                    if not last:
                        copy_wT(i + 1)
                    mix(i, b, (7,))
                    if not last:
                        begin(i + 1, 1 - b, h + b)

                pairs_of_tiles(dve, tile)

            @block.tensor
            def _(pe):
                def products(out_ap, lhs, rhs, parts):
                    terms = [(k, a, b) for k in range(parts) for a, b in ((0, 0), (0, 1), (1, 0))]
                    for q, (k, a, b) in enumerate(terms):
                        mm = pe.matmul(out_ap, lhs[a](k), rhs[b](k), start=q == 0, stop=q == len(terms) - 1)
                    return mm

                def project(i, b):
                    pe.wait_ge(att_hi, i + 1)
                    pe.wait_ge(att_lo, i + 1)
                    pe.wait_ge(y_done, i)
                    products(psum[:, WO_BANK, :], [lambda j, A=A: A[b][:, j, :] for A in (o_hi, o_lo)],
                             [lambda j, W=W: W[:, j, :] for W in (wo_hi, wo_lo)], NG).then_inc(wo_mm, 1)

                def turn(i):
                    pe.wait_ge(yn_ready, i + 1)
                    pe.wait_ge(yl_done, i)
                    for k in range(KT):
                        mm = pe.transpose(psum[:, T_BANK, k * P:(k + 1) * P], yn[:, k * P:(k + 1) * P], ident[:])
                    mm.then_inc(turned, 1)

                def route(i, b):
                    pe.wait_ge(yh_done, i + 1)
                    pe.wait_ge(yl_done, i + 1)
                    pe.wait_ge(wT_ready, i)
                    products(psum[:, R_BANK, 0:NE], [lambda k, A=A: A[b][:, k, :] for A in (y_hi, y_lo)],
                             [lambda k, W=W: W[:, k, :] for W in (wr_hi, wr_lo)], KT).then_inc(r_mm, 1)

                def turn_w(i, b):
                    pe.wait_ge(w_ready, i + 1)
                    pe.transpose(psum[0:NE, R_BANK, P:2 * P], w[b][:], ident[:]).then_inc(w_turned, 1)

                def biases(i):
                    pe.wait_ge(wT_ready, i + 1)
                    pe.wait_ge(begun, i)
                    pe.matmul(psum[:, B_BANK, :], wT[:], be_sb[:], start=True, stop=True).then_inc(b_mm, 1)

                def expert(i, b, es):
                    for e in es:
                        if e >= ROUND:
                            pe.wait_ge(mixed, i * NE + (e - ROUND + 1))
                        elif e == 0:
                            pe.wait_ge(mixed, i * NE)
                        products(psum[:, e % ROUND, :], [lambda k, A=A: A[b][:, k, :] for A in (y_hi, y_lo)],
                                 [lambda k, W=W: W[:, k, e, :] for W in (we_hi, we_lo)], KT).then_inc(e_mm, 1)

                pe.wait_ge(hi_ready, 1)
                pe.wait_ge(lo_ready, 1)
                project(0, 0)
                turn(0)
                pe.wait_ge(hi_ready, 2)
                pe.wait_ge(lo_ready, 2)
                route(0, 0)
                turn_w(0, 0)
                pe.wait_ge(small_in, 64)
                biases(0)

                def tile(i, b, h, last):
                    if not last:
                        project(i + 1, 1 - b)
                    expert(i, b, (0, 1))
                    if not last:
                        turn(i + 1)
                    expert(i, b, (2, 3))
                    if not last:
                        route(i + 1, 1 - b)
                    expert(i, b, (4, 5, 6))
                    if not last:
                        turn_w(i + 1, 1 - b)
                    expert(i, b, (7,))
                    if not last:
                        biases(i + 1)

                pe.wait_ge(hi_ready, NE + 2)
                pe.wait_ge(lo_ready, NE + 2)
                pairs_of_tiles(pe, tile)


_DRAM = ["x", "ctxT", "Wq", "bq", "Wk", "bk", "Wv", "bv", "Wo", "bo", "WeT", "be", "WrT", "br"]


def kernel(x, ctx_1024, L0_xattn_Wq, L0_xattn_bq, L0_xattn_Wk, L0_xattn_bk, L0_xattn_Wv, L0_xattn_bv,
           L0_xattn_Wo, L0_xattn_bo, L0_ffn_W_experts, L0_ffn_b_experts, L0_ffn_W_router, L0_ffn_b_router):
    import numpy as np
    import concourse.bacc as bacc
    from concourse.bass_utils import run_bass_kernel_spmd

    x, ctx = np.asarray(x)[0], np.asarray(ctx_1024)[0]
    experts_in_out = np.asarray(L0_ffn_W_experts).transpose(2, 0, 1)


    def columns(bias):
        return np.asarray(bias).reshape(-1, P).T

    laid_out = [
        x, ctx.T, L0_xattn_Wq, columns(L0_xattn_bq), L0_xattn_Wk, columns(L0_xattn_bk), L0_xattn_Wv, L0_xattn_bv,
        L0_xattn_Wo, L0_xattn_bo, experts_in_out.reshape(experts_in_out.shape[0], -1), L0_ffn_b_experts,
        np.asarray(L0_ffn_W_router).T, L0_ffn_b_router,
    ]
    nc = bacc.Bacc("TRN2", target_bir_lowering=False, num_devices=1)
    arrays, aps = {}, []
    for name, a in zip(_DRAM, laid_out):
        a = np.ascontiguousarray(a)
        arrays[f"in_{name}"] = a
        aps.append(nc.dram_tensor(f"in_{name}", a.shape, mybir.dt.from_np(a.dtype), kind="ExternalInput").ap())
    out = nc.dram_tensor("out", x.shape, F32, kind="ExternalOutput").ap()
    build_program(nc, *aps, out)
    r = run_bass_kernel_spmd(nc, [arrays], core_ids=[0])
    return r.results[0]["out"][None]
```

```python
from contextlib import ExitStack

import concourse.bass as bass
from concourse import mybir

F32 = mybir.dt.float32
F32R = mybir.dt.float32r
U32 = mybir.dt.uint32
I32 = mybir.dt.int32
ALU = mybir.AluOpType
ACT = mybir.ActivationFunctionType
AX = mybir.AxisListType
ds = bass.ds

P = 128
CH = 512
EPS = 1e-5
HEADS, DH = 16, 32
HG = P // DH
BIAS_STEP = 32
WIDEST = 30.0
SLACK = 1.02
S_RING = 3
P_RING = 6
LAG = 3
SUM_ON_POOL = (1, 4, 7, 10, 13, 16, 19, 22)
SUMS_AT = 1
DIVIDE_AT = 1
PIECE_ENDS = (1, 8, 17)


def build_program(nc, x, ctxT, Wq, bq, Wk, bk, Wv, bv, Wo, bo, WeT, be, WrT, br, out):
    L, D = x.shape
    S = ctxT.shape[1]
    KT = D // P
    NG = HEADS // HG
    NC = L // CH
    NSC = -(-S // CH)
    NT = -(-S // P)
    SP_ = NT * P
    LAST = S - (NT - 1) * P
    NE = br.shape[0]
    SCALE = float(DH) ** -0.5
    TPC = CH // P

    def dram(name, shape, dt):
        return nc.dram_tensor(name, shape, dt, kind="Internal").ap()

    kh_d = dram("kh_scratch", [P, NG, SP_], F32)
    kl_d = dram("kl_scratch", [P, NG, SP_], F32)
    v_d = dram("v_scratch", [P, NT, D], F32)
    qh_d = dram("qh_scratch", [P, NG, L], F32)
    ql_d = dram("ql_scratch", [P, NG, L], F32)
    shift_d = dram("shift_scratch", [HG, NG, L], F32)
    o_d = dram("o_scratch", [D, L], F32)

    ctx = ExitStack()
    with ctx:
        def sb(name, shape, dt, where=None):
            return (where or ctx).enter_context(nc.sbuf_tensor(name, shape, dt))

        def sem(name):
            return ctx.enter_context(nc.semaphore(name))

        psum = ctx.enter_context(nc.psum_tensor("psum", [P, 8, CH], F32))
        ident = sb("ident", [P, P], F32)
        ident_ready = sem("ident_ready")
        unbounded = sb("unbounded", [1, 1], I32)


        projections(nc, ExitStack(), sb, sem, psum, ident, ident_ready, unbounded, locals())

        wo_hi = sb("wo_hi", [P, NG, D], F32R)
        wo_lo = sb("wo_lo", [P, NG, D], F32R)
        wr = sb("wr", [P, KT, 2, NE], F32R)
        wr_raw = sb("wr_raw", [P, KT, NE], F32)
        bo_all = sb("bo_all", [P, D], F32)
        br_all = sb("br_all", [P, NE], F32)
        be_st = sb("be_st", [2 * BIAS_STEP + NE, D], F32R)
        o_raw = [sb(f"o_raw{b}", [P, NG, P], F32) for b in range(2)]
        small_in = sem("small_in")
        wo_in = sem("wo_in")
        be_in = sem("be_in")
        wo_hi_ready = sem("wo_hi_ready")
        wo_lo_ready = sem("wo_lo_ready")
        o_in = [sem(f"o_in{b}") for b in range(2)]
        o_stored = sem("o_stored")

        def load_o(sp, b, head):
            o_v = o_d.rearrange("n (k a u r) -> n a k u r", a=HG, u=2, r=P)
            for a in range(HG):
                sp.dma_start(o_raw[b][a * DH:(a + 1) * DH, :, :], o_v[ds(head * DH, DH), a, :, b, :]).then_inc(o_in[b], 16)

        attention(nc, ExitStack(), sb, sem, psum, unbounded, locals())
        experts(nc, ExitStack(), sb, sem, psum, ident, locals())


def projections(nc, mem, sb0, sem, psum, ident, ident_ready, unbounded, g):
    L, D, S, KT, NG, NC, NSC, NT, LAST, TPC = (g[n] for n in "L D S KT NG NC NSC NT LAST TPC".split())
    x, ctxT, kh_d, kl_d, v_d, qh_d, ql_d, shift_d, SCALE = (g[n] for n in "x ctxT kh_d kl_d v_d qh_d ql_d shift_d SCALE".split())
    last_w = S - (NSC - 1) * CH

    with mem:
        def sb(name, shape, dt):
            return sb0(name, shape, dt, mem)

        w_raw = [sb(f"w_raw_{n}", [P, KT, D], F32) for n in "kvq"]
        w_hi = [sb(f"w_hi_{n}", [P, KT, D], F32R) for n in "kvq"]
        w_lo = [sb(f"w_lo_{n}", [P, KT, D], F32R) for n in "kvq"]
        bk_col = sb("bk_col", [P, NG], F32)
        bq_col = sb("bq_col", [P, NG], F32)
        bv_all = sb("bv_all", [P, D], F32)
        raw = [sb(f"raw{b}", [P, TPC, CH], F32) for b in range(2)]
        a_hi = [sb(f"a_hi{b}", [P, KT, CH], F32R) for b in range(2)]
        a_lo = [sb(f"a_lo{b}", [P, KT, CH], F32R) for b in range(2)]
        o_hi = [sb(f"o_hi{b}", [P, NG, CH], F32R) for b in range(2)]
        o_lo = [sb(f"o_lo{b}", [P, NG, CH], F32R) for b in range(2)]
        v_sb = [sb(f"v_sb{b}", [P, TPC, D], F32) for b in range(2)]
        xn = [sb(f"xn{b}", [P, TPC, D], F32) for b in range(2)]
        stats = sb("stats", [P, TPC, 6], F32)
        mv = sb("mv", [P, TPC, 2], F32)
        var = sb("var", [P, TPC], F32)
        std = sb("std", [P, TPC], F32)
        rstd = sb("rstd", [P, TPC], F32)
        tmp = sb("tmp", [P, TPC], F32)
        squares = sb("squares", [P, NG, CH], F32R)
        of_head = sb("of_head", [P, NG, P], F32R)
        k_norms = sb("k_norms", [P, NSC], F32)
        q_norms = sb("q_norms", [P, NC], F32)
        k_norm = sb("k_norm", [P, 1], F32)
        q_norm = sb("q_norm", [P, 1], F32)
        norms = sb("norms", [P, 1], F32)
        widest = sb("widest", [1, 1], F32)
        bound = sb("bound", [1, 1], F32)
        too_wide = sb("too_wide", [1, 1], F32)
        ones_row = sb("ones_row", [1, CH], F32)
        neg_bound = sb("neg_bound", [1, CH], F32R)

        w_in = {n: sem(f"w_in_{'kvq'[n]}") for n in (1, 2)}
        bias_in = sem("bias_in")
        w_hi_ready = sem("w_hi_ready")
        w_lo_ready = sem("w_lo_ready")
        wq_lo_ready = sem("wq_lo_ready")
        c_in = [sem(f"c_in{b}") for b in range(2)]
        first_in = [sem(f"first_in{k}") for k in range(KT)]
        first_hi = sem("first_hi")
        first_lo = sem("first_lo")
        x_in = [sem(f"x_in{b}") for b in range(2)]
        c_hi = sem("c_hi")
        c_lo = sem("c_lo")
        k_mm = sem("k_mm")
        v_mm = sem("v_mm")
        k_hi = sem("k_hi")
        k_lo = sem("k_lo")
        v_out = sem("v_out")
        k_stored = [sem(f"k_stored{b}") for b in range(2)]
        v_stored = [sem(f"v_stored{b}") for b in range(2)]
        ln_step = sem("ln_step")
        stats_ready = sem("stats_ready")
        stats_passed = sem("stats_passed")
        var_ready = sem("var_ready")
        std_ready = sem("std_ready")
        xn_ready = sem("xn_ready")
        x_turned = sem("x_turned")
        x_hi = sem("x_hi")
        x_lo = sem("x_lo")
        q_mm = sem("q_mm")
        q_hi = sem("q_hi")
        q_lo = sem("q_lo")
        q_stored = [sem(f"q_stored{b}") for b in range(2)]
        shift_stored = sem("shift_stored")
        selector = sem("selector")
        k_squared = sem("k_squared")
        q_squared = sem("q_squared")
        k_summed = sem("k_summed")
        q_summed = sem("q_summed")
        k_searched = sem("k_searched")
        q_searched = sem("q_searched")
        fold = sem("fold")
        folded = sem("folded")
        norms_turned = sem("norms_turned")
        widest_ready = sem("widest_ready")
        bound_ready = sem("bound_ready")
        neg_ready = sem("neg_bound_ready")

        ctx_v = ctxT.rearrange("(k p) s -> p k s", p=P)
        x_v = x.rearrange("(u p s) d -> p s u d", p=P, s=HEADS)
        per_place = L // HEADS // P
        places = TPC // per_place
        pairs = (NSC - 1) // 2
        assert NSC % 2 == 1 and NC % 2 == 0
        K_SUM_BANK, Q_SUM_BANK = 0, 3
        LN_STEPS = TPC + 5

        half = NG // 2

        def q_chunks(eng, body):
            body(0, 0, 0)
            with eng.Fori(0, (NC - 4) // 2) as i:
                body(i * 2 + 1, 1, i)
                body(i * 2 + 2, 0, i + 1)
            for c in range(NC - 3, NC):
                body(c, c % 2, c // 2)

        def ahead(c, n):
            return not isinstance(c, int) or c + n < NC

        with nc.Block() as block:
            @block.sync
            def _(sp):
                def load_ctx(c, b, w):
                    sp.dma_start(raw[b][:, :, 0:w], ctx_v[:, :, ds(c * CH, w)]).then_inc(c_in[b], 16)

                def load_x(c, b):
                    for s in range(places):
                        sp.dma_start(xn[b][:, s * per_place:(s + 1) * per_place, :],
                                     x_v[:, ds(c * places + s, 1), :, :].rearrange("p s u d -> p (s u) d")).then_inc(x_in[b], 16)

                for k in range(KT):
                    sp.dma_start(w_raw[0][:, k, :], g["Wk"][k * P:(k + 1) * P, :]).then_inc(first_in[k], 16)
                    sp.dma_start(raw[0][:, k, :], ctx_v[:, k, 0:CH]).then_inc(first_in[k], 16)
                sp.dma_start(w_raw[1][:], g["Wv"].rearrange("(k p) n -> p k n", p=P)).then_inc(w_in[1], 16)
                sp.dma_start(bk_col[:], g["bk"]).then_inc(bias_in, 16)
                sp.dma_start(bq_col[:], g["bq"]).then_inc(bias_in, 16)
                sp.dma_start(bv_all[:], g["bv"].rearrange("(o n) -> o n", o=1).to_broadcast([P, D])).then_inc(bias_in, 16)
                load_ctx(1, 1, CH)
                sp.dma_start(w_raw[2][:], g["Wq"].rearrange("(k p) n -> p k n", p=P)).then_inc(w_in[2], 16)
                load_x(0, 0)
                load_x(1, 1)

                def store_kv(c, b, w):
                    sp.wait_ge(k_hi, (c + 1) * NG)
                    sp.wait_ge(k_lo, (c + 1) * NG)
                    sp.dma_start(kh_d[:, :, ds(c * CH, w)], o_hi[b][:, :, 0:w].bitcast(F32)).then_inc(k_stored[b], 16)
                    sp.dma_start(kl_d[:, :, ds(c * CH, w)], o_lo[b][:, :, 0:w].bitcast(F32)).then_inc(k_stored[b], 16)
                    if w == CH:
                        sp.wait_ge(v_out, (c + 1) * TPC)
                        sp.dma_start(v_d[:, ds(c * TPC, TPC), :], v_sb[b][:]).then_inc(v_stored[b], 16)
                    else:
                        full = w // P
                        sp.wait_ge(v_out, c * TPC + full + 1)
                        sp.dma_start(v_d[:, ds(c * TPC, full), :], v_sb[b][:, 0:full, :]).then_inc(v_stored[b], 16)
                        sp.dma_start(v_d[0:LAST, ds(c * TPC + full, 1), :], v_sb[b][0:LAST, full:full + 1, :]).then_inc(v_stored[b], 16)

                with sp.Fori(0, pairs - 1) as i:
                    for b in range(2):
                        c = i * 2 + b
                        sp.wait_ge(c_hi, c + 1)
                        sp.wait_ge(c_lo, c + 1)
                        load_ctx(c + 2, b, CH)
                        store_kv(c, b, CH)
                c = 2 * (pairs - 1)
                sp.wait_ge(c_hi, c + 1)
                sp.wait_ge(c_lo, c + 1)
                load_ctx(c + 2, 0, last_w)
                store_kv(c, 0, CH)
                store_kv(c + 1, 1, CH)

                store_kv(c + 2, 0, last_w)

                def store_q(c, b):
                    sp.wait_ge(q_hi, (c + 1) * NG)
                    sp.wait_ge(q_lo, (c + 1) * NG)
                    sp.dma_start(qh_d[:, :, ds(c * CH, CH)], o_hi[b][:].bitcast(F32)).then_inc(q_stored[b], 16)
                    sp.dma_start(ql_d[:, :, ds(c * CH, CH)], o_lo[b][:].bitcast(F32)).then_inc(q_stored[b], 16)

                def next_x(c, b):
                    sp.wait_ge(x_turned, (c - 1) * KT)
                    load_x(c, b)

                next_x(2, 0)
                with sp.Fori(0, (NC - 4) // 2) as i:
                    for b in range(2):
                        next_x(i * 2 + (b + 3), 1 - b)
                        store_q(i * 2 + b, b)
                next_x(NC - 1, 1)
                for c in range(NC - 4, NC):
                    store_q(c, c % 2)
                sp.wait_ge(neg_ready, 1)
                sp.dma_start(shift_d.rearrange("(o g) j (c n) -> o (g j c) n", o=1, n=CH),
                             neg_bound[:].bitcast(F32).rearrange("o (r n) -> o r n", r=1).to_broadcast([1, HG * NG * NC, CH])).then_inc(shift_stored, 16)
                sp.wait_ge(shift_stored, 16)
                for b in range(2):
                    sp.wait_ge(k_stored[b], 32 * ((NSC + 1 - b) // 2))
                    sp.wait_ge(v_stored[b], 16 * ((NSC + 1 - b) // 2 + (1 - b)))
                    sp.wait_ge(q_stored[b], 32 * (NC // 2))

            @block.gpsimd
            def _(pool):
                pool.memset(ident[:], 0.0).then_inc(ident_ready, 1)
                pool.wait_ge(ident_ready, 1)
                pool.affine_select(out=ident[:], in_=ident[:], compare_op=ALU.not_equal, fill=1.0,
                                   base=0, pattern=[[-1, P]], channel_multiplier=1).then_inc(ident_ready, 1)
                def square(c, b, w, hi, squared, summed):
                    for j in range(NG):
                        pool.wait_ge(hi, c * NG + (j + 1))
                        if j == 0 and summed is not None:
                            pool.wait_ge(*summed)
                        h = o_hi[b][:, j, 0:w].bitcast(F32)
                        pool.tensor_tensor(squares[:, j, 0:w], h, h, ALU.mult).then_inc(squared, 1)

                square(0, 0, CH, k_hi, k_squared, None)
                pool.wait_ge(w_in[2], 16)
                pool.wait_ge(w_hi_ready, 3)
                pool.tensor_tensor(w_lo[2][:], w_raw[2][:], w_hi[2][:].bitcast(F32), ALU.subtract).then_inc(wq_lo_ready, 1)
                with pool.Fori(0, pairs - 1) as i:
                    square(i * 2 + 1, 1, CH, k_hi, k_squared, (k_summed, i * 2 + 1))
                    square(i * 2 + 2, 0, CH, k_hi, k_squared, (k_summed, i * 2 + 2))
                square(NSC - 2, 1, CH, k_hi, k_squared, (k_summed, NSC - 2))
                square(NSC - 1, 0, last_w, k_hi, k_squared, (k_summed, NSC - 1))
                square(0, 0, CH, q_hi, q_squared, (k_summed, NSC))
                with pool.Fori(0, NC // 2 - 1) as i:
                    square(i * 2 + 1, 1, CH, q_hi, q_squared, (q_summed, i * 2 + 1))
                    square(i * 2 + 2, 0, CH, q_hi, q_squared, (q_summed, i * 2 + 2))
                square(NC - 1, 1, CH, q_hi, q_squared, (q_summed, NC - 1))

            @block.scalar
            def _(act):
                for k in range(KT):
                    last = k == KT - 1
                    act.wait_ge(first_in[k], 32)
                    act.activation(w_hi[0][:, k, :], w_raw[0][:, k, :], ACT.Copy).then_inc(w_hi_ready if last else first_hi, 1)
                    act.activation(a_hi[0][:, k, :], raw[0][:, k, :], ACT.Copy).then_inc(c_hi if last else first_hi, 1)

                def ctx_chunk(c, b, i, w):
                    act.wait_ge(c_in[b], 16 * (i + b))
                    act.wait_ge(v_mm, (c - 1) * TPC)
                    act.activation(a_hi[b][:, :, 0:w], raw[b][:, :, 0:w], ACT.Copy).then_inc(c_hi, 1)

                def k_chunk(c, b, i, w):
                    act.wait_ge(k_stored[b], i * 32)
                    for j in range(NG):
                        act.wait_ge(k_mm, c * NG + (j + 1))
                        act.activation(o_hi[b][:, j, 0:w], psum[:, j, 0:w], ACT.Identity,
                                       bias=bk_col[:, j:j + 1]).then_inc(k_hi, 1)

                act.wait_ge(w_in[1], 16)
                act.activation(w_hi[1][:], w_raw[1][:], ACT.Copy).then_inc(w_hi_ready, 1)
                act.wait_ge(w_in[2], 16)
                act.activation(w_hi[2][:], w_raw[2][:], ACT.Copy).then_inc(w_hi_ready, 1)
                act.wait_ge(bias_in, 48)

                def ctx_pair(i, w_next):
                    k_chunk(i * 2, 0, i, CH)
                    ctx_chunk(i * 2 + 1, 1, i, CH)
                    k_chunk(i * 2 + 1, 1, i, CH)
                    ctx_chunk(i * 2 + 2, 0, i + 1, w_next)

                with act.Fori(0, pairs - 1) as i:
                    ctx_pair(i, CH)
                ctx_pair(pairs - 1, last_w)

                def x_stats(c):
                    act.wait_ge(var_ready, c + 1)
                    act.activation(std[:], var[:], ACT.Sqrt).then_inc(std_ready, 1)

                x_stats(0)
                k_chunk(NSC - 1, 0, pairs, last_w)

                def x_split(c, b):
                    for k in range(KT):
                        act.wait_ge(x_turned, c * KT + (k + 1))
                        act.activation(a_hi[b][:, k, :], psum[:, k, :], ACT.Copy).then_inc(x_hi, 1)

                def q_split(c, b, i, js):
                    if js.start == 0:
                        act.wait_ge(q_stored[b], i * 32)
                    for j in js:
                        act.wait_ge(q_mm, c * NG + (j + 1))
                        act.activation(o_hi[b][:, j, :], psum[:, 4 + j, :], ACT.Identity,
                                       bias=bq_col[:, j:j + 1]).then_inc(q_hi, 1)

                act.wait_ge(v_mm, (NSC - 1) * TPC + last_w // P + 1)
                for b in range(2):
                    act.wait_ge(k_stored[b], 32 * ((NSC + 1 - b) // 2))
                x_split(0, 0)
                x_stats(1)

                def q_chunk(c, b, i):
                    q_split(c, b, i, range(half))
                    if ahead(c, 1):
                        x_split(c + 1, 1 - b)
                    q_split(c, b, i, range(half, NG - 1))
                    if ahead(c, 2):
                        x_stats(c + 2)
                    q_split(c, b, i, range(NG - 1, NG))

                q_chunks(act, q_chunk)
                act.wait_ge(widest_ready, 1)
                act.activation(bound[:], widest[:], ACT.Sqrt, scale=SLACK).then_inc(bound_ready, 1)

            @block.vector
            def _(dve):
                def w_low(n):
                    dve.wait_ge(w_hi_ready, n + 1)
                    dve.tensor_tensor(w_lo[n][:], w_raw[n][:], w_hi[n][:].bitcast(F32), ALU.subtract).then_inc(w_lo_ready, 1)

                def ctx_low(c, b, w):
                    dve.wait_ge(c_hi, c + 1)
                    dve.tensor_tensor(a_lo[b][:, :, 0:w], raw[b][:, :, 0:w], a_hi[b][:, :, 0:w].bitcast(F32),
                                      ALU.subtract).then_inc(c_lo, 1)

                def k_low(c, b, w):
                    for j in range(NG):
                        dve.wait_ge(k_hi, c * NG + (j + 1))
                        dve.scalar_tensor_tensor(out=o_lo[b][:, j, 0:w], in0=psum[:, j, 0:w], scalar=bk_col[:, j:j + 1],
                                                 in1=o_hi[b][:, j, 0:w].bitcast(F32), op0=ALU.add, op1=ALU.subtract).then_inc(k_lo, 1)

                def v_chunk(c, b, i, w):
                    dve.wait_ge(v_stored[b], i * 16)
                    for t in range(-(-w // P)):
                        n = min(P, w - t * P)
                        dve.wait_ge(v_mm, c * TPC + (t + 1))
                        dve.tensor_tensor(v_sb[b][0:n, t, :], psum[0:n, 4 + t, :], bv_all[0:n, :], ALU.add).then_inc(v_out, 1)
                        if t == min(1, w // P - 1):
                            search(k_norms, c, K_SUM_BANK, w, k_summed, k_searched)

                def search(norms_of, c, bank, w, summed, searched):
                    dve.wait_ge(summed, c + 1)
                    dve.tensor_reduce(norms_of[:, ds(c, 1)], psum[:, bank, 0:w], AX.X, ALU.max).then_inc(searched, 1)

                for k in range(KT):
                    last = k == KT - 1
                    for wanted, now, ready in ((2 * k + 1, w_hi_ready, w_lo_ready), (2 * k + 2, c_hi, c_lo)):
                        dve.wait_ge(now if last else first_hi, 1 if last else wanted)
                        raw_k, hi_k, lo_k = (w_raw[0], w_hi[0], w_lo[0]) if ready is w_lo_ready else (raw[0], a_hi[0], a_lo[0])
                        dve.tensor_tensor(lo_k[:, k, :], raw_k[:, k, :], hi_k[:, k, :].bitcast(F32), ALU.subtract).then_inc(ready if last else first_lo, 1)
                dve.memset(of_head[:].bitcast(F32), 0.0).then_inc(selector, 1)
                dve.memset(ones_row[:], 1.0).then_inc(selector, 1)
                dve.wait_ge(selector, 1)
                for j in range(NG):
                    for h in range(HG):
                        dve.memset(of_head[h * DH:(h + 1) * DH, j, HG * j + h:HG * j + h + 1].bitcast(F32), 1.0).then_inc(selector, 1)
                w_low(1)
                dve.wait_ge(bias_in, 48)

                def ctx_pair(i, w_next):
                    k_low(i * 2, 0, CH)
                    ctx_low(i * 2 + 1, 1, CH)
                    v_chunk(i * 2, 0, i, CH)
                    k_low(i * 2 + 1, 1, CH)
                    ctx_low(i * 2 + 2, 0, w_next)
                    v_chunk(i * 2 + 1, 1, i, CH)

                with dve.Fori(0, pairs - 1) as i:
                    ctx_pair(i, CH)
                ctx_pair(pairs - 1, last_w)
                def ln(c, b, i):
                    base = c * LN_STEPS
                    n = [0]

                    def step(ins, wait=True):
                        n[0] += 1
                        ins.then_inc(ln_step, 1)
                        if wait:
                            dve.wait_ge(ln_step, base + n[0])

                    dve.wait_ge(x_in[b], (16 * places) * (i + 1))
                    for t in range(TPC):
                        ins = dve.bn_stats(stats[:, t, :], xn[b][:, t, :])
                    ins.then_inc(stats_ready, 1)
                    dve.wait_ge(stats_ready, c + 1)
                    dve.sem_inc(stats_passed, 1)
                    for t in range(TPC):
                        step(dve.bn_aggr(mv[:, t, :], stats[:, t, :]), t == TPC - 1)
                    dve.tensor_scalar(var[:], mv[:, :, 1], EPS, None, ALU.add).then_inc(var_ready, 1)
                    dve.wait_ge(std_ready, c + 1)
                    step(dve.reciprocal(rstd[:], std[:]))
                    step(dve.tensor_tensor(tmp[:], rstd[:], rstd[:], ALU.mult))
                    step(dve.tensor_tensor(tmp[:], tmp[:], var[:], ALU.mult))
                    step(dve.tensor_scalar(tmp[:], tmp[:], -0.5, 1.5, ALU.mult, ALU.add))
                    step(dve.tensor_tensor(rstd[:], rstd[:], tmp[:], ALU.mult))
                    assert n[0] == LN_STEPS
                    for t in range(TPC):
                        ins = dve.tensor_scalar(xn[b][:, t, :], xn[b][:, t, :], mv[:, t, 0:1], rstd[:, t:t + 1],
                                                ALU.subtract, ALU.mult)
                    ins.then_inc(xn_ready, 1)

                def x_low(c, b):
                    for k in range(KT):
                        dve.wait_ge(x_hi, c * KT + (k + 1))
                        dve.tensor_tensor(a_lo[b][:, k, :], psum[:, k, :], a_hi[b][:, k, :].bitcast(F32),
                                          ALU.subtract).then_inc(x_lo, 1)

                def q_low(c, b, js):
                    for j in js:
                        dve.wait_ge(q_hi, c * NG + (j + 1))
                        dve.scalar_tensor_tensor(out=o_lo[b][:, j, :], in0=psum[:, 4 + j, :], scalar=bq_col[:, j:j + 1],
                                                 in1=o_hi[b][:, j, :].bitcast(F32), op0=ALU.add, op1=ALU.subtract).then_inc(q_lo, 1)

                def q_search(c):
                    search(q_norms, c, Q_SUM_BANK, CH, q_summed, q_searched)

                ln(0, 0, 0)
                k_low(NSC - 1, 0, last_w)
                v_chunk(NSC - 1, 0, pairs, last_w)
                x_low(0, 0)
                ln(1, 1, 0)

                def q_chunk(c, b, i):
                    q_low(c, b, range(half))
                    if not (isinstance(c, int) and c == 0):
                        q_search(c - 1)
                    if ahead(c, 1):
                        x_low(c + 1, 1 - b)
                    if ahead(c, 2):
                        ln(c + 2, b, i + 1)
                    q_low(c, b, range(half, NG))

                q_chunks(dve, q_chunk)
                q_search(NC - 1)

                dve.wait_ge(k_searched, NSC)
                dve.wait_ge(q_searched, NC)
                dve.tensor_reduce(k_norm[:], k_norms[:], AX.X, ALU.max).then_inc(fold, 1)
                dve.tensor_reduce(q_norm[:], q_norms[:], AX.X, ALU.max).then_inc(fold, 1)
                dve.wait_ge(fold, 2)
                dve.tensor_tensor(norms[:], k_norm[:], q_norm[:], ALU.mult).then_inc(folded, 1)
                dve.wait_ge(norms_turned, 1)
                dve.tensor_reduce(widest[:], psum[0:1, K_SUM_BANK, 0:P], AX.X, ALU.max).then_inc(widest_ready, 1)
                dve.wait_ge(bound_ready, 1)
                dve.tensor_scalar(neg_bound[:], ones_row[:], bound[:], -1.0, ALU.mult, ALU.mult).then_inc(neg_ready, 1)
                dve.tensor_scalar(too_wide[:], bound[:], WIDEST / SCALE, None, ALU.is_le).then_inc(fold, 1)
                dve.wait_ge(fold, 3)
                dve.tensor_scalar(too_wide[:], too_wide[:], -1.0, 1.0, ALU.mult, ALU.add).then_inc(fold, 1)
                dve.wait_ge(fold, 4)
                dve.tensor_copy(unbounded[:], too_wide[:]).then_inc(fold, 1)
                dve.wait_ge(fold, 5)

            @block.tensor
            def _(pe):
                def products(bank, m, n, lhs, rhs):
                    terms = [(k, a, b) for k in range(KT) for a, b in ((0, 0), (0, 1), (1, 0))]
                    for q, (k, a, b) in enumerate(terms):
                        mm = pe.matmul(psum[0:m, bank, 0:n], lhs[a](k), rhs[b](k), start=q == 0, stop=q == len(terms) - 1)
                    return mm

                def sum_squares(c, bank, w, squared, summed):
                    pe.wait_ge(squared, (c + 1) * NG)
                    for j in range(NG):
                        mm = pe.matmul(psum[:, bank, 0:w], of_head[:, j, :], squares[:, j, 0:w], start=j == 0, stop=j == NG - 1)
                    mm.then_inc(summed, 1)

                def k_products(c, b, w):
                    pe.wait_ge(k_searched, c)
                    pe.wait_ge(c_hi, c + 1)
                    pe.wait_ge(c_lo, c + 1)
                    pe.wait_ge(k_lo, c * NG)
                    for j in range(NG):
                        products(j, P, w, [lambda k, W=W: W[0][:, k, j * P:(j + 1) * P] for W in (w_hi, w_lo)],
                                 [lambda k, A=A: A[b][:, k, 0:w] for A in (a_hi, a_lo)]).then_inc(k_mm, 1)

                def v_products(c, b, w):
                    pe.wait_ge(v_out, c * TPC)
                    for t in range(-(-w // P)):
                        products(4 + t, P, D, [lambda k, A=A: A[b][:, k, t * P:(t + 1) * P] for A in (a_hi, a_lo)],
                                 [lambda k, W=W: W[1][:, k, :] for W in (w_hi, w_lo)]).then_inc(v_mm, 1)
                        if t == min(1, w // P - 1):
                            pe.wait_ge(k_lo, c * NG + 1)
                            sum_squares(c, K_SUM_BANK, w, k_squared, k_summed)

                for k in range(KT):
                    last = k == KT - 1
                    if not last:
                        pe.wait_ge(first_hi, 2 * k + 2)
                        pe.wait_ge(first_lo, 2 * k + 2)
                    else:
                        for ready in (w_hi_ready, c_hi, w_lo_ready, c_lo):
                            pe.wait_ge(ready, 1)
                    for j in range(NG):
                        terms = ((w_hi, a_hi), (w_hi, a_lo), (w_lo, a_hi))
                        for n, (W, A) in enumerate(terms):
                            mm = pe.matmul(psum[:, j, :], W[0][:, k, j * P:(j + 1) * P], A[0][:, k, :],
                                           start=k == 0 and n == 0, stop=last and n == len(terms) - 1)
                        if last:
                            mm.then_inc(k_mm, 1)
                pe.wait_ge(w_hi_ready, 2)
                pe.wait_ge(w_lo_ready, 2)
                pe.wait_ge(selector, 2 + HEADS)

                def ctx_pair(i, w_next):
                    v_products(i * 2, 0, CH)
                    k_products(i * 2 + 1, 1, CH)
                    v_products(i * 2 + 1, 1, CH)
                    k_products(i * 2 + 2, 0, w_next)

                with pe.Fori(0, pairs - 1) as i:
                    ctx_pair(i, CH)
                ctx_pair(pairs - 1, last_w)
                v_products(NSC - 1, 0, last_w)

                def turn(c, b):
                    pe.wait_ge(xn_ready, c + 1)
                    pe.wait_ge(x_lo, c * KT)
                    for k in range(KT):
                        if k == Q_SUM_BANK and not (isinstance(c, int) and c < 2):
                            pe.wait_ge(q_searched, c - 1)
                        for t in range(TPC):
                            mm = pe.transpose(psum[:, k, t * P:(t + 1) * P], xn[b][:, t, k * P:(k + 1) * P], ident[:])
                        mm.then_inc(x_turned, 1)

                def q_products(c, b, js):
                    pe.wait_ge(x_hi, (c + 1) * KT)
                    pe.wait_ge(x_lo, (c + 1) * KT)
                    if not (isinstance(c, int) and c == 0):
                        pe.wait_ge(q_lo, c * NG + (js.stop - NG))
                    for j in js:
                        products(4 + j, P, CH, [lambda k, W=W: W[2][:, k, j * P:(j + 1) * P] for W in (w_hi, w_lo)],
                                 [lambda k, A=A: A[b][:, k, :] for A in (a_hi, a_lo)]).then_inc(q_mm, 1)

                pe.wait_ge(ident_ready, 2)
                pe.wait_ge(k_lo, NSC * NG)
                pe.wait_ge(k_searched, NSC)
                turn(0, 0)
                pe.wait_ge(v_out, (NSC - 1) * TPC + last_w // P + 1)
                pe.wait_ge(w_hi_ready, 3)
                pe.wait_ge(wq_lo_ready, 1)
                def q_chunk(c, b, i):
                    q_products(c, b, range(half))
                    if not (isinstance(c, int) and c == 0):
                        sum_squares(c - 1, Q_SUM_BANK, CH, q_squared, q_summed)
                    if ahead(c, 1):
                        turn(c + 1, 1 - b)
                    q_products(c, b, range(half, NG))

                q_chunks(pe, q_chunk)
                pe.wait_ge(q_searched, NC - 1)
                sum_squares(NC - 1, Q_SUM_BANK, CH, q_squared, q_summed)
                pe.wait_ge(folded, 1)
                pe.transpose(psum[0:1, K_SUM_BANK, 0:P], norms[:], ident[:]).then_inc(norms_turned, 1)


def attention(nc, mem, sb0, sem, psum, unbounded, g):
    S, SP_, NG, NC, NT, LAST, SCALE, D = (g[n] for n in "S SP_ NG NC NT LAST SCALE D".split())
    kh_d, kl_d, v_d, qh_d, ql_d, shift_d, o_d = (g[n] for n in "kh_d kl_d v_d qh_d ql_d shift_d o_d".split())
    NE, be_in = g["NE"], g["be_in"]
    NIT = NG * NC
    NP = 2 * NT
    ROWS = 3 * DH
    FILLS = 4
    SH = ROWS
    ROUND = 2 * S_RING
    MIDDLE = (NIT - 2) // ROUND * ROUND
    O_BANK, SUM_BANK = 6, 7
    TPC = CH // P

    with mem:
        def sb(name, shape, dt):
            return sb0(name, shape, dt, mem)

        k_st = sb("k_st", [SH + 1, HG, SP_], F32R)
        q_st = sb("q_st", [SH + 1, 2, HG, CH], F32R)
        v_st = sb("v_st", [P, NT, P], F32)
        ones = sb("ones", [P, DH], F32)
        probs = sb("probs", [P, P_RING + LAG, HG, CH], F32)
        sums = [sb(f"sums{b}", [P, HG, CH], F32) for b in range(2)]
        wo_raw = sums[1]
        pool_sums = sb("pool_sums", [P, HG, CH], F32)
        recip = sb("recip", [P, CH], F32)
        o_sb = sb("o_sb", [P, CH], F32)
        be_raw = recip[0:2 * BIAS_STEP + NE]
        mx = sb("mx", [P, TPC, HG, 2], F32)
        mxx = sb("mxx", [P, HG, TPC], F32)
        neg = sb("neg", [P, HG, TPC], F32R)

        cuts = [0, *PIECE_ENDS, NT]
        pieces = [(a, b - a) for a, b in zip(cuts, cuts[1:])]
        K_PIECES = len(pieces)
        piece_of = {a: n for n, (a, _) in enumerate(pieces)}

        filled = sem("filled")
        rows_filled = [sem(f"rows_filled{n}") for n in range(K_PIECES)]
        ma_k_in = sem("ma_k_in")
        ma_q_in = sem("ma_q_in")
        ma_mm = sem("ma_mm")
        ma_max = sem("ma_max")
        ma_neg = sem("ma_neg")
        ma_fold = sem("ma_fold")
        ma_stored = sem("ma_stored")
        q_in = [sem(f"q_in{b}") for b in range(2)]
        k_in = [sem(f"k_in{n}") for n in range(K_PIECES)]
        v_in = [sem(f"v_in{n}") for n in range(K_PIECES)]
        s_ready = sem("s_ready")
        exp_done = sem("exp_done")
        pv_done = sem("pv_done")
        added = sem("added")
        pool_added = sem("pool_added")
        pool_taken = sem("pool_taken")
        sums_ready = sem("sums_ready")
        inverted = sem("inverted")
        o_final = sem("o_final")
        o_left = sem("o_left")
        small_in, wo_in, wo_hi_ready, wo_lo_ready, o_stored = (
            g[n] for n in "small_in wo_in wo_hi_ready wo_lo_ready o_stored".split())
        wo_hi, wo_lo, wr_raw, wr, bo_all, br_all, be_st = (g[n] for n in "wo_hi wo_lo wr_raw wr bo_all br_all be_st".split())

        def load_k(sp, j, first, n, count):
            for r, src in enumerate((kh_d, kh_d, kl_d)):
                sp.dma_start(k_st[r * DH:(r + 1) * DH, :, first:first + n].bitcast(F32),
                             src[:, ds(j, 1), first:first + n].rearrange("(h d) o s -> d (h o) s", d=DH)).then_inc(count, 16)

        def load_q(sp, b, it, count):
            for r, src in enumerate((qh_d, ql_d, qh_d)):
                sp.dma_start(q_st[r * DH:(r + 1) * DH, b, :, :].bitcast(F32),
                             src.rearrange("(h d) j l -> d h (j l)", d=DH)[:, :, ds(it * CH, CH)]).then_inc(count, 16)

        def s_slot(phase, n):
            return (phase * NP + n) % S_RING

        p_slot = [t % P_RING if t < NT - LAG else P_RING + t - (NT - LAG) for t in range(NT)]

        def before(t):
            found = [(0, u) for u in range(t) if p_slot[u] == p_slot[t]] or [(-1, u) for u in range(NT) if p_slot[u] == p_slot[t]]
            return found[-1]

        on_pool = list(SUM_ON_POOL)
        on_dve = [t for t in range(NT) if t not in on_pool] + [None]
        adds, pool_adds = len(on_dve) - 1, len(on_pool) - 1
        add_of = {t: max(n, 1) for n, t in enumerate(on_dve)}
        pool_add_of = {t: max(n, 1) for n, t in enumerate(on_pool)}

        def fill_rows(eng, heads):
            for n, (a, m) in enumerate(pieces):
                eng.memset(k_st[SH:SH + 1, heads[0]:heads[1], a * P:min((a + m) * P, S)].bitcast(F32), 1.0).then_inc(rows_filled[n], 1)

        with nc.Block() as block:
            @block.gpsimd
            def _(pool):
                fill_rows(pool, (0, HG // 2))
                for n in range(K_PIECES):
                    pool.wait_ge(rows_filled[n], 2)

                def step(it):
                    for k, t in enumerate(on_pool[1:]):
                        if k == pool_adds // 2 and isinstance(it, int):
                            pool.wait_ge(wo_hi_ready, 3)
                            pool.tensor_tensor(wo_lo[:], wo_raw[:], wo_hi[:].bitcast(F32), ALU.subtract).then_inc(wo_lo_ready, 1)
                            pool.tensor_tensor(wr[:, :, 1, :], wr_raw[:], wr[:, :, 0, :].bitcast(F32), ALU.subtract).then_inc(wo_lo_ready, 1)
                            pool.wait_ge(wo_lo_ready, 2)
                            third = slice(2 * BIAS_STEP, 2 * BIAS_STEP + NE)
                            pool.tensor_tensor(be_st[third], be_raw[third], be_st[third].bitcast(F32), ALU.subtract).then_inc(wo_lo_ready, 1)
                            pool.wait_ge(wo_lo_ready, 3)
                        pool.wait_ge(exp_done, it * NP + (2 * t + 2))
                        if k == 0:
                            pool.wait_ge(pool_taken, it)
                            a = probs[:, p_slot[on_pool[0]]]
                        else:
                            pool.wait_ge(pool_added, it * pool_adds + k)
                            a = pool_sums[:]
                        pool.tensor_tensor(pool_sums[:], a, probs[:, p_slot[t]], ALU.add).then_inc(pool_added, 1)

                step(0)
                with pool.Fori(1, NIT) as it:
                    step(it)

            @block.sync
            def _(sp):
                with sp.If(sp.value_load(unbounded[0:1, 0:1], min_val=0, max_val=1) == 1):
                    with sp.Fori(0, NG) as j:
                        sp.wait_ge(ma_mm, j * (NC * TPC * HG * 2))
                        load_k(sp, j, 0, S, ma_k_in)
                        with sp.Fori(0, NC) as c:
                            sp.wait_ge(ma_mm, j * (NC * TPC * HG * 2) + c * (TPC * HG * 2))
                            load_q(sp, 0, j * NC + c, ma_q_in)
                            sp.wait_ge(ma_neg, j * NC + c + 1)
                            for h in range(HG):
                                sp.dma_start(shift_d[h, ds(j, 1), ds(c * CH, CH)].rearrange("o (t p) -> p (o t)", p=P),
                                             neg[:, h, :].bitcast(F32), allow_slow_non_contiguous=True).then_inc(ma_stored, 16)
                    sp.wait_ge(ma_stored, NIT * HG * 16)

                def queries(it, b):
                    load_q(sp, b, it, q_in[b])
                    sp.dma_start(q_st[SH:SH + 1, b, :, :].bitcast(F32),
                                 shift_d.rearrange("(o h) j l -> o h (j l)", o=1)[:, :, ds(it * CH, CH)]).then_inc(q_in[b], 16)

                def keys(j, before, n):
                    a, m = pieces[n]
                    if before is not None:
                        sp.wait_ge(s_ready, before * NP + 2 * (a + m))
                    load_k(sp, j, a * P, min((a + m) * P, S) - a * P, k_in[n])

                def values(j, before, n):
                    a, m = pieces[n]
                    if before is not None:
                        sp.wait_ge(pv_done, before * NT + (a + m))
                    full = m - (n == K_PIECES - 1)
                    sp.dma_start(v_st[:, a:a + full, :], v_d[:, a:a + full, ds(j * P, P)]).then_inc(v_in[n], 16)
                    if n == K_PIECES - 1:
                        if before is None:
                            sp.wait_ge(filled, FILLS)
                        sp.dma_start(v_st[0:LAST, NT - 1, :], v_d[0:LAST, NT - 1, ds(j * P, P)]).then_inc(v_in[n], 16)

                def keys_values(j, before):
                    for n in range(K_PIECES):
                        keys(j, before, n)
                        values(j, before, n)

                def result(j, c, it):
                    sp.wait_ge(o_final, it + 1)
                    sp.dma_start(o_d[ds(j * P, P), ds(c * CH, CH)], o_sb[:]).then_inc(o_stored, 16)

                def step(j, c, b, reload, more=True):
                    it = j * NC + c
                    if more:
                        sp.wait_ge(s_ready, it * NP)
                        queries(it + 1, 1 - b)
                    if reload:
                        keys_values(j + 1, it)
                    result(j, c, it)

                keys(0, None, 0)
                queries(0, 0)
                for n in range(K_PIECES):
                    if n > 0:
                        keys(0, None, n)
                    values(0, None, n)
                sp.dma_start(wo_raw[:], g["Wo"].rearrange("(j p) n -> p j n", p=P)).then_inc(wo_in, 16)
                sp.dma_start(wr_raw[:], g["WrT"].rearrange("(k p) e -> p k e", p=P)).then_inc(wo_in, 16)
                sp.dma_start(bo_all[:], g["bo"].rearrange("(o n) -> o n", o=1).to_broadcast(list(bo_all.shape))).then_inc(small_in, 16)
                sp.dma_start(br_all[:], g["br"].rearrange("(o n) -> o n", o=1).to_broadcast(list(br_all.shape))).then_inc(small_in, 16)
                for n in range(3):
                    sp.dma_start(be_raw[n * BIAS_STEP:n * BIAS_STEP + NE], g["be"]).then_inc(be_in, 16)

                def group(j, last):
                    with sp.Fori(0, NC // 2 - 1) as i:
                        for b in range(2):
                            step(j, i * 2 + b, b, False)
                    step(j, NC - 2, 0, False)
                    step(j, NC - 1, 1, not last, not last)

                with sp.Fori(0, NG - 1) as j:
                    group(j, False)
                sp.wait_ge(o_stored, NC * 16)
                for b in range(2):
                    g["load_o"](sp, b, 0)
                group(NG - 1, True)
                sp.wait_ge(o_stored, NIT * 16)

            @block.scalar
            def _(act):
                act.preload_act_table(ACT.Exp)

                def step(it, phase):
                    first = isinstance(it, int) and it == 0
                    for n in range(NP):
                        t, half = divmod(n, 2)
                        slot = s_slot(phase, n)
                        if first and n == NP // 3:
                            act.wait_ge(wo_in, 32)
                            act.activation(wo_hi[:], wo_raw[:], ACT.Copy).then_inc(wo_hi_ready, 1)
                            act.activation(wr[:, :, 0, :], wr_raw[:], ACT.Copy).then_inc(wo_hi_ready, 1)
                            act.wait_ge(be_in, 48)
                            act.activation(be_st[:], be_raw, ACT.Copy).then_inc(wo_hi_ready, 1)
                        act.wait_ge(s_ready, it * NP + (n + 1))
                        if half == 0:
                            ago, u = before(t)
                            if not (first and ago):
                                act.wait_ge(pv_done, (it + ago) * NT + (u + 1))
                                if u in add_of:
                                    act.wait_ge(added, (it + ago) * adds + add_of[u])
                                if u in pool_add_of:
                                    act.wait_ge(pool_added, (it + ago) * pool_adds + pool_add_of[u])
                        nc.scalar.activation(probs[:, p_slot[t], 2 * half:2 * half + 2, :],
                                             psum[:, 2 * slot:2 * slot + 2, :], ACT.Exp, scale=SCALE).then_inc(exp_done, 1)

                step(0, 0)
                with act.Fori(0, MIDDLE // S_RING) as r:
                    for u in range(S_RING):
                        step(r * S_RING + (u + 1), (u + 1) % S_RING)
                for it in range(MIDDLE + 1, NIT):
                    step(it, it % S_RING)

            @block.vector
            def _(dve):
                dve.memset(k_st[:, :, S:SP_].bitcast(F32), 0.0).then_inc(filled, 1)
                dve.memset(v_st[:, NT - 1, :], 0.0).then_inc(filled, 1)
                dve.memset(ones[:], 1.0).then_inc(filled, 1)
                dve.memset(be_raw, 0.0).then_inc(filled, 1)
                fill_rows(dve, (HG // 2, HG))

                with dve.If(dve.value_load(unbounded[0:1, 0:1], min_val=0, max_val=1) == 1):
                    with dve.Fori(0, NIT) as it:
                        k = 0
                        for t in range(TPC):
                            for h in range(HG):
                                for half in range(2):
                                    k += 1
                                    dve.wait_ge(ma_mm, it * (TPC * HG * 2) + k)
                                    w = 4 * CH if half == 0 else S - 4 * CH
                                    dve.tensor_reduce(mx[:, t, h, half:half + 1],
                                                      psum[:, 4 * half:8, :].rearrange("p b n -> p (b n)")[:, 0:w], AX.X, ALU.max).then_inc(ma_max, 1)
                        dve.wait_ge(ma_max, (it + 1) * (TPC * HG * 2))
                        dve.tensor_tensor(mxx[:], mx[:, :, :, 0].rearrange("p t h -> p h t"), mx[:, :, :, 1].rearrange("p t h -> p h t"),
                                          ALU.max).then_inc(ma_fold, 1)
                        dve.wait_ge(ma_fold, it + 1)
                        dve.wait_ge(ma_stored, it * (HG * 16))
                        dve.tensor_scalar(neg[:], mxx[:], -1.0, None, ALU.mult).then_inc(ma_neg, 1)

                def add(it, b, k):
                    t = on_dve[k + 1]
                    n = P
                    if t is None:
                        dve.wait_ge(pool_added, (it + 1) * pool_adds)
                        term = pool_sums
                        done = pool_taken
                    else:
                        dve.wait_ge(exp_done, it * NP + (2 * t + 2))
                        term = probs[:, p_slot[t]]
                        if t == NT - 1:
                            n = LAST
                    if k == 0:
                        if not (isinstance(it, int) and it < 2):
                            dve.wait_ge(sums_ready, it - 1)
                        a = probs[:, p_slot[on_dve[0]]]
                    else:
                        dve.wait_ge(added, it * adds + k)
                        a = sums[b]
                    nc.vector.tensor_tensor(sums[b][0:n], a[0:n], term[0:n], ALU.add).then_inc(added, 1)
                    if t is None:
                        dve.wait_ge(added, (it + 1) * adds)
                        dve.sem_inc(pool_taken, 1)

                def fetch(it):
                    dve.wait_ge(pv_done, (it + 1) * NT)
                    dve.wait_ge(o_stored, it * 16)
                    nc.vector.tensor_copy(o_sb[:], psum[:, O_BANK, :]).then_inc(o_left, 1)

                def divide(it):
                    dve.wait_ge(sums_ready, it + 1)
                    nc.vector.reciprocal(recip[:], psum[:, SUM_BANK, :]).then_inc(inverted, 1)
                    dve.wait_ge(o_left, it + 1)
                    dve.wait_ge(inverted, it + 1)
                    nc.vector.tensor_tensor(o_sb[:], o_sb[:], recip[:], ALU.mult).then_inc(o_final, 1)

                def step(it, b, last=False):
                    for k in range(adds):
                        if k == adds - 1 and not last:
                            fetch(it)
                        add(it, b, k)
                        if k == DIVIDE_AT and not (isinstance(it, int) and it == 0):
                            divide(it - 1)
                    if last:
                        fetch(it)

                step(0, 0)
                dve.wait_ge(wo_lo_ready, 3)
                with dve.Fori(0, NIT // 2 - 1) as i:
                    step(i * 2 + 1, 1)
                    step(i * 2 + 2, 0)
                step(NIT - 1, 1, True)
                divide(NIT - 1)

            @block.tensor
            def _(pe):
                with pe.If(pe.value_load(unbounded[0:1, 0:1], min_val=0, max_val=1) == 1):
                    with pe.Fori(0, NG) as j:
                        with pe.Fori(0, NC) as c:
                            it = j * NC + c
                            pe.wait_ge(ma_k_in, (j + 1) * 48)
                            pe.wait_ge(ma_q_in, (it + 1) * 48)
                            k = 0
                            for t in range(TPC):
                                for h in range(HG):
                                    for half in range(2):
                                        if k >= 2:
                                            pe.wait_ge(ma_max, it * (TPC * HG * 2) + (k - 1))
                                        elif k == 0:
                                            pe.wait_ge(ma_max, it * (TPC * HG * 2))
                                        k += 1
                                        for b in range(4 * half, min(4 * half + 4, -(-S // CH))):
                                            w = min(CH, S - b * CH)
                                            mm = pe.matmul(psum[:, b, 0:w], q_st[0:ROWS, 0, h, t * P:(t + 1) * P],
                                                           k_st[0:ROWS, h, b * CH:b * CH + w], start=True, stop=True)
                                        mm.then_inc(ma_mm, 1)

                def scores(it, u, i_of, t, first=False):
                    b = u % 2
                    if t == 0:
                        pe.wait_ge(q_in[b], (i_of + 1) * 64)
                    if t in piece_of:
                        pe.wait_ge(k_in[piece_of[t]], (i_of // (NC // 2) + 1) * 48)
                        if first:
                            pe.wait_ge(rows_filled[piece_of[t]], 2)
                    for half in range(2):
                        n = 2 * t + half
                        slot = s_slot(u % S_RING, n)
                        if n >= S_RING:
                            pe.wait_ge(exp_done, it * NP + (n + 1 - S_RING))
                        elif not first:
                            pe.wait_ge(exp_done, (it - 1) * NP + (NP + n + 1 - S_RING))
                        for h in (2 * half, 2 * half + 1):
                            mm = nc.tensor.matmul(psum[:, 2 * slot + h % 2, :], k_st[:, h, t * P:(t + 1) * P],
                                                  q_st[:, b, h, :], start=True, stop=True)
                        mm.then_inc(s_ready, 1)

                def over_keys(bank, lhs, rhs, start, stop):
                    for h in range(HG):
                        mm = nc.tensor.matmul(psum[h * DH:(h + 1) * DH, bank, :], lhs(h), rhs(h), start=start, stop=stop)
                    return mm

                def weigh(it, i, t):
                    if t in piece_of:
                        n = piece_of[t]
                        pe.wait_ge(v_in[n], (i // (NC // 2) + 1) * (16 * (1 + (n == K_PIECES - 1))))
                    pe.wait_ge(exp_done, it * NP + (2 * t + 2))
                    if t == 0:
                        pe.wait_ge(o_left, it)
                    p = p_slot[t]

                    over_keys(O_BANK, lambda h: v_st[:, t, h * DH:(h + 1) * DH], lambda h: probs[:, p, h, :], t == 0,
                              t == NT - 1).then_inc(pv_done, 1)

                def sum_up(it, b):
                    pe.wait_ge(added, (it + 1) * adds)
                    pe.wait_ge(inverted, it)
                    over_keys(SUM_BANK, lambda h: ones[:], lambda h: sums[b][:, h, :], True, True).then_inc(sums_ready, 1)

                pe.wait_ge(filled, FILLS)

                def step(it, u, i, i_next):
                    first = isinstance(it, int) and it == 0
                    for t in range(NT):
                        if t + LAG < NT:
                            scores(it, u, i, t + LAG, first)
                        elif i_next is not None:
                            scores(it + 1, u + 1, i_next, t + LAG - NT)
                        weigh(it, i, t)
                        if t == SUMS_AT and not first:
                            sum_up(it - 1, (u + 1) % 2)

                for t in range(LAG):
                    scores(0, 0, 0, t, True)
                step(0, 0, 0, 0)
                with pe.Fori(0, MIDDLE // ROUND) as r:
                    for u in range(1, ROUND + 1):
                        step(r * ROUND + u, u, r * S_RING + u // 2, r * S_RING + (u + 1) // 2)
                for it in range(MIDDLE + 1, NIT):
                    step(it, it, it // 2, (it + 1) // 2 if it + 1 < NIT else None)
                sum_up(NIT - 1, 1)


def experts(nc, mem, sb0, sem, psum, ident, g):
    L, D, KT, NG, NE = (g[n] for n in "L D KT NG NE".split())
    x, out, WeT, load_o = (g[n] for n in "x out WeT load_o".split())
    wo_hi, wo_lo, wr, bo_all, br_all, be_st, o_raw = (g[n] for n in "wo_hi wo_lo wr bo_all br_all be_st o_raw".split())
    PARTS = be_st.shape[0]
    small_in, o_in, wo_lo_ready = (g[n] for n in "small_in o_in wo_lo_ready".split())
    NTL = L // P
    assert NTL == 2 * HEADS
    ROUND = 4
    WO_BANK, T_BANK, R_BANK, B_BANK = 4, 5, 6, 7

    with mem:
        def sb(name, shape, dt):
            return sb0(name, shape, dt, mem)

        we_hi = sb("we_hi", [P, KT, NE, D], F32R)
        we_lo = sb("we_lo", [P, KT, NE, D], F32R)
        LANDINGS = 3
        we_raw = [sb(f"we_raw{b}", [P, KT, D], F32) for b in range(LANDINGS)]
        number = sb("number", [P, NE], F32)

        def two(name, shape, dt):
            return [sb(f"{name}{b}", shape, dt) for b in range(2)]

        xb = two("xb", [P, D], F32)
        o_hi = two("att_hi", [P, NG, P], F32R)
        o_lo = two("att_lo", [P, NG, P], F32R)
        y = two("y", [P, D], F32)
        y_hi = two("y_hi", [P, KT, P], F32R)
        y_lo = two("y_lo", [P, KT, P], F32R)
        acc = two("acc", [P, D], F32)
        w = two("w", [P, NE], F32)
        w_st = sb("w_st", [P, PARTS], F32R)
        wT = sb("wT", [PARTS, P], F32R)
        stats = sb("stats3", [P, 6], F32)
        mv = sb("mv3", [P, 2], F32)
        row_numbers = sb("row_numbers", [P, 8], F32)
        var, std, rstd, tmp, neg_top, total, inv = (row_numbers[:, n:n + 1] for n in range(7))
        logits = sb("logits", [P, NE], F32)
        top = sb("top", [P, 8], F32)
        top_at = sb("top_at", [P, 8], U32)
        top_at_f = sb("top_at_f", [P, 2], F32)
        ex = sb("ex", [P, NE], F32)
        chosen1 = sb("chosen1", [P, NE], F32)
        chosen = sb("chosen", [P, NE], F32)

        we_in = [sem(f"we_in{e}") for e in range(NE)]
        hi_ready = sem("hi_ready")
        lo_ready = [sem(f"lo_ready{b}") for b in range(2)]
        numbered = sem("numbered")
        x_in = [sem(f"x_in3{b}") for b in range(2)]
        att_hi = sem("att_hi_done")
        att_lo = sem("att_lo_done")
        xb_done = sem("xb_done")
        wo_mm = sem("wo_mm")
        chain = sem("chain")
        stats_ready = sem("stats_ready3")
        y_done = sem("y_done")
        var_ready = sem("var_ready3")
        std_ready = sem("std_ready3")
        yn_ready = sem("yn_ready")
        turned = sem("turned")
        yh_done = sem("yh_done")
        yl_done = sem("yl_done")
        r_mm = sem("r_mm")
        logits_ready = sem("logits_ready")
        neg_ready = sem("neg_ready")
        ex_ready = sem("ex_ready")
        w_ready = sem("w_ready")
        w_turned = sem("w_turned")
        w_zeroed = sem("w_zeroed")
        wT_ready = sem("wT_ready")
        b_mm = sem("b_mm")
        begun = sem("begun")
        e_mm = sem("e_mm")
        mixed = sem("mixed")
        stored = [sem(f"stored{b}") for b in range(2)]

        CHAIN = 15

        def pairs_of_tiles(eng, body):
            for b in range(2):
                body(b, b, 0, 2)
            with eng.Fori(1, NTL // 2 - 1) as h:
                for b in range(2):
                    body(h * 2 + b, b, h, 2)
            for b in range(2):
                body(NTL - 2 + b, b, NTL // 2 - 1, 1 - b)

        with nc.Block() as block:
            @block.sync
            def _(sp):
                def load_x(i, b):
                    sp.dma_start(xb[b][:], x[ds(i * P, P), :]).then_inc(x_in[b], 16)

                for b in range(2):
                    load_x(b, b)
                for e in range(NE):
                    if e >= LANDINGS:
                        sp.wait_ge(hi_ready, e - LANDINGS + 1)
                        sp.wait_ge(lo_ready[(e - LANDINGS) % 2], (e - LANDINGS) // 2 + 1)
                    sp.dma_start(we_raw[e % LANDINGS][:], WeT[:, e * D:(e + 1) * D].rearrange("(k p) n -> p k n", p=P)).then_inc(we_in[e], 16)

                def tile(i, b, h, left):
                    if left == 2:
                        sp.wait_ge(att_lo, i + 1)
                        load_o(sp, b, h + 1)
                        sp.wait_ge(y_done, i + 1)
                        load_x(i + 2, b)
                    sp.wait_ge(mixed, (i + 1) * NE)
                    sp.dma_start(out[ds(i * P, P), :], acc[b][:]).then_inc(stored[b], 16)

                pairs_of_tiles(sp, tile)
                for b in range(2):
                    sp.wait_ge(stored[b], 16 * (NTL // 2))

            @block.gpsimd
            def _(pool):
                pool.iota(number[:], [[1, NE]], base=0, channel_multiplier=0, allow_small_or_imprecise_dtypes=True).then_inc(numbered, 1)
                pool.wait_ge(small_in, 32)

                def inputs(i, b, h):
                    if not (isinstance(i, int) and i < 2):
                        pool.wait_ge(wo_mm, i - 1)
                    pool.wait_ge(att_hi, i + 1)
                    pool.tensor_tensor(o_lo[b][:], o_raw[b][:], o_hi[b][:].bitcast(F32), ALU.subtract).then_inc(att_lo, 1)
                    pool.wait_ge(x_in[b], (h + 1) * 16)
                    pool.tensor_tensor(xb[b][:], xb[b][:], bo_all[:], ALU.add).then_inc(xb_done, 1)

                inputs(0, 0, 0)
                inputs(1, 1, 0)
                for e in range(1, NE, 2):
                    pool.wait_ge(hi_ready, e + 1)
                    pool.tensor_tensor(we_lo[:, :, e, :], we_raw[e % LANDINGS][:], we_hi[:, :, e, :].bitcast(F32),
                                       ALU.subtract).then_inc(lo_ready[1], 1)
                with pool.Fori(1, NTL // 2) as h:
                    for b in range(2):
                        inputs(h * 2 + b, b, h)

            @block.scalar
            def _(act):
                def att_split(i, b, h):
                    act.wait_ge(o_in[b], (h + 1) * (16 * HG))
                    if not (isinstance(i, int) and i < 2):
                        act.wait_ge(wo_mm, i - 1)
                    act.activation(o_hi[b][:], o_raw[b][:], ACT.Copy).then_inc(att_hi, 1)

                def root(i):
                    act.wait_ge(var_ready, i + 1)
                    act.activation(std[:], var[:], ACT.Sqrt).then_inc(std_ready, 1)

                def y_split(i, b):
                    act.wait_ge(turned, i + 1)
                    act.activation(y_hi[b][:], psum[:, T_BANK, :].rearrange("p (k n) -> p k n", k=KT), ACT.Copy).then_inc(yh_done, 1)

                def exps(i):
                    act.wait_ge(neg_ready, i + 1)
                    act.activation(ex[:], logits[:], ACT.Exp, bias=neg_top[:], accum_out=total[:]).then_inc(ex_ready, 1)

                def expert_hi(e):
                    act.wait_ge(we_in[e], 16)
                    act.activation(we_hi[:, :, e, :], we_raw[e % LANDINGS][:], ACT.Copy).then_inc(hi_ready, 1)

                att_split(0, 0, 0)
                att_split(1, 1, 0)
                expert_hi(0)
                root(0)
                expert_hi(1)
                y_split(0, 0)
                expert_hi(2)
                exps(0)
                expert_hi(3)
                expert_hi(4)
                expert_hi(5)

                def tile(i, b, h, left):
                    if left == 0:
                        return
                    root(i + 1)
                    if isinstance(i, int) and i == 0:
                        for e in (6, 7):
                            expert_hi(e)
                    y_split(i + 1, 1 - b)
                    exps(i + 1)
                    if left == 2:
                        att_split(i + 2, b, h + 1)

                pairs_of_tiles(act, tile)

            @block.vector
            def _(dve):
                def before_turn(i, b, h, n):
                    def step(ins):
                        n[0] += 1
                        ins.then_inc(chain, 1)
                        dve.wait_ge(chain, i * CHAIN + n[0])

                    dve.wait_ge(wo_mm, i + 1)
                    dve.wait_ge(xb_done, i + 1)
                    dve.tensor_tensor(y[b][:], psum[:, WO_BANK, :], xb[b][:], ALU.add).then_inc(y_done, 1)
                    dve.wait_ge(y_done, i + 1)
                    dve.bn_stats(stats[:], y[b][:]).then_inc(stats_ready, 1)
                    dve.wait_ge(numbered, 1)
                    dve.wait_ge(stats_ready, i + 1)
                    step(dve.bn_aggr(mv[:], stats[:]))
                    dve.tensor_scalar(var[:], mv[:, 1:2], EPS, None, ALU.add).then_inc(var_ready, 1)
                    dve.wait_ge(std_ready, i + 1)
                    step(dve.reciprocal(rstd[:], std[:]))
                    step(dve.tensor_tensor(tmp[:], rstd[:], rstd[:], ALU.mult))
                    step(dve.tensor_tensor(tmp[:], tmp[:], var[:], ALU.mult))
                    step(dve.tensor_scalar(tmp[:], tmp[:], -0.5, 1.5, ALU.mult, ALU.add))
                    step(dve.tensor_tensor(rstd[:], rstd[:], tmp[:], ALU.mult))
                    if h is not None:
                        dve.wait_ge(stored[b], h * 16)
                    dve.tensor_scalar(acc[b][:], y[b][:], mv[:, 0:1], rstd[:], ALU.subtract, ALU.mult).then_inc(yn_ready, 1)

                def after_turn(i, b):
                    dve.wait_ge(yh_done, i + 1)
                    dve.tensor_tensor(y_lo[b][:], psum[:, T_BANK, :].rearrange("p (k n) -> p k n", k=KT),
                                      y_hi[b][:].bitcast(F32), ALU.subtract).then_inc(yl_done, 1)

                def route(i, b, n):
                    def step(ins):
                        n[0] += 1
                        ins.then_inc(chain, 1)
                        dve.wait_ge(chain, i * CHAIN + n[0])

                    dve.wait_ge(r_mm, i + 1)
                    step(dve.tensor_tensor(logits[:], psum[:, R_BANK, 0:NE], br_all[:], ALU.add))
                    dve.tensor_tensor(logits[:], psum[:, R_BANK, NE:2 * NE], logits[:], ALU.add).then_inc(logits_ready, 1)
                    dve.wait_ge(numbered, 1)
                    dve.wait_ge(logits_ready, i + 1)
                    step(dve.max(top[:], logits[:]))
                    dve.tensor_scalar(neg_top[:], top[:, 0:1], -1.0, None, ALU.mult).then_inc(neg_ready, 1)
                    step(dve.max_index(top_at[:], top[:], logits[:]))
                    step(dve.tensor_copy(top_at_f[:], top_at[:, 0:2]))
                    step(dve.tensor_scalar(chosen1[:], number[:], top_at_f[:, 0:1], None, ALU.is_equal))
                    dve.scalar_tensor_tensor(out=chosen[:], in0=number[:], scalar=top_at_f[:, 1:2], in1=chosen1[:],
                                             op0=ALU.is_equal, op1=ALU.add).then_inc(chain, 1)
                    n[0] += 1
                    dve.wait_ge(ex_ready, i + 1)
                    dve.reciprocal(inv[:], total[:]).then_inc(chain, 1)
                    n[0] += 1
                    dve.wait_ge(chain, i * CHAIN + n[0])
                    step(dve.scalar_tensor_tensor(out=w[b][:], in0=ex[:], scalar=inv[:], in1=chosen[:],
                                                  op0=ALU.mult, op1=ALU.mult))
                    dve.wait_ge(w_turned, i)
                    step(dve.tensor_copy(w_st[:, 0:NE], w[b][:]))
                    assert n[0] == CHAIN
                    dve.tensor_copy(w_st[:, 2 * BIAS_STEP:PARTS], w[b][:]).then_inc(w_ready, 1)
                    dve.tensor_tensor(w_st[:, BIAS_STEP:BIAS_STEP + NE], w[b][:], w_st[:, 0:NE].bitcast(F32), ALU.subtract).then_inc(w_ready, 1)

                def copy_wT(i):
                    dve.wait_ge(w_turned, i + 1)
                    dve.tensor_copy(wT[:], psum[0:PARTS, R_BANK, P:2 * P]).then_inc(wT_ready, 1)

                def begin(i, b):
                    dve.wait_ge(b_mm, i + 1)
                    dve.tensor_tensor(acc[b][:], psum[:, B_BANK, :], y[b][:], ALU.add).then_inc(begun, 1)

                def mix(i, b, es):
                    for e in es:
                        if e == 0:
                            dve.wait_ge(begun, i + 1)
                        else:
                            dve.wait_ge(mixed, i * NE + e)
                        dve.wait_ge(e_mm, i * NE + (e + 1))
                        dve.scalar_tensor_tensor(out=acc[b][:], in0=psum[:, e % ROUND, :], scalar=w[b][:, e:e + 1],
                                                 in1=acc[b][:], op0=ALU.mult, op1=ALU.add).then_inc(mixed, 1)

                def expert_lo(e):
                    dve.wait_ge(hi_ready, e + 1)
                    dve.tensor_tensor(we_lo[:, :, e, :], we_raw[e % LANDINGS][:], we_hi[:, :, e, :].bitcast(F32),
                                      ALU.subtract).then_inc(lo_ready[0], 1)

                dve.wait_ge(small_in, 32)
                dve.wait_ge(numbered, 1)
                n = [0]
                dve.memset(w_st[:].bitcast(F32), 0.0).then_inc(w_zeroed, 1)
                dve.wait_ge(w_zeroed, 1)
                before_turn(0, 0, None, n)
                expert_lo(0)
                after_turn(0, 0)
                expert_lo(2)
                route(0, 0, n)
                copy_wT(0)
                begin(0, 0)
                expert_lo(4)

                def tile(i, b, h, left):
                    n = [0]
                    if left:
                        before_turn(i + 1, 1 - b, None if isinstance(i, int) and i == 0 else h + b, n)
                    mix(i, b, (0, 1))
                    if left:
                        after_turn(i + 1, 1 - b)
                    if isinstance(i, int) and i == 0:
                        expert_lo(6)
                    mix(i, b, (2, 3))
                    if left:
                        route(i + 1, 1 - b, n)
                    mix(i, b, (4, 5, 6))
                    if left:
                        copy_wT(i + 1)
                    mix(i, b, (7,))
                    if left:
                        begin(i + 1, 1 - b)

                pairs_of_tiles(dve, tile)

            @block.tensor
            def _(pe):
                def products(out_ap, lhs, rhs, parts):
                    terms = [(k, a, b) for k in range(parts) for a, b in ((0, 0), (0, 1), (1, 0))]
                    for q, (k, a, b) in enumerate(terms):
                        mm = pe.matmul(out_ap, lhs[a](k), rhs[b](k), start=q == 0, stop=q == len(terms) - 1)
                    return mm

                def project(i, b):
                    pe.wait_ge(att_hi, i + 1)
                    pe.wait_ge(att_lo, i + 1)
                    pe.wait_ge(y_done, i)
                    products(psum[:, WO_BANK, :], [lambda j, A=A: A[b][:, j, :] for A in (o_hi, o_lo)],
                             [lambda j, W=W: W[:, j, :] for W in (wo_hi, wo_lo)], NG).then_inc(wo_mm, 1)

                def turn(i, b):
                    pe.wait_ge(yn_ready, i + 1)
                    pe.wait_ge(yl_done, i)
                    for k in range(KT):
                        mm = pe.transpose(psum[:, T_BANK, k * P:(k + 1) * P], acc[b][:, k * P:(k + 1) * P], ident[:])
                    mm.then_inc(turned, 1)

                def route(i, b):
                    pe.wait_ge(yh_done, i + 1)
                    pe.wait_ge(yl_done, i + 1)
                    pe.wait_ge(wT_ready, i)
                    for k in range(KT):
                        pe.matmul(psum[:, R_BANK, 0:2 * NE], y_hi[b][:, k, :], wr[:, k, :, :].rearrange("p h e -> p (h e)"), start=k == 0, stop=False)
                    for k in range(KT):
                        mm = pe.matmul(psum[:, R_BANK, 0:NE], y_lo[b][:, k, :], wr[:, k, 0, :], start=False, stop=k == KT - 1)
                    mm.then_inc(r_mm, 1)

                def turn_w(i, b):
                    pe.wait_ge(w_ready, (i + 1) * 2)
                    pe.transpose(psum[0:PARTS, R_BANK, P:2 * P], w_st[:].bitcast(F32), ident[:]).then_inc(w_turned, 1)

                def biases(i):
                    pe.wait_ge(wT_ready, i + 1)
                    pe.wait_ge(begun, i)
                    pe.matmul(psum[:, B_BANK, :], wT[:], be_st[:], start=True, stop=True).then_inc(b_mm, 1)

                def expert(i, b, es):
                    for e in es:
                        if isinstance(i, int) and i == 0:
                            pe.wait_ge(hi_ready, e + 1)
                            pe.wait_ge(lo_ready[e % 2], e // 2 + 1)
                        if e >= ROUND:
                            pe.wait_ge(mixed, i * NE + (e - ROUND + 1))
                        elif e == 0 and not (isinstance(i, int) and i == 0):
                            pe.wait_ge(mixed, i * NE)
                        products(psum[:, e % ROUND, :], [lambda k, A=A: A[b][:, k, :] for A in (y_hi, y_lo)],
                                 [lambda k, W=W: W[:, k, e, :] for W in (we_hi, we_lo)], KT).then_inc(e_mm, 1)

                pe.wait_ge(wo_lo_ready, 3)
                project(0, 0)
                turn(0, 0)
                route(0, 0)

                def tile(i, b, h, left):
                    if left:
                        project(i + 1, 1 - b)
                    expert(i, b, (0, 1))
                    if isinstance(i, int) and i == 0:
                        turn_w(0, 0)
                        biases(0)
                    if left:
                        turn(i + 1, 1 - b)
                    expert(i, b, (2, 3))
                    if left:
                        route(i + 1, 1 - b)
                    expert(i, b, (4, 5, 6))
                    if left:
                        turn_w(i + 1, 1 - b)
                    expert(i, b, (7,))
                    if left:
                        biases(i + 1)

                pairs_of_tiles(pe, tile)


_DRAM = ["x", "ctxT", "Wq", "bq", "Wk", "bk", "Wv", "bv", "Wo", "bo", "WeT", "be", "WrT", "br"]


def kernel(x, ctx_1024, L0_xattn_Wq, L0_xattn_bq, L0_xattn_Wk, L0_xattn_bk, L0_xattn_Wv, L0_xattn_bv,
           L0_xattn_Wo, L0_xattn_bo, L0_ffn_W_experts, L0_ffn_b_experts, L0_ffn_W_router, L0_ffn_b_router):
    import numpy as np
    import concourse.bacc as bacc
    from concourse.bass_utils import run_bass_kernel_spmd

    x, ctx = np.asarray(x)[0], np.asarray(ctx_1024)[0]
    experts_in_out = np.asarray(L0_ffn_W_experts).transpose(2, 0, 1)

    def columns(bias):
        return np.asarray(bias).reshape(-1, P).T

    laid_out = [
        x, ctx.T, L0_xattn_Wq, columns(L0_xattn_bq), L0_xattn_Wk, columns(L0_xattn_bk), L0_xattn_Wv, L0_xattn_bv,
        L0_xattn_Wo, L0_xattn_bo, experts_in_out.reshape(experts_in_out.shape[0], -1), L0_ffn_b_experts,
        np.asarray(L0_ffn_W_router).T, L0_ffn_b_router,
    ]
    nc = bacc.Bacc("TRN2", target_bir_lowering=False, num_devices=1)
    arrays, aps = {}, []
    for name, a in zip(_DRAM, laid_out):
        a = np.ascontiguousarray(a)
        arrays[f"in_{name}"] = a
        aps.append(nc.dram_tensor(f"in_{name}", a.shape, mybir.dt.from_np(a.dtype), kind="ExternalInput").ap())
    out = nc.dram_tensor("out", x.shape, F32, kind="ExternalOutput").ap()
    build_program(nc, *aps, out)
    r = run_bass_kernel_spmd(nc, [arrays], core_ids=[0])
    return r.results[0]["out"][None]
```
